# Optimizing a Trainium2 kernel written in Bass

```python
import numpy as np
import jax
import jax.numpy as jnp

def _softmax(x, axis=-1):
    return jax.nn.softmax(x, axis=axis)

def _gelu(x):
    return jax.nn.gelu(x, approximate=True)

def _silu(x):
    return jax.nn.silu(x)

def _sigmoid(x):
    return jax.nn.sigmoid(x)

def _layernorm(x, axis=-1, eps=1e-05):
    m = jnp.mean(x, axis=axis, keepdims=True)
    v = jnp.var(x, axis=axis, keepdims=True)
    return (x - m) / jnp.sqrt(v + eps)

def _scatter_add(tgt, idx, src, axis=0):
    return tgt.at[idx].add(src)

def _segment_sum(src, seg, n):
    return jax.ops.segment_sum(src, seg, n)
kernel_name = 'mk_decoder_postln_d1_seqx_r4_ef0be5'

def setup_inputs(seed: int=0):
    np.random.seed(seed)
    _w = jnp.asarray

    def _rec_inputs():
        import jax
        import jax.numpy as jnp
        _rk = jax.random.key(seed)
        x = -0.0002928 + 1 * jax.random.normal(jax.random.fold_in(_rk, 1), (4, 512, 256), jnp.float32)
        _lenS = 512 - jax.random.randint(jax.random.fold_in(_rk, 7), (4,), 0, max(1, 512 // 4) + 1, jnp.int32)
        _lenS2 = 64 - jax.random.randint(jax.random.fold_in(_rk, 8), (4,), 0, max(1, 64 // 4) + 1, jnp.int32)
        _ctx_768P = jax.random.normal(jax.random.fold_in(_rk, 11), (4, 16, 192), jnp.float32)
        _ctx_768c = jax.random.dirichlet(jax.random.fold_in(_rk, 511), 0.3 * jnp.ones((16,), jnp.float32), (4, 64))
        _ctx_768t = jnp.einsum('bsk,bkd->bsd', _ctx_768c, _ctx_768P)
        _ctx_768t = _ctx_768t * jax.lax.rsqrt(jnp.mean(jnp.square(_ctx_768t)) + 1e-12) * 0.953939
        ctx_768 = 2.09791e-05 + 1.00001 * (_ctx_768t + 0.3 * jax.random.normal(jax.random.fold_in(_rk, 611), (4, 64, 192), jnp.float32))
        return (x, ctx_768)
    x, ctx_768 = _rec_inputs()

    def _L0_attn_setup():
        import jax, jax.numpy as jnp
        import numpy as np
        import math
        DIM = 256
        NUM_HEADS = 16
        HEAD_DIM = DIM // NUM_HEADS
        B, S = (2, 512)
        key = jax.random.key(seed)
        ks = jax.random.split(key, 9)
        sc = 0.02
        return {'x': jax.random.normal(ks[0], (B, S, DIM), jnp.float32), 'Wq': jax.random.normal(ks[1], (DIM, DIM), jnp.float32) * sc, 'bq': jax.random.normal(ks[2], (DIM,), jnp.float32) * sc, 'Wk': jax.random.normal(ks[3], (DIM, DIM), jnp.float32) * sc, 'bk': jax.random.normal(ks[4], (DIM,), jnp.float32) * sc, 'Wv': jax.random.normal(ks[5], (DIM, DIM), jnp.float32) * sc, 'bv': jax.random.normal(ks[6], (DIM,), jnp.float32) * sc, 'Wo': jax.random.normal(ks[7], (DIM, DIM), jnp.float32) * sc, 'bo': jax.random.normal(ks[8], (DIM,), jnp.float32) * sc}
    _L0_attn_all = _L0_attn_setup()
    _L0_attn_in = {k: v for k, v in _L0_attn_all.items() if k in ('Wq', 'bq', 'Wk', 'bk', 'Wv', 'bv', 'Wo', 'bo')}
    del _L0_attn_all

    def _L0_xattn_setup():
        import jax, jax.numpy as jnp
        import numpy as np
        N_HEADS = 16
        D_HEAD = 64
        key = jax.random.key(seed)
        ks = jax.random.split(key, 7)
        B, SQ, SKV = (2, 512, 512)
        D_MODEL, D_COND, D_ATTN = (256, 192, N_HEADS * D_HEAD)
        return {'x': jax.random.normal(ks[0], (B, SQ, D_MODEL), jnp.float32), 'cond': jax.random.normal(ks[1], (B, SKV, D_COND), jnp.float32), 'w_q': jax.random.normal(ks[2], (D_MODEL, D_ATTN), jnp.float32) * D_MODEL ** (-0.5), 'w_k': jax.random.normal(ks[3], (D_COND, D_ATTN), jnp.float32) * D_COND ** (-0.5), 'w_v': jax.random.normal(ks[4], (D_COND, D_ATTN), jnp.float32) * D_COND ** (-0.5), 'w_out': jax.random.normal(ks[5], (D_ATTN, D_MODEL), jnp.float32) * D_ATTN ** (-0.5), 'b_out': jnp.zeros((D_MODEL,), jnp.float32)}
    _L0_xattn_all = _L0_xattn_setup()
    _L0_xattn_in = {k: v for k, v in _L0_xattn_all.items() if k in ('w_q', 'w_k', 'w_v', 'w_out', 'b_out')}
    del _L0_xattn_all

    def _L0_ffn_setup():
        import jax, jax.numpy as jnp
        import numpy as np
        HIDDEN = 256
        INTER = 1024
        N_EXPERTS = 8
        TOP_K = 2
        INIT_STD = 0.02
        key = jax.random.key(seed)
        ks = jax.random.split(key, 6)
        x = jax.random.normal(ks[0], (2, 256, HIDDEN), dtype=jnp.float32)
        Wg = jax.random.normal(ks[1], (N_EXPERTS, HIDDEN), dtype=jnp.float32) * INIT_STD
        W1 = jax.random.normal(ks[2], (N_EXPERTS, HIDDEN, INTER), dtype=jnp.float32) * INIT_STD
        b1 = jnp.zeros((N_EXPERTS, INTER), dtype=jnp.float32)
        W2 = jax.random.normal(ks[3], (N_EXPERTS, INTER, HIDDEN), dtype=jnp.float32) * INIT_STD
        b2 = jnp.zeros((N_EXPERTS, HIDDEN), dtype=jnp.float32)
        return {'x': x, 'Wg': Wg, 'W1': W1, 'b1': b1, 'W2': W2, 'b2': b2}
    _L0_ffn_all = _L0_ffn_setup()
    _L0_ffn_in = {k: v for k, v in _L0_ffn_all.items() if k in ('Wg', 'W1', 'b1', 'W2', 'b2')}
    del _L0_ffn_all
    return {'x': x, 'ctx_768': ctx_768, 'L0_attn_Wq': _L0_attn_in['Wq'], 'L0_attn_bq': _L0_attn_in['bq'], 'L0_attn_Wk': _L0_attn_in['Wk'], 'L0_attn_bk': _L0_attn_in['bk'], 'L0_attn_Wv': _L0_attn_in['Wv'], 'L0_attn_bv': _L0_attn_in['bv'], 'L0_attn_Wo': _L0_attn_in['Wo'], 'L0_attn_bo': _L0_attn_in['bo'], 'L0_xattn_w_q': _L0_xattn_in['w_q'], 'L0_xattn_w_k': _L0_xattn_in['w_k'], 'L0_xattn_w_v': _L0_xattn_in['w_v'], 'L0_xattn_w_out': _L0_xattn_in['w_out'], 'L0_xattn_b_out': _L0_xattn_in['b_out'], 'L0_ffn_Wg': _L0_ffn_in['Wg'], 'L0_ffn_W1': _L0_ffn_in['W1'], 'L0_ffn_b1': _L0_ffn_in['b1'], 'L0_ffn_W2': _L0_ffn_in['W2'], 'L0_ffn_b2': _L0_ffn_in['b2']}

def reference(x, ctx_768, L0_attn_Wq, L0_attn_bq, L0_attn_Wk, L0_attn_bk, L0_attn_Wv, L0_attn_bv, L0_attn_Wo, L0_attn_bo, L0_xattn_w_q, L0_xattn_w_k, L0_xattn_w_v, L0_xattn_w_out, L0_xattn_b_out, L0_ffn_Wg, L0_ffn_W1, L0_ffn_b1, L0_ffn_W2, L0_ffn_b2):
    import jax
    import jax.numpy as jnp

    def _L0_attn_ref(x, Wq, bq, Wk, bk, Wv, bv, Wo, bo):
        import jax, jax.numpy as jnp
        import numpy as np
        import math
        DIM = 256
        NUM_HEADS = 16
        HEAD_DIM = DIM // NUM_HEADS
        B, S = (2, 512)
        b, s, d = x.shape
        h, hd = (NUM_HEADS, HEAD_DIM)

        def split_heads(t):
            return t.reshape(b, s, h, hd).transpose(0, 2, 1, 3)
        q = split_heads(x @ Wq + bq)
        k = split_heads(x @ Wk + bk)
        v = split_heads(x @ Wv + bv)
        scores = jnp.einsum('bhqd,bhkd->bhqk', q, k) / math.sqrt(hd)
        causal = jnp.tril(jnp.ones((s, s), dtype=bool))
        scores = jnp.where(causal[None, None], scores, jnp.asarray(-10000.0, scores.dtype))
        probs = jax.nn.softmax(scores, axis=-1)
        ctx = jnp.einsum('bhqk,bhkd->bhqd', probs, v)
        ctx = ctx.transpose(0, 2, 1, 3).reshape(b, s, d)
        return ctx @ Wo + bo

    def _L0_xattn_ref(x, cond, w_q, w_k, w_v, w_out, b_out):
        import jax, jax.numpy as jnp
        import numpy as np
        N_HEADS = 16
        D_HEAD = 64
        B, SQ, _ = x.shape
        SKV = cond.shape[1]
        scale = D_HEAD ** (-0.5)
        q = (x @ w_q).reshape(B, SQ, N_HEADS, D_HEAD)
        k = (cond @ w_k).reshape(B, SKV, N_HEADS, D_HEAD)
        v = (cond @ w_v).reshape(B, SKV, N_HEADS, D_HEAD)
        attn = jnp.einsum('bqhd,bkhd->bhqk', q, k) * scale
        attn = jax.nn.softmax(attn, axis=-1)
        out = jnp.einsum('bhqk,bkhd->bqhd', attn, v).reshape(B, SQ, N_HEADS * D_HEAD)
        return out @ w_out + b_out

    def _L0_ffn_ref(x, Wg, W1, b1, W2, b2):
        import jax, jax.numpy as jnp
        import numpy as np
        HIDDEN = 256
        INTER = 1024
        N_EXPERTS = 8
        TOP_K = 2
        INIT_STD = 0.02
        orig_shape = x.shape
        xt = x.reshape(-1, HIDDEN)
        T = xt.shape[0]
        logits = xt @ Wg.T
        topk_logits, topk_idx = jax.lax.top_k(logits, TOP_K)
        w = jax.nn.softmax(topk_logits, axis=-1)
        rows = jnp.arange(T)[:, None]
        gates = jnp.zeros((T, N_EXPERTS), xt.dtype).at[rows, topk_idx].add(w)
        h = jnp.einsum('th,ehi->tei', xt, W1) + b1
        h = jax.nn.gelu(h, approximate=False)
        o = jnp.einsum('tei,eih->teh', h, W2) + b2
        y = jnp.einsum('te,teh->th', gates, o)
        return y.reshape(orig_shape)
    x = _layernorm(x + _L0_attn_ref(x, L0_attn_Wq, L0_attn_bq, L0_attn_Wk, L0_attn_bk, L0_attn_Wv, L0_attn_bv, L0_attn_Wo, L0_attn_bo), axis=-1)
    x = _layernorm(x + _L0_xattn_ref(x, ctx_768, L0_xattn_w_q, L0_xattn_w_k, L0_xattn_w_v, L0_xattn_w_out, L0_xattn_b_out), axis=-1)
    x = _layernorm(x + _L0_ffn_ref(x, L0_ffn_Wg, L0_ffn_W1, L0_ffn_b1, L0_ffn_W2, L0_ffn_b2), axis=-1)
    return x

_drawn_inputs = setup_inputs


def setup_inputs(seed=0):
    import zlib

    import numpy as np

    out = dict(_drawn_inputs(seed))
    spreads = {'L0_xattn_b_out': (0.0, 0.1), 'L0_ffn_b1': (0.0, 0.309), 'L0_ffn_b2': (0.0, 0.1)}
    factors = {'L0_attn_Wq': 8.0,
     'L0_attn_bq': 8.0,
     'L0_attn_Wk': 8.0,
     'L0_attn_bk': 64.0,
     'L0_attn_Wv': 4.654,
     'L0_attn_bv': 4.868,
     'L0_attn_Wo': 3.812,
     'L0_attn_bo': 3.922}
    for name, (base, spread) in spreads.items():
        noise = np.random.default_rng([zlib.crc32(name.encode()), seed]).standard_normal(out[name].shape)
        drawn = base * np.exp(spread * noise) if base else spread * noise
        out[name] = jnp.asarray(drawn.astype(out[name].dtype))
    for name, factor in factors.items():
        out[name] = (out[name] * factor).astype(out[name].dtype)
    return out
```

```python
import concourse.bass as bass
from concourse import mybir
from contextlib import ExitStack

F32 = mybir.dt.float32
F16 = mybir.dt.float16
I32 = mybir.dt.int32
U32 = mybir.dt.uint32
ALU = mybir.AluOpType
ACT = mybir.ActivationFunctionType
AX = mybir.AxisListType

NB, S, D = 4, 512, 256
T = NB * S
NQ = S // 128
NT = T // 128
DC = D // 128
H, HD = 16, 16
PAIRS = H // 2
GROUPS = H // 4
XH, XD, KV, DCOND = 16, 64, 64, 192
XA = XH * XD
NE, FF = 8, 1024
FM = FF // 128
SLOTS = 256
TILES = (2 * T + NE * (SLOTS - 1)) // SLOTS
EPS = 1e-5
WS = 64.0
XS = 16.0
QS = 4.0
NEG = -60000.0
STACK = 3 * HD

G_USES = ["xT0", "xT1", "q0", "q1", "k0", "k1", "v0", "v1", "cT0", "cT1", "kT", "vT", "mT",
          "ct0", "ct1", "ct2", "ct3", "cx0", "cx1", "o0", "o1", "xa0", "xa1",
          "O0", "O1", "O2", "O3", "xr0", "xr1", "lg"]
R_USES = (["A0", "A1"] + [f"m{n}" for n in range(NQ * PAIRS)] + ["VW0", "VW1"]
          + [f"s{n}" for n in range(GROUPS * NQ * 2)]
          + ["S0", "S1", "T0", "S2", "T1", "S3", "T2", "T3"])
STEPS = GROUPS * NQ * 2


def attention_block(nc, ctx, dram, keep):
    assert len(G_USES) % 2 == 0 and len(R_USES) % 2 == 0
    G_PER, R_PER = len(G_USES) // 2, len(R_USES) // 2
    START = 1

    def sb(name, shape, dt=F32):
        return ctx.enter_context(nc.sbuf_tensor(name, shape, dt))

    def sem(name):
        return ctx.enter_context(nc.semaphore(name))

    ident, ident16 = keep["ident"], keep["ident16"]
    logits, xhl = keep["logits"], keep["xhl"]
    causal = sb("causal", [128, 128], F16)
    zeros = sb("zeros", [128, 512], F16)
    power = sb("power", [128, 2 * NQ])
    x_tok = sb("x_tok", [128, NQ, D])
    x_bo = sb("x_bo", [128, NQ, D])
    xT = sb("xT", [128, 2, DC, S], F16)
    qf = sb("qf", [128, 2, S])
    qk = sb("qk", [128, 2, 4, S], F16)
    qs = sb("qs", [128, PAIRS, S], F16)
    ks = sb("ks", [128, PAIRS, S], F16)
    v_aug = sb("v_aug", [128, NQ, H, 32])
    rowmax = sb("rowmax", [128, NQ, H])
    neg_maxT = sb("neg_maxT", [H, S], F16)
    probs = sb("probs", [128, 3, 2, S])
    cu = sb("cu", [128, 2, S])
    inv = sb("inv", [128, GROUPS, NQ, 4])
    ctx_tok = sb("ctx_tok", [128, NQ, D])
    ctxT = sb("ctxT", [128, 2, DC, S], F16)
    x1 = sb("x1", [128, NQ, D])
    x1_b = sb("x1_b", [128, NQ, D])
    x1T = sb("x1T", [128, 2, DC, S], F16)
    x2 = sb("x2", [128, NQ, D])
    x2T = cu
    stats = sb("stats", [128, NQ, 6])
    meanvar = sb("meanvar", [128, NQ, 2])
    rstd = sb("rstd", [128, NQ])
    e_x = sb("e_x", [128, 2, XA])
    xmax = sb("xmax", [128, 2, XH])
    xsum = sb("xsum", [128, 2, XH])
    xinv = sb("xinv", [128, 2, XH])
    pT = sb("pT", [128, 2, 2, PAIRS, 128], F16)
    a_x = sb("a_x", [128, 2, DC, XA], F16)
    vw = sb("vw", [128, 2, PAIRS, D], F16)
    w_hl = sb("w_hl", [128, 2, 4, DC, D], F16)
    wqT = sb("wqT", [128, PAIRS, D])
    wkv = sb("wkv", [128, 2, XA])
    wkv2 = sb("wkv2", [DCOND - 128, 2, XA])
    wout = sb("wout", [128, PAIRS, D])
    cond = sb("cond", [KV, DCOND])
    cT = sb("cT", [128, 2, KV])
    kvT = sb("kvT", [128, 2, PAIRS, KV])
    qk_bias = sb("qk_bias", [128, 2, 2])
    b_rows = sb("b_rows", [128, 3, D])

    R = [ctx.enter_context(nc.psum_tensor(f"R{i}", [128, 2, 512], F32)) for i in range(2)]
    PV = [ctx.enter_context(nc.psum_tensor(f"PV{i}", [128, 512], F32)) for i in range(2)]
    G = [ctx.enter_context(nc.psum_tensor(f"G{i}", [128, 512], F32)) for i in range(2)]

    w_in, b_in, wx_in, z_out = sem("w_in"), sem("b_in"), sem("wx_in"), sem("z_out")
    const_step, consts = sem("const_step"), sem("consts")
    w_hi, w_lo, wqT_done, bias_done = sem("w_hi"), sem("w_lo"), sem("wqT_done"), sem("bias_done")
    x_in, c_in = sem("x_in"), sem("c_in")
    qk_stored, stack_in, m_stored, m_in = sem("qk_stored"), sem("stack_in"), sem("m_stored"), sem("m_in")
    g_full = [sem(f"g_full{i}") for i in range(2)]
    g_empty = [sem(f"g_empty{i}") for i in range(2)]
    r_full = [sem(f"r_full{i}") for i in range(2)]
    r_empty = [sem(f"r_empty{i}") for i in range(2)]
    pv_empty = [sem(f"pv_empty{i}") for i in range(2)]
    hi_done = sem("hi_done")
    xb_done, x1b_done = sem("xb_done"), sem("x1b_done")
    qhi_done, qlo_done = sem("qhi_done"), sem("qlo_done")
    probs_ready, probs_used = sem("probs_ready"), sem("probs_used")
    ctx_done, x1_ready, x2_ready = sem("ctx_done"), sem("x1_ready"), sem("x2_ready")
    var_done, rstd_done, pool_step, dve_step = sem("var_done"), sem("rstd_done"), sem("pool_step"), sem("dve_step")
    e_exp, e_inv, e_prob = sem("e_exp"), sem("e_inv"), sem("e_prob")
    exp_seen = sem("exp_seen")
    xhi_done, x2_stored = sem("xhi_done"), sem("x2_stored")

    def g(i, name):
        n = G_USES.index(name)
        return n % 2, i * G_PER + n // 2 + START

    def r(i, name):
        n = R_USES.index(name)
        return n % 2, i * R_PER + n // 2 + START

    QK = ["q0", "q1", "k0", "k1"]
    HIS = ["xT0", "xT1", "A0", "A1", "VW0", "VW1", "cx0", "cx1", "xa0", "xa1", "T0", "T1", "T2", "T3"]

    def his(i, name):
        return i * len(HIS) + HIS.index(name) + 1

    def flat(ap):
        return ap.rearrange("p a b -> p (a b)")

    def step_of(s):
        return s // (2 * NQ), s // 2 % NQ, s % 2

    block = ctx.enter_context(nc.Block())

    @block.sync
    def _(sp):
        for free in (g_full[0], g_full[1], g_empty[0], g_empty[1], pv_empty[0], pv_empty[1], probs_used, stack_in,
                     qk_stored, m_stored, qlo_done, x2_stored, x1_ready):
            sp.sem_inc(free, START)

        def load_batch(b):
            sp.dma_start(x_tok[:, :, :], dram["x"][bass.ds(b * S, S), :]
                         .rearrange("(t p) d -> p t d", p=128)).then_inc(x_in, 16)
            sp.dma_start(cond[:, :], dram["cond"][bass.ds(b * KV, KV), :]).then_inc(c_in, 16)

        load_batch(0)
        for n, w in enumerate(("Wq", "Wk", "Wv", "Wo")):
            sp.dma_start(flat(probs[:, n // 2, :, :])[:, (n % 2) * 512:(n % 2) * 512 + 512]
                         .rearrange("p (c n) -> p c n", c=DC),
                         dram[w].rearrange("(c p) n -> p c n", p=128)).then_inc(w_in, 16)
        sp.dma_start(qk_bias[:, 0, :], dram["bq"]).then_inc(b_in, 16)
        sp.dma_start(qk_bias[:, 1, :], dram["bk"]).then_inc(b_in, 16)
        for n, b in enumerate(("bo", "bv", "b_out")):
            sp.dma_start(b_rows[:, n, :], dram[b].partition_broadcast(128)).then_inc(b_in, 16)
        sp.dma_start(keep["WgT"][:, :, :], dram["WgT"]).then_inc(b_in, 16)
        with nc.sync.Fori(0, NB) as i:
            sp.wait_ge(probs_used, i * STEPS + START)
            sp.wait_ge(stack_in, i * 12 * 16 + START)
            sp.wait_ge(qlo_done, i * 4 + 4 + START)
            for hl in range(2):
                sp.dma_start(dram["qk"][hl, :, :].rearrange("(m p) s -> p m s", p=128),
                             qk[:, hl, :, :]).then_inc(qk_stored, 16)
            sp.wait_ge(qk_stored, i * 32 + 32 + START)
            for t, (dst, parts) in enumerate(((qs, (0, 0, 1)), (ks, (0, 1, 0)))):
                for par in range(2):
                    for n, hl in enumerate(parts):
                        row = 64 * par + n * HD
                        src = dram["qk"][hl, t * D:(t + 1) * D, :].rearrange(
                            "(p r d) s -> r d p s", r=2, d=HD)[par, :, :, :]
                        sp.dma_start(dst[row:row + HD, :, :], src).then_inc(stack_in, 16)
            slot, value = g(i, "mT")
            sp.wait_ge(g_empty[slot], value + 1)
            sp.dma_start(dram["m"], neg_maxT[:, :]).then_inc(m_stored, 16)
            sp.wait_ge(m_stored, i * 16 + 16 + START)
            for par in range(2):
                row = 64 * par + STACK
                sp.dma_start(qs[row:row + 1, :, :],
                             dram["m"].rearrange("(p r) s -> r p s", r=2)[par:par + 1, :, :]).then_inc(m_in, 16)
            sp.wait_ge(xb_done, i + 1)
            load_batch((i + 1) % NB)
            sp.wait_ge(x2_ready, i + 1)
            sp.dma_start(dram["x2"][bass.ds(i * S, S), :].rearrange("(t p) d -> p t d", p=128),
                         x2[:, :, :]).then_inc(x2_stored, 16)
        sp.wait_ge(x2_stored, NB * 16 + START)
        sp.wait_ge(z_out, 16)
        sp.wait_ge(x_in, (NB + 1) * 16)
        sp.wait_ge(c_in, (NB + 1) * 16)

    @block.gpsimd
    def _(pool):
        P = nc.gpsimd
        P.memset(ident[:, :], 0.0).then_inc(const_step, 1)
        P.memset(causal[:, :], 0.0).then_inc(const_step, 1)
        P.memset(zeros[:, :], 0.0).then_inc(const_step, 1)
        P.memset(power[:, 0:NQ], EPS).then_inc(const_step, 1)
        P.memset(power[:, NQ:], -0.5).then_inc(const_step, 1)
        P.memset(ks[:, :, :], 1.0).then_inc(const_step, 1)
        P.memset(v_aug[:, :, :, :], 1.0).then_inc(const_step, 1)
        pool.wait_ge(const_step, 7)
        P.affine_select(out=ident[:, :], in_=ident[:, :], compare_op=ALU.not_equal, fill=1.0, base=0,
                        pattern=[[-1, 128]], channel_multiplier=1).then_inc(const_step, 1)
        P.affine_select(out=causal[:, :], in_=causal[:, :], compare_op=ALU.is_ge, fill=NEG, base=0,
                        pattern=[[-1, 128]], channel_multiplier=1).then_inc(const_step, 1)
        pool.wait_ge(const_step, 9)
        P.tensor_copy(ident16[:, :], ident[:, :]).then_inc(consts, 1)
        pool.dma_start(dram["xs"].rearrange("(n p) d -> p n d", p=128),
                       zeros[:, :].unsqueeze(1).to_broadcast([128, TILES * SLOTS // 128, 2 * D])
                       ).then_inc(z_out, 16)
        pool.dma_start(flat(e_x[:, :, :]).rearrange("p (c n) -> p c n", c=DC),
                       dram["w_q"].rearrange("(c p) n -> p c n", p=128)).then_inc(wx_in, 16)
        for n, w in enumerate(("w_k", "w_v")):
            pool.dma_start(wkv[:, n, :], dram[w][0:128, :]).then_inc(wx_in, 16)
            pool.dma_start(wkv2[:, n, :], dram[w][128:DCOND, :]).then_inc(wx_in, 16)
        pool.dma_start(wout[:, :, :], dram["w_out"].rearrange("(k p) n -> p k n", p=128)).then_inc(wx_in, 16)
        pool.wait_ge(b_in, 6 * 16)

        def root(i, n):
            pool.wait_ge(var_done, i * 2 + n + 1)
            P.tensor_tensor(rstd[:, :], meanvar[:, :, 1], power[:, 0:NQ], ALU.add).then_inc(pool_step, 1)
            pool.wait_ge(pool_step, i * 2 + n + 1)
            P.tensor_tensor(rstd[:, :], rstd[:, :], power[:, NQ:], ALU.pow).then_inc(rstd_done, 1)

        with nc.gpsimd.Fori(0, NB) as i:
            pool.wait_ge(x_in, i * 16 + 16)
            pool.wait_ge(x1_ready, i + START)
            P.tensor_tensor(x_bo[:, :, :], x_tok[:, :, :],
                            b_rows[:, 0:1, :].to_broadcast([128, NQ, D]), ALU.add).then_inc(xb_done, 1)
            pool.wait_ge(qk_stored, i * 32 + START)
            for n in range(4):
                pool.wait_ge(qhi_done, i * 4 + n + 1)
                P.tensor_tensor(qk[:, 1, n, :], qf[:, n % 2, :], qk[:, 0, n, :],
                                ALU.subtract).then_inc(qlo_done, 1)
            for s in range(STEPS):
                slot, value = r(i, f"s{s}")
                pool.wait_ge(r_empty[slot], value + 1)
                pool.sem_inc(exp_seen, 1)
                diag = probs[:, s % 3, :, 0:128]
                P.affine_select(out=diag, in_=diag, compare_op=ALU.is_ge, fill=0.0, base=0,
                                pattern=[[0, 2], [1, 128]], channel_multiplier=-1).then_inc(probs_ready, 1)
            root(i, 0)
            pool.wait_ge(x1_ready, i + 1 + START)
            P.tensor_tensor(x1_b[:, :, :], x1[:, :, :],
                            b_rows[:, 2:3, :].to_broadcast([128, NQ, D]), ALU.add).then_inc(x1b_done, 1)
            for t in range(NQ):
                pool.wait_ge(e_inv, i * NQ + t + 1)
                e3 = e_x[:, t % 2, :].rearrange("p (h k) -> p h k", h=XH)
                P.tensor_tensor(e3, e3, xinv[:, t % 2, :].unsqueeze(2).to_broadcast([128, XH, KV]),
                                ALU.mult).then_inc(e_prob, 1)
            root(i, 1)

    @block.scalar
    def _(act):
        A = nc.scalar
        act.wait_ge(w_in, 4 * 16)
        A.activation(w_hl[:, 0, :, :, :].rearrange("p w c n -> p (w c n)"),
                     probs[:, 0:2, :, :].rearrange("p a b n -> p (a b n)"), ACT.Copy, scale=WS).then_inc(w_hi, 1)
        for n in range(2):
            act.wait_ge(r_full[n], 1)
            A.activation(wqT[:, n * 4:n * 4 + 4, :].rearrange("p k n -> p (k n)"), flat(R[n][:, :, :]),
                         ACT.Copy).then_inc(r_empty[n], 1)

        def hi(i, out, bank, full, value, scale):
            act.wait_ge(full, value + 1)
            A.activation(out, bank, ACT.Copy, scale=scale).then_inc(hi_done, 1)

        def copy_out(i, name, out, bank):
            slot, value = g(i, name)
            act.wait_ge(g_full[slot], value + 1)
            A.activation(out, bank(G[slot]), ACT.Copy).then_inc(g_empty[slot], 1)

        with nc.scalar.Fori(0, NB) as i:
            for c in range(DC):
                slot, value = g(i, f"xT{c}")
                hi(i, xT[:, 0, c, :], G[slot][:, :], g_full[slot], value, XS)
            act.wait_ge(qk_stored, i * 32 + START)
            for n in range(4):
                slot, value = g(i, QK[n])
                act.wait_ge(g_empty[slot], value + 1)
                A.activation(qk[:, 0, n, :], qf[:, n % 2, :], ACT.Copy).then_inc(qhi_done, 1)
            copy_out(i, "cT0", cT[:, 0, :], lambda b: b[:, 0:KV])
            copy_out(i, "cT1", cT[0:DCOND - 128, 1, :], lambda b: b[0:DCOND - 128, 0:KV])
            for n, name in enumerate(("kT", "vT")):
                copy_out(i, name, kvT[:, n, :, :].rearrange("p k s -> p (k s)"), lambda b: b[:, :])
            for c in range(DC):
                slot, value = r(i, f"A{c}")
                hi(i, a_x[:, 0, c, :], flat(R[slot][:, :, :]), r_full[slot], value, WS)
            act.wait_ge(m_stored, i * 16 + START)
            slot, value = g(i, "mT")
            act.wait_ge(g_full[slot], value + 1)
            A.activation(neg_maxT[:, :], G[slot][0:H, :], ACT.Copy, scale=-1.0).then_inc(g_empty[slot], 1)
            for n in range(2):
                slot, value = r(i, f"VW{n}")
                hi(i, vw[:, 0, n * 4:n * 4 + 4, :].rearrange("p k n -> p (k n)"), flat(R[slot][:, :, :]),
                   r_full[slot], value, WS)

            def pv_out(gr):
                act.wait_ge(probs_used, i * STEPS + 2 * NQ * (gr + 1) + START)
                A.activation(cu[:, gr % 2, :], PV[gr % 2][:, :], ACT.Copy).then_inc(pv_empty[gr % 2], 1)

            for s in range(STEPS):
                gr, j, _ = step_of(s)
                slot, value = r(i, f"s{s}")
                act.wait_ge(r_full[slot], value + 1)
                act.wait_ge(probs_used, i * STEPS + max(s - 2, 0) + START)
                A.activation(probs[:, s % 3, :, 0:S - 128 * j], R[slot][:, :, 0:S - 128 * j], ACT.Exp,
                             scale=1.0 / (QS * QS)).then_inc(r_empty[slot], 1)
                if s % (2 * NQ) == 1 and gr > 0:
                    pv_out(gr - 1)
            pv_out(GROUPS - 1)
            for src, dst in (("cx", ctxT), ("xa", x1T)):
                for c in range(DC):
                    slot, value = g(i, f"{src}{c}")
                    hi(i, dst[:, 0, c, :], G[slot][:, :], g_full[slot], value, XS)

            def x_exp(t):
                slot, value = r(i, f"S{t}")
                act.wait_ge(r_empty[slot], value + 1)
                A.activation(e_x[:, t % 2, :], e_x[:, t % 2, :], ACT.Exp,
                             scale=XD ** -0.5 / (WS * XS)).then_inc(e_exp, 1)

            def p_hi(t):
                slot, value = r(i, f"T{t}")
                hi(i, pT[:, t % 2, 0, :, :].rearrange("p k q -> p (k q)"), flat(R[slot][:, :, :]),
                   r_full[slot], value, WS)

            x_exp(0)
            x_exp(1)
            p_hi(0)
            x_exp(2)
            p_hi(1)
            x_exp(3)
            p_hi(2)
            p_hi(3)
            act.wait_ge(x2_ready, i + 1)
            A.activation(xhl[:, bass.ds(i * NQ, NQ), 0:D], x2[:, :, :], ACT.Copy, scale=XS).then_inc(xhi_done, 1)
            for c in range(DC):
                copy_out(i, f"xr{c}", x2T[:, c, :], lambda b: b[:, :])

    @block.vector
    def _(dve):
        V = nc.vector
        dve.wait_ge(w_hi, 1)
        V.scalar_tensor_tensor(w_hl[:, 1, :, :, :].rearrange("p w c n -> p (w c n)"),
                               probs[:, 0:2, :, :].rearrange("p a b n -> p (a b n)"), WS,
                               w_hl[:, 0, :, :, :].rearrange("p w c n -> p (w c n)"),
                               ALU.mult, ALU.subtract).then_inc(w_lo, 1)
        dve.wait_ge(b_in, 6 * 16)
        dve.wait_ge(consts, 1)
        V.tensor_scalar(qk_bias[:, 0, :], qk_bias[:, 0, :], QS * HD ** -0.5, None, ALU.mult).then_inc(bias_done, 1)
        V.tensor_scalar(qk_bias[:, 1, :], qk_bias[:, 1, :], QS, None, ALU.mult).then_inc(bias_done, 1)
        dve.wait_ge(bias_done, 2)
        STEPS_DVE = GROUPS + 2 + 2 * NQ
        count = [0]

        with nc.vector.Fori(0, NB) as i:
            def after(ins, first=None):
                count[0] += 1
                ins.then_inc(dve_step, 1)
                if first is not None:
                    dve.wait_ge(first, 1)
                dve.wait_ge(dve_step, i * STEPS_DVE + count[0])

            def lo(name, out, bank, high, full, empty, value, scale):
                dve.wait_ge(hi_done, his(i, name))
                V.scalar_tensor_tensor(out, bank, scale, high, ALU.mult, ALU.subtract).then_inc(empty, 1)

            def g_lo(name, dst, c):
                slot, value = g(i, name)
                lo(name, dst[:, 1, c, :], G[slot][:, :], dst[:, 0, c, :], g_full[slot], g_empty[slot], value, XS)

            def layernorm(n, buf, done, first):
                for t in range(NQ):
                    last = V.bn_stats(stats[:, t, :], buf[:, t, :])
                after(last, consts)
                for t in range(NQ):
                    last = V.bn_aggr(meanvar[:, t, :], stats[:, t, :])
                last.then_inc(var_done, 1)
                dve.wait_ge(rstd_done, i * 2 + n + 1)
                for t in range(NQ):
                    last = V.tensor_scalar(buf[:, t, :], buf[:, t, :], meanvar[:, t, 0:1], rstd[:, t:t + 1],
                                           ALU.subtract, ALU.mult)
                last.then_inc(done, 1)
                dve.wait_ge(done, i + 1 + first)

            for c in range(DC):
                g_lo(f"xT{c}", xT, c)
            for n in range(4):
                dve.wait_ge(qlo_done, i * 4 + max(n - 1, 0) + START)
                slot, value = g(i, QK[n])
                dve.wait_ge(g_full[slot], value + 1)
                scale = QS / (WS * XS) * (HD ** -0.5 if n < 2 else 1.0)
                V.tensor_scalar(qf[:, n % 2, :], G[slot][:, :], scale, qk_bias[:, n // 2, n % 2:n % 2 + 1],
                                ALU.mult, ALU.add).then_inc(g_empty[slot], 1)
            for n in range(2):
                slot, value = g(i, f"v{n}")
                dve.wait_ge(g_full[slot], value + 1)
                V.scalar_tensor_tensor(v_aug[:, 2 * n:2 * n + 2, :, 0:HD],
                                       G[slot][:, :].rearrange("p (t h d) -> p t h d", t=2, h=H), 1.0 / (WS * XS),
                                       b_rows[:, 1:2, :].rearrange("p o (h d) -> p o h d", h=H)
                                       .to_broadcast([128, 2, H, HD]),
                                       ALU.mult, ALU.add).then_inc(g_empty[slot], 1)
            for c in range(DC):
                slot, value = r(i, f"A{c}")
                lo(f"A{c}", a_x[:, 1, c, :], flat(R[slot][:, :, :]), a_x[:, 0, c, :],
                   r_full[slot], r_empty[slot], value, WS)
            for n in range(NQ * PAIRS):
                t, p = n // PAIRS, n % PAIRS
                slot, value = r(i, f"m{n}")
                dve.wait_ge(r_full[slot], value + 1)
                V.tensor_reduce(rowmax[:, t, 2 * p:2 * p + 2], R[slot][:, :, 0:128 * (t + 1)], AX.X,
                                ALU.max).then_inc(r_empty[slot], 1)
            for n in range(2):
                slot, value = r(i, f"VW{n}")
                lo(f"VW{n}", vw[:, 1, n * 4:n * 4 + 4, :].rearrange("p k n -> p (k n)"), flat(R[slot][:, :, :]),
                   vw[:, 0, n * 4:n * 4 + 4, :].rearrange("p k n -> p (k n)"),
                   r_full[slot], r_empty[slot], value, WS)
            for gr in range(GROUPS):
                slot, value = g(i, f"ct{gr}")
                dve.wait_ge(g_full[slot], value + 1)
                bank = G[slot][:, :].rearrange("p (t h d) -> p t h d", t=NQ, h=4)
                after(V.reciprocal(inv[:, gr, :, :], bank[:, :, :, HD]))
                V.tensor_tensor(ctx_tok[:, :, gr * 64:gr * 64 + 64].rearrange("p t (h d) -> p t h d", h=4),
                                bank[:, :, :, 0:HD], inv[:, gr, :, :].unsqueeze(3).to_broadcast([128, NQ, 4, HD]),
                                ALU.mult).then_inc(g_empty[slot], 1)
            for c in range(DC):
                g_lo(f"cx{c}", ctxT, c)
            dve.wait_ge(xb_done, i + 1)
            for n in range(2):
                slot, value = g(i, f"o{n}")
                dve.wait_ge(g_full[slot], value + 1)
                V.scalar_tensor_tensor(x1[:, 2 * n:2 * n + 2, :],
                                       G[slot][:, :].rearrange("p (t d) -> p t d", t=2), 1.0 / (WS * XS),
                                       x_bo[:, 2 * n:2 * n + 2, :], ALU.mult, ALU.add).then_inc(g_empty[slot], 1)
                dve.wait_ge(g_empty[slot], value + 1)
            layernorm(0, x1, x1_ready, START)
            for c in range(DC):
                g_lo(f"xa{c}", x1T, c)

            def x_shift(t):
                slot, value = r(i, f"S{t}")
                dve.wait_ge(r_full[slot], value + 1)
                s3 = flat(R[slot][:, :, :]).rearrange("p (h k) -> p h k", h=XH)
                after(V.tensor_reduce(xmax[:, t % 2, :], s3, AX.X, ALU.max))
                V.tensor_tensor(e_x[:, t % 2, :].rearrange("p (h k) -> p h k", h=XH), s3,
                                xmax[:, t % 2, :].unsqueeze(2).to_broadcast([128, XH, KV]),
                                ALU.subtract).then_inc(r_empty[slot], 1)

            def x_sum(t):
                dve.wait_ge(e_exp, i * NQ + t + 1)
                after(V.tensor_reduce(xsum[:, t % 2, :], e_x[:, t % 2, :].rearrange("p (h k) -> p h k", h=XH),
                                      AX.X, ALU.add))
                V.reciprocal(xinv[:, t % 2, :], xsum[:, t % 2, :]).then_inc(e_inv, 1)

            def p_lo(t):
                slot, value = r(i, f"T{t}")
                lo(f"T{t}", pT[:, t % 2, 1, :, :].rearrange("p k q -> p (k q)"), flat(R[slot][:, :, :]),
                   pT[:, t % 2, 0, :, :].rearrange("p k q -> p (k q)"), r_full[slot], r_empty[slot], value, WS)

            def x_out(t):
                slot, value = g(i, f"O{t}")
                dve.wait_ge(g_full[slot], value + 1)
                V.scalar_tensor_tensor(x2[:, t, :], G[slot][:, 0:D], 1.0 / (WS * WS), x1_b[:, t, :],
                                       ALU.mult, ALU.add).then_inc(g_empty[slot], 1)

            x_shift(0)
            x_shift(1)
            x_sum(0)
            x_sum(1)
            p_lo(0)
            x_shift(2)
            p_lo(1)
            x_sum(2)
            dve.wait_ge(x2_stored, i * 16 + START)
            dve.wait_ge(x1b_done, i + 1)
            x_out(0)
            x_shift(3)
            x_sum(3)
            p_lo(2)
            x_out(1)
            p_lo(3)
            x_out(2)
            x_out(3)
            slot, value = g(i, "O3")
            dve.wait_ge(g_empty[slot], value + 1)
            layernorm(1, x2, x2_ready, 0)
            dve.wait_ge(xhi_done, i + 1)
            V.scalar_tensor_tensor(xhl[:, bass.ds(i * NQ, NQ), D:2 * D], x2[:, :, :], XS,
                                   xhl[:, bass.ds(i * NQ, NQ), 0:D], ALU.mult, ALU.subtract)
            slot, value = g(i, "lg")
            dve.wait_ge(g_full[slot], value + 1)
            V.tensor_copy(logits[:, bass.ds(i * NQ * NE, NQ * NE)], G[slot][:, 0:NQ * NE]).then_inc(g_empty[slot], 1)
            assert count[0] == STEPS_DVE, count

    @block.tensor
    def _(pe):
        M = nc.tensor
        pe.wait_ge(consts, 1)
        pe.wait_ge(wx_in, 6 * 16)
        for n in range(2):
            for k in range(4):
                for c in range(DC):
                    at = k * D + c * 128
                    last = M.transpose(flat(R[n][:, :, :])[:, at:at + 128],
                                       e_x[:, c, (4 * n + k) * 128:(4 * n + k) * 128 + 128], ident[:, :])
            last.then_inc(r_full[n], 1)
        pe.wait_ge(w_lo, 1)

        with nc.tensor.Fori(0, NB) as i:
            def g_open(name):
                slot, value = g(i, name)
                pe.wait_ge(g_empty[slot], value)
                return G[slot], g_full[slot]

            def r_open(name):
                slot, value = r(i, name)
                pe.wait_ge(r_empty[slot], value)
                return R[slot], r_full[slot]

            def g_read(name):
                slot, value = g(i, name)
                pe.wait_ge(g_empty[slot], value + 1)

            def r_read(name):
                slot, value = r(i, name)
                pe.wait_ge(r_empty[slot], value + 1)

            def three(out, left, right, n):
                for k in range(n):
                    for m, (a, b) in enumerate(((0, 0), (0, 1), (1, 0))):
                        last = M.matmul(out, left(a, k), right(b, k), start=(k == 0 and m == 0),
                                        stop=(k == n - 1 and m == 2))
                return last

            def transposed(name, c, src):
                bank, full = g_open(f"{name}{c}")
                for t in range(NQ):
                    last = M.transpose(bank[:, t * 128:t * 128 + 128], src[:, t, c * 128:c * 128 + 128], ident[:, :])
                last.then_inc(full, 1)

            pe.wait_ge(x_in, i * 16 + 16)
            for c in range(DC):
                transposed("xT", c, x_tok)
            for c in range(DC):
                g_read(f"xT{c}")
            for n in range(4):
                bank, full = g_open(QK[n])
                w, m = n // 2, n % 2
                three(bank[:, :], lambda hl, c: w_hl[:, hl, w, c, m * 128:m * 128 + 128],
                      lambda hl, c: xT[:, hl, c, :], DC).then_inc(full, 1)
            for n in range(2):
                bank, full = g_open(f"v{n}")
                for t in range(2):
                    at = (2 * n + t) * 128
                    last = three(bank[:, t * D:t * D + D], lambda hl, c: xT[:, hl, c, at:at + 128],
                                 lambda hl, c: w_hl[:, hl, 2, c, :], DC)
                last.then_inc(full, 1)
            pe.wait_ge(c_in, i * 16 + 16)
            bank, full = g_open("cT0")
            M.matmul(bank[:, 0:KV], cond[:, 0:128], ident[0:KV, 0:KV], start=True, stop=True).then_inc(full, 1)
            pe.wait_ge(consts, 1)
            bank, full = g_open("cT1")
            M.transpose(bank[0:DCOND - 128, 0:KV], cond[:, 128:DCOND], ident[0:KV, 0:KV]).then_inc(full, 1)
            for c in range(2):
                g_read(f"cT{c}")
            for n, name in enumerate(("kT", "vT")):
                bank, full = g_open(name)
                for p in range(PAIRS):
                    M.matmul(bank[:, p * KV:p * KV + KV], wkv[:, n, p * 128:p * 128 + 128], cT[:, 0, :],
                             start=True, stop=False)
                    last = M.matmul(bank[:, p * KV:p * KV + KV], wkv2[:, n, p * 128:p * 128 + 128],
                                    cT[0:DCOND - 128, 1, :], start=False, stop=True)
                last.then_inc(full, 1)
            for c in range(DC):
                pe.wait_ge(consts, 1)
                g_read("kT")
                bank, full = r_open(f"A{c}")
                for p in range(PAIRS):
                    for par in range(2):
                        half = slice(64 * par, 64 * par + 64)
                        last = M.matmul(bank[:, par, p * KV:p * KV + KV], wqT[half, p, c * 128:c * 128 + 128],
                                        kvT[half, 0, p, :], start=True, stop=True)
                last.then_inc(full, 1)
            pe.wait_ge(stack_in, (i + 1) * 12 * 16 + START)
            for n in range(NQ * PAIRS):
                t, p = n // PAIRS, n % PAIRS
                bank, full = r_open(f"m{n}")
                for par in range(2):
                    rows = slice(64 * par, 64 * par + STACK)
                    M.matmul(bank[:, par, 0:128 * (t + 1)], qs[rows, p, t * 128:t * 128 + 128],
                             ks[rows, p, 0:128 * (t + 1)], start=True, stop=False)
                for par in range(2):
                    last = M.matmul(bank[:, par, 128 * t:128 * (t + 1)], ident16[:, :], causal[:, :],
                                    start=False, stop=True)
                last.then_inc(full, 1)
            r_read(f"m{NQ * PAIRS - 1}")
            r_read(f"m{NQ * PAIRS - 2}")
            bank, full = g_open("mT")
            for t in range(NQ):
                last = M.transpose(bank[0:H, t * 128:t * 128 + 128], rowmax[:, t, :], ident[:, :])
            last.then_inc(full, 1)
            for n in range(2):
                pe.wait_ge(consts, 1)
                g_read("vT")
                bank, full = r_open(f"VW{n}")
                rows = slice(64 * n, 64 * n + 64)
                for p in range(PAIRS):
                    at = 64 * (p % 2)
                    last = M.matmul(flat(bank[:, :, :])[at:at + 64, p // 2 * D:p // 2 * D + D], kvT[rows, 1, p, :],
                                    wout[rows, p, :], start=True, stop=True)
                last.then_inc(full, 1)

            def score(s):
                gr, j, k = step_of(s)
                bank, full = r_open(f"s{s}")
                p = 2 * gr + k
                for par in range(2):
                    rows = slice(64 * par, 64 * par + STACK + 1)
                    last = M.matmul(bank[:, par, 0:S - 128 * j], ks[rows, p, 128 * j:128 * j + 128],
                                    qs[rows, p, 128 * j:S], start=True, stop=True)
                last.then_inc(full, 1)

            def weigh(s):
                gr, j, k = step_of(s)
                if j == 0 and k == 0:
                    pe.wait_ge(pv_empty[gr % 2], i * 2 + gr // 2 + START)
                pe.wait_ge(probs_ready, i * STEPS + s + 1)
                for par in range(2):
                    at = 32 * (2 * k + par)
                    last = M.matmul(PV[gr % 2][at:at + 32, 128 * j:S], v_aug[:, j, 4 * gr + 2 * k + par, :],
                                    probs[:, s % 3, par, 0:S - 128 * j], start=(j == 0), stop=(j == NQ - 1))
                last.then_inc(probs_used, 1)

            def tokens(gr):
                pe.wait_ge(pv_empty[gr % 2], i * 2 + gr // 2 + 1 + START)
                bank, full = g_open(f"ct{gr}")
                for t in range(NQ):
                    last = M.transpose(bank[:, t * 128:t * 128 + 128], cu[:, gr % 2, t * 128:t * 128 + 128], ident[:, :])
                last.then_inc(full, 1)

            g_read("v0")
            g_read("v1")
            pe.wait_ge(m_in, (i + 1) * 32)
            score(0)
            score(1)
            for s in range(STEPS):
                weigh(s)
                gr = s // (2 * NQ)
                if s + 2 < STEPS:
                    score(s + 2)
                if s % (2 * NQ) == 3 and gr > 0:
                    tokens(gr - 1)
            tokens(GROUPS - 1)
            for gr in range(GROUPS):
                g_read(f"ct{gr}")
            for c in range(DC):
                transposed("cx", c, ctx_tok)
            for c in range(DC):
                g_read(f"cx{c}")
            for n in range(2):
                bank, full = g_open(f"o{n}")
                for t in range(2):
                    at = (2 * n + t) * 128
                    last = three(bank[:, t * D:t * D + D], lambda hl, c: ctxT[:, hl, c, at:at + 128],
                                 lambda hl, c: w_hl[:, hl, 3, c, :], DC)
                last.then_inc(full, 1)
            pe.wait_ge(x1_ready, i + 1 + START)
            for c in range(DC):
                transposed("xa", c, x1)
            for c in range(DC):
                g_read(f"xa{c}")

            def x_score(t):
                bank, full = r_open(f"S{t}")
                for half in range(2):
                    last = three(bank[:, half, :], lambda hl, c: x1T[:, hl, c, t * 128:t * 128 + 128],
                                 lambda hl, c: a_x[:, hl, c, half * 512:half * 512 + 512], DC)
                last.then_inc(full, 1)

            def x_prob(t):
                pe.wait_ge(e_prob, i * NQ + t + 1)
                bank, full = r_open(f"T{t}")
                for k in range(PAIRS):
                    last = M.transpose(flat(bank[:, :, :])[:, k * 128:k * 128 + 128],
                                       e_x[:, t % 2, k * 128:k * 128 + 128], ident[:, :])
                last.then_inc(full, 1)

            def x_out(t):
                r_read(f"T{t}")
                bank, full = g_open(f"O{t}")
                three(bank[:, 0:D], lambda hl, k: pT[:, t % 2, hl, k, :],
                      lambda hl, k: vw[:, hl, k, :], PAIRS).then_inc(full, 1)

            x_score(0)
            x_score(1)
            x_prob(0)
            x_score(2)
            x_prob(1)
            x_out(0)
            x_score(3)
            x_prob(2)
            x_out(1)
            x_prob(3)
            x_out(2)
            x_out(3)
            pe.wait_ge(x2_ready, i + 1)
            for c in range(DC):
                transposed("xr", c, x2)
            for c in range(DC):
                g_read(f"xr{c}")
            bank, full = g_open("lg")
            for t in range(NQ):
                for c in range(DC):
                    last = M.matmul(bank[:, t * NE:t * NE + NE], x2T[:, c, t * 128:t * 128 + 128],
                                    keep["WgT"][:, c, :], start=(c == 0), stop=(c == DC - 1))
            last.then_inc(full, 1)


def expert_block(nc, ctx, dram, keep):
    ident, ident16, logits, xhl = keep["ident"], keep["ident16"], keep["logits"], keep["xhl"]

    def sb(name, shape, dt=F32):
        return ctx.enter_context(nc.sbuf_tensor(name, shape, dt))

    def sem(name):
        return ctx.enter_context(nc.semaphore(name))

    before = sb("before", [128, 128], F16)
    ones16 = sb("ones16", [128, 128], F16)
    w_scale = sb("w_scale", [128, 1])
    iota_e = sb("iota_e", [128, NE])
    iota_s = sb("iota_s", [128, NE])
    iota_t = sb("iota_t", [128, TILES])
    top = sb("top", [128, NT, 8])
    topi = sb("topi", [128, NT, 8], U32)
    topf = sb("topf", [128, NT, 2])
    gap = sb("gap", [128, NT])
    gate = sb("gate", [128, 2, NT])
    hot = sb("hot", [128, 2, NT, NE])
    hot16 = sb("hot16", [128, NT, NE], F16)
    run = sb("run", [128, 2, NT, NE])
    fits = sb("fits", [128, NE, NE])
    tiles_e = sb("tiles_e", [128, NE])
    upto = sb("upto", [128, 2, NE])
    pos = sb("pos", [128, NT, NE])
    pick = sb("pick", [128, 2, NT, NE])
    slot_f = sb("slot_f", [128, 2, NT])
    slot = sb("slot", [128, 2, NT], I32)
    below = sb("below", [128, TILES, NE])
    eid_f = sb("eid_f", [128, TILES])
    eid = sb("eid", [128, TILES], I32)
    b1r = sb("b1r", [NE * FM, 128])
    b1T = sb("b1T", [128, NE * FM])
    b1 = sb("b1", [128, 2, FM])
    w1f = sb("w1f", [128, 2, DC, FF])
    w2f = sb("w2f", [128, 2, FM, D])
    w1 = sb("w1", [128, 2, 2, DC, FF], F16)
    w2 = sb("w2", [128, 2, 2, FM, D], F16)
    xg = sb("xg", [128, 2, 2, 2 * D], F16)
    xT = sb("xT2", [128, 2, 2 * DC, SLOTS], F16)
    hf = sb("hf", [128, FM, SLOTS])
    h = sb("h", [128, 2, 2, FM, SLOTS], F16)
    b2_rows = sb("b2_rows", [128, NE * D])
    b2 = sb("b2", [128, 2, D])
    y = sb("y", [128, 2, 2, D])
    power = sb("power2", [128, 2 * NQ])
    parts = sb("parts", [128, NT, 2, D])
    z = sb("z", [128, NT, D])
    stats = sb("stats2", [128, NQ, 6])
    meanvar = sb("meanvar2", [128, NQ, 2])
    rstd = sb("rstd2", [128, NQ])

    HB = [ctx.enter_context(nc.psum_tensor(f"HB{i}", [128, 2, SLOTS], F32)) for i in range(4)]
    YB = [ctx.enter_context(nc.psum_tensor(f"YB{i}", [128, 2, D], F32)) for i in range(2)]
    XB = ctx.enter_context(nc.psum_tensor("XB", [128, 2 * DC, SLOTS], F16))
    RB = ctx.enter_context(nc.psum_tensor("RB", [128, 512], F32))
    rank, total = RB[:, 0:128], RB[:, 128:256]

    const_step, consts, rt_step, ranks = sem("ec_step"), sem("ec_done"), sem("rt_step"), sem("ranks")
    gap_done, gexp_done, slot_done, eid_done, b1_in = (
        sem("gap_done"), sem("gexp_done"), sem("slot_done"), sem("eid_done"), sem("b1_in"))
    scattered = sem("scattered")
    w1_in = [sem(f"w1_in{i}") for i in range(2)]
    w2_in = [sem(f"w2_in{i}") for i in range(2)]
    xg_in = [sem(f"xg_in{i}") for i in range(2)]
    b2_in, b2_done = sem("b2_in"), sem("b2_done")
    w2_scaled = sem("w2_scaled")
    w1_hi, w2_hi, w1_split, w2_split = sem("w1_hi"), sem("w2_hi"), sem("w1_split"), sem("w2_split")
    xt_full, xt_done, b1_done = sem("xt_full"), sem("xt_done"), sem("b1_done")
    h_full, h_gelu, h_hi, h_split = sem("h_full"), sem("h_gelu"), sem("h_hi"), sem("h_split")
    y_full, y_done = sem("y_full"), sem("y_done")
    y_out = [sem(f"y_out{i}") for i in range(2)]
    hot_done, x2_in = sem("hot_done"), sem("x2_in")
    parts_in = [sem(f"parts_in{i}") for i in range(NT // NQ)]
    var_done, pool_step, rstd_done = sem("var2_done"), sem("pool2_step"), sem("rstd2_done")
    z_done, stored = sem("z_done"), sem("stored")

    TRIPS = (TILES - 3) // 2
    assert TILES % 2 == 1 and NT // NQ * NQ == NT and T // SLOTS <= NE

    def run_steps(eng, step):
        step(0, 0, 0)
        step(1, 0, 1)
        with eng.Fori(0, TRIPS) as i:
            step(2 * i + 2, i + 1, 0)
            step(2 * i + 3, i + 1, 1)
        step(TILES - 1, TILES // 2, 0)

    def is_int(n, *values):
        return isinstance(n, int) and n in values

    def following(n, j, q):
        return n + 1, j + q, 1 - q

    block = ctx.enter_context(nc.Block())

    @block.sync
    def _(sp):
        sp.dma_start(b1r[:, :], dram["b1"].rearrange("e (m p) -> (e m) p", p=128)).then_inc(b1_in, 16)
        sp.dma_start(b2_rows[:, :], dram["b2"].rearrange("e d -> (e d)")
                     .partition_broadcast(128)).then_inc(b2_in, 16)
        sp.wait_ge(eid_done, 1)

        def load(n, j, q):
            old = not is_int(n, 0, 1)
            e = nc.sync.value_load(eid[0:1, bass.ds(n, 1)], min_val=0, max_val=NE - 1)
            if old:
                sp.wait_ge(w1_split, n - 1)
            sp.dma_start(w1f[:, q, :, :], dram["W1"][bass.ds(e * D, D), :]
                         .rearrange("(c p) f -> p c f", p=128)).then_inc(w1_in[q], 16)
            if old:
                sp.wait_ge(w2_split, n - 1)
            sp.dma_start(w2f[:, q, :, :], dram["W2"][bass.ds(e * FF, FF), :]
                         .rearrange("(m p) d -> p m d", p=128)).then_inc(w2_in[q], 16)
            if old:
                sp.wait_ge(xt_full, n - 1)
            else:
                sp.wait_ge(scattered, 2 * NT * 16)
            sp.dma_start(xg[:, q, :, :], dram["xs"][bass.ds(n * SLOTS, SLOTS), :]
                         .rearrange("(t p) d -> p t d", p=128)).then_inc(xg_in[q], 16)

        run_steps(nc.sync, load)
        sp.dma_start(z[:, :, :], dram["x2"].rearrange("(t p) d -> p t d", p=128)).then_inc(x2_in, 16)
        for k in range(NT // NQ):
            sp.wait_ge(z_done, k + 1)
            sp.dma_start(dram["out"][k * S:(k + 1) * S, :].rearrange("(t p) d -> p t d", p=128),
                         z[:, k * NQ:(k + 1) * NQ, :]).then_inc(stored, 16)
        sp.wait_ge(stored, NT // NQ * 16)

    @block.gpsimd
    def _(pool):
        P = nc.gpsimd
        P.memset(before[:, :], 0.0).then_inc(const_step, 1)
        P.memset(ones16[:, :], 1.0).then_inc(const_step, 1)
        P.iota(topi[:, 0, :], pattern=[[1, NE]], base=0, channel_multiplier=0).then_inc(const_step, 1)
        P.iota(eid[:, :], pattern=[[1, TILES]], base=0, channel_multiplier=0).then_inc(const_step, 1)
        P.memset(power[:, 0:NQ], EPS).then_inc(const_step, 1)
        P.memset(power[:, NQ:], -0.5).then_inc(const_step, 1)
        P.memset(w_scale[:, :], WS).then_inc(const_step, 1)
        pool.wait_ge(const_step, 7)
        P.affine_select(out=before[:, :], in_=before[:, :], compare_op=ALU.is_ge, fill=1.0, base=0,
                        pattern=[[-1, 128]], channel_multiplier=1).then_inc(consts, 1)
        P.tensor_copy(iota_e[:, :], topi[:, 0, :]).then_inc(consts, 1)
        P.tensor_copy(iota_t[:, :], eid[:, :]).then_inc(consts, 1)
        pool.wait_ge(slot_done, 1)
        for t in range(NT):
            for c in range(2):
                pool.indirect_dma_start(out=dram["xs"], out_offset=bass.IndirectOffsetOnAxis(slot[:, c, t:t + 1], 0),
                                        in_=xhl[:, t, :], in_offset=None).then_inc(scattered, 16)

        def split(n, j, q):
            pool.wait_ge(w2_in[q], j * 16 + 16)
            scaled = w2f[:, q, :, :].rearrange("p m d -> p (m d)")
            P.tensor_tensor(scaled, scaled, w_scale[:, :].to_broadcast([128, FM * D]), ALU.mult).then_inc(w2_scaled, 1)
            pool.wait_ge(w2_hi, n + 1)
            P.tensor_tensor(w2[:, q, 1, :, :].rearrange("p m d -> p (m d)"), scaled,
                            w2[:, q, 0, :, :].rearrange("p m d -> p (m d)"), ALU.subtract).then_inc(w2_split, 1)

        run_steps(nc.gpsimd, split)
        pool.wait_ge(y_out[0], (TILES + 1) // 2 * 16)
        pool.wait_ge(y_out[1], TILES // 2 * 16)

        def gather(k):
            for t in range(k * NQ, (k + 1) * NQ):
                for c in range(2):
                    pool.indirect_dma_start(out=parts[:, t, c, :], out_offset=None, in_=dram["ys"],
                                            in_offset=bass.IndirectOffsetOnAxis(slot[:, c, t:t + 1], 0)
                                            ).then_inc(parts_in[k], 16)

        def root(k):
            pool.wait_ge(var_done, k + 1)
            P.tensor_tensor(rstd[:, :], meanvar[:, :, 1], power[:, 0:NQ], ALU.add).then_inc(pool_step, 1)
            pool.wait_ge(pool_step, k + 1)
            P.tensor_tensor(rstd[:, :], rstd[:, :], power[:, NQ:], ALU.pow).then_inc(rstd_done, 1)

        gather(0)
        for k in range(1, NT // NQ):
            gather(k)
            root(k - 1)
        root(NT // NQ - 1)

    @block.scalar
    def _(act):
        A = nc.scalar
        act.wait_ge(gap_done, 1)
        A.activation(gate[:, 1, :], gap[:, :], ACT.Exp).then_inc(gexp_done, 1)

        def w1_high(n, j, q):
            act.wait_ge(w1_in[q], j * 16 + 16)
            if not is_int(n, 0, 1):
                act.wait_ge(h_full, 4 * n - 4)
            A.activation(w1[:, q, 0, :, :].rearrange("p c f -> p (c f)"),
                         w1f[:, q, :, :].rearrange("p c f -> p (c f)"), ACT.Copy, scale=WS).then_inc(w1_hi, 1)

        def store(n, q):
            act.wait_ge(y_done, n + 1)
            act.dma_start(dram["ys"][bass.ds(n * SLOTS, SLOTS), :].rearrange("(t p) d -> p t d", p=128),
                          y[:, q, :, :]).then_inc(y_out[q], 16)

        def step(n, j, q):
            act.wait_ge(b1_done, n + 1)
            for b in range(4):
                act.wait_ge(h_full, 4 * n + b + 1)
                if not is_int(n, 0):
                    act.wait_ge(h_split, 4 * n - 3 + b)
                for m in range(2):
                    last = A.activation(hf[:, 2 * b + m, :], HB[b][:, m, :], ACT.Gelu,
                                        bias=b1[:, q, 2 * b + m:2 * b + m + 1], scale=1.0 / (WS * XS))
                last.then_inc(h_gelu, 1)
            if not is_int(n, TILES - 1):
                w1_high(*following(n, j, q))
            act.wait_ge(w2_scaled, n + 1)
            if not is_int(n, 0, 1):
                act.wait_ge(y_full, n - 1)
            A.activation(w2[:, q, 0, :, :].rearrange("p m d -> p (m d)"),
                         w2f[:, q, :, :].rearrange("p m d -> p (m d)"), ACT.Copy).then_inc(w2_hi, 1)
            if not is_int(n, 0, 1):
                store(n - 2, q)

        w1_high(0, 0, 0)
        run_steps(nc.scalar, step)
        store(TILES - 2, 1)
        store(TILES - 1, 0)

    @block.vector
    def _(dve):
        V = nc.vector
        count = [0]

        def after(ins):
            count[0] += 1
            ins.then_inc(rt_step, 1)
            dve.wait_ge(rt_step, count[0])

        def wide(ap, *shape):
            return ap.to_broadcast([128, *shape])

        dve.wait_ge(consts, 3)
        for t in range(NT):
            last = V.max(top[:, t, :], logits[:, t * NE:t * NE + NE])
        after(last)
        V.tensor_tensor(gap[:, :], top[:, :, 1], top[:, :, 0], ALU.subtract).then_inc(gap_done, 1)
        for t in range(NT):
            last = V.max_index(topi[:, t, :], top[:, t, :], logits[:, t * NE:t * NE + NE])
        after(last)
        after(V.tensor_copy(topf[:, :, :], topi[:, :, 0:2]))
        for c in range(2):
            last = V.tensor_tensor(hot[:, c, :, :], wide(topf[:, :, c:c + 1], NT, NE),
                                   wide(iota_e[:, :].unsqueeze(1), NT, NE), ALU.is_equal)
        after(last)
        V.tensor_tensor(hot16[:, :, :], hot[:, 0, :, :], hot[:, 1, :, :], ALU.add).then_inc(hot_done, 1)
        V.tensor_scalar(iota_s[:, :], iota_e[:, :], float(SLOTS), None, ALU.mult)
        dve.wait_ge(ranks, 1)
        V.tensor_copy(b1T[:, :], RB[:, 256:256 + NE * FM])
        after(V.tensor_copy(run[:, 0, :, :], total.rearrange("p (t e) -> p t e", e=NE)))
        cur = 0
        for k in (1, 2, 4, 8):
            V.tensor_copy(run[:, 1 - cur, 0:k, :], run[:, cur, 0:k, :])
            after(V.tensor_tensor(run[:, 1 - cur, k:, :], run[:, cur, k:, :], run[:, cur, 0:NT - k, :], ALU.add))
            cur = 1 - cur
        after(V.tensor_tensor(fits[:, :, :], wide(run[:, cur, NT - 1, :].unsqueeze(2), NE, NE),
                              wide(iota_s[:, :].unsqueeze(1), NE, NE), ALU.is_gt))
        after(V.tensor_reduce(tiles_e[:, :], fits[:, :, :], AX.X, ALU.add))
        after(V.tensor_copy(upto[:, 0, :], tiles_e[:, :]))
        at = 0
        for k in (1, 2, 4):
            V.tensor_copy(upto[:, 1 - at, 0:k], upto[:, at, 0:k])
            after(V.tensor_tensor(upto[:, 1 - at, k:], upto[:, at, k:], upto[:, at, 0:NE - k], ALU.add))
            at = 1 - at
        after(V.tensor_tensor(below[:, :, :], wide(upto[:, at, :].unsqueeze(1), TILES, NE),
                              wide(iota_t[:, :].unsqueeze(2), TILES, NE), ALU.is_le))
        after(V.tensor_reduce(eid_f[:, :], below[:, :, :], AX.X, ALU.add))
        V.tensor_scalar(eid[:, :], eid_f[:, :], NE - 1.0, None, ALU.min).then_inc(eid_done, 1)
        V.tensor_tensor(upto[:, 1 - at, :], upto[:, at, :], tiles_e[:, :], ALU.subtract)
        after(V.tensor_tensor(run[:, 1 - cur, :, :], run[:, cur, :, :],
                              total.rearrange("p (t e) -> p t e", e=NE), ALU.subtract))
        after(V.tensor_tensor(run[:, cur, :, :], run[:, 1 - cur, :, :],
                              rank.rearrange("p (t e) -> p t e", e=NE), ALU.add))
        after(V.scalar_tensor_tensor(pos[:, :, :], wide(upto[:, 1 - at, :].unsqueeze(1), NT, NE), float(SLOTS),
                                     run[:, cur, :, :], ALU.mult, ALU.add))
        after(V.tensor_tensor(pick[:, :, :, :], hot[:, :, :, :], wide(pos[:, :, :].unsqueeze(1), 2, NT, NE), ALU.mult))
        after(V.tensor_reduce(slot_f[:, :, :], pick[:, :, :, :], AX.X, ALU.add))
        V.tensor_copy(slot[:, :, :], slot_f[:, :, :]).then_inc(slot_done, 1)
        dve.wait_ge(gexp_done, 1)
        after(V.tensor_scalar(gap[:, :], gate[:, 1, :], 1.0, None, ALU.add))
        after(V.reciprocal(gate[:, 0, :], gap[:, :]))
        after(V.tensor_tensor(gate[:, 1, :], gate[:, 1, :], gate[:, 0, :], ALU.mult))
        dve.wait_ge(eid_done, 1)

        def ready(n, j, q):
            e = nc.vector.value_load(eid[0:1, bass.ds(n, 1)], min_val=0, max_val=NE - 1)
            V.tensor_copy(b1[:, q, :], b1T[:, bass.ds(e * FM, FM)]).then_inc(b1_done, 1)
            dve.wait_ge(xt_full, n + 1)
            V.tensor_copy(xT[:, q, :, :], XB[:, :, :]).then_inc(xt_done, 1)
            dve.wait_ge(w1_hi, n + 1)
            V.scalar_tensor_tensor(w1[:, q, 1, :, :].rearrange("p c f -> p (c f)"),
                                   w1f[:, q, :, :].rearrange("p c f -> p (c f)"), WS,
                                   w1[:, q, 0, :, :].rearrange("p c f -> p (c f)"),
                                   ALU.mult, ALU.subtract).then_inc(w1_split, 1)

        def output(n, j, q):
            e = nc.vector.value_load(eid[0:1, bass.ds(n, 1)], min_val=0, max_val=NE - 1)
            V.tensor_copy(b2[:, q, :], b2_rows[:, bass.ds(e * D, D)]).then_inc(b2_done, 1)
            dve.wait_ge(b2_done, n + 1)
            dve.wait_ge(y_full, n + 1)
            if not is_int(n, 0, 1):
                dve.wait_ge(y_out[q], j * 16)
            V.scalar_tensor_tensor(y[:, q, :, :], YB[q][:, :, :], 1.0 / (WS * XS),
                                   wide(b2[:, q, :].unsqueeze(1), 2, D), ALU.mult, ALU.add).then_inc(y_done, 1)

        def step(n, j, q):
            if not is_int(n, 0, 1):
                dve.wait_ge(y_full, n - 1)
            for b in range(4):
                pair = slice(2 * b, 2 * b + 2)
                dve.wait_ge(h_gelu, 4 * n + b + 1)
                V.tensor_scalar(h[:, q, 0, pair, :], hf[:, pair, :], XS, None, ALU.mult).then_inc(h_hi, 1)
                dve.wait_ge(h_hi, 4 * n + b + 1)
                V.scalar_tensor_tensor(h[:, q, 1, pair, :], hf[:, pair, :], XS, h[:, q, 0, pair, :],
                                       ALU.mult, ALU.subtract).then_inc(h_split, 1)
            if not is_int(n, TILES - 1):
                ready(*following(n, j, q))
            if not is_int(n, 0):
                output(n - 1, j - 1 + q, 1 - q)

        dve.wait_ge(b2_in, 16)
        ready(0, 0, 0)
        run_steps(nc.vector, step)
        output(TILES - 1, TILES // 2, 0)

        dve.wait_ge(x2_in, 16)
        for k in range(NT // NQ):
            dve.wait_ge(parts_in[k], 2 * NQ * 16)
            tiles = range(k * NQ, (k + 1) * NQ)
            for c in range(2):
                for t in tiles:
                    last = V.scalar_tensor_tensor(z[:, t, :], parts[:, t, c, :], gate[:, c, t:t + 1], z[:, t, :],
                                                  ALU.mult, ALU.add)
                after(last)
            for t in tiles:
                last = V.bn_stats(stats[:, t % NQ, :], z[:, t, :])
            after(last)
            for t in tiles:
                last = V.bn_aggr(meanvar[:, t % NQ, :], stats[:, t % NQ, :])
            last.then_inc(var_done, 1)
            dve.wait_ge(rstd_done, k + 1)
            for t in tiles:
                last = V.tensor_scalar(z[:, t, :], z[:, t, :], meanvar[:, t % NQ, 0:1], rstd[:, t % NQ:t % NQ + 1],
                                       ALU.subtract, ALU.mult)
            last.then_inc(z_done, 1)

    @block.tensor
    def _(pe):
        M = nc.tensor
        pe.wait_ge(consts, 3)
        pe.wait_ge(b1_in, 16)
        M.transpose(RB[:, 256:256 + NE * FM], b1r[:, :], ident[0:NE * FM, 0:NE * FM])
        pe.wait_ge(hot_done, 1)
        hot2 = hot16[:, :, :].rearrange("p t e -> p (t e)")
        M.matmul(rank, before[:, :], hot2, start=True, stop=True)
        M.matmul(total, ones16[:, :], hot2, start=True, stop=True).then_inc(ranks, 1)

        def three(out, left, right, n):
            for k in range(n):
                for m, (a, b) in enumerate(((0, 0), (0, 1), (1, 0))):
                    last = M.matmul(out, left(a, k), right(b, k), start=(k == 0 and m == 0),
                                    stop=(k == n - 1 and m == 2))
            return last

        def transposes(n, j, q):
            pe.wait_ge(xg_in[q], j * 16 + 16)
            if not is_int(n, 0):
                pe.wait_ge(xt_done, n)
            for k in range(2 * DC):
                for t in range(2):
                    last = M.transpose(XB[:, k, t * 128:t * 128 + 128], xg[:, q, t, k * 128:k * 128 + 128],
                                       ident16[:, :])
            last.then_inc(xt_full, 1)

        def second(n, j, q):
            pe.wait_ge(h_split, 4 * n + 4)
            pe.wait_ge(w2_split, n + 1)
            if not is_int(n, 0, 1):
                pe.wait_ge(y_done, n - 1)
            for t in range(2):
                last = three(YB[q][:, t, :], lambda hl, m: h[:, q, hl, m, t * 128:t * 128 + 128],
                             lambda hl, m: w2[:, q, hl, m, :], FM)
            last.then_inc(y_full, 1)

        def step(n, j, q):
            pe.wait_ge(xt_done, n + 1)
            pe.wait_ge(w1_split, n + 1)
            for b in range(4):
                if not is_int(n, 0):
                    pe.wait_ge(h_gelu, 4 * n - 3 + b)
                for m in range(2):
                    at = (2 * b + m) * 128
                    last = three(HB[b][:, m, :], lambda hl, c: w1[:, q, hl, c, at:at + 128],
                                 lambda hl, c: xT[:, q, hl * DC + c, :], DC)
                last.then_inc(h_full, 1)
            if not is_int(n, TILES - 1):
                transposes(*following(n, j, q))
            if not is_int(n, 0):
                second(n - 1, j - 1 + q, 1 - q)

        transposes(0, 0, 0)
        run_steps(nc.tensor, step)
        second(TILES - 1, TILES // 2, 0)


def decoder_layer(nc, dram):
    with ExitStack() as outer:
        keep = {}
        for name, shape, dt in (("ident", [128, 128], F32), ("ident16", [128, 128], F16),
                                ("logits", [128, NT * NE], F32), ("xhl", [128, NT, 2 * D], F16),
                                ("WgT", [128, DC, NE], F32)):
            keep[name] = outer.enter_context(nc.sbuf_tensor(name, shape, dt))
        with ExitStack() as ctx:
            attention_block(nc, ctx, dram, keep)
        with ExitStack() as ctx:
            expert_block(nc, ctx, dram, keep)


_INS = {"x": "x", "ctx_768": "cond", "L0_attn_Wq": "Wq", "L0_attn_bq": "bq", "L0_attn_Wk": "Wk", "L0_attn_bk": "bk",
        "L0_attn_Wv": "Wv", "L0_attn_bv": "bv", "L0_attn_Wo": "Wo", "L0_attn_bo": "bo",
        "L0_xattn_w_q": "w_q", "L0_xattn_w_k": "w_k", "L0_xattn_w_v": "w_v", "L0_xattn_w_out": "w_out",
        "L0_xattn_b_out": "b_out", "L0_ffn_Wg": "WgT", "L0_ffn_W1": "W1", "L0_ffn_b1": "b1",
        "L0_ffn_W2": "W2", "L0_ffn_b2": "b2"}


def kernel(**inputs):
    import numpy as np
    import concourse.bacc as bacc
    from concourse.bass_utils import run_bass_kernel_spmd

    nc = bacc.Bacc("TRN2", target_bir_lowering=False, num_devices=1)
    arrays, dram = {}, {}
    for name, short in _INS.items():
        a = np.asarray(inputs[name])
        if short == "x" or short == "cond" or short in ("W1", "W2"):
            a = a.reshape(-1, a.shape[-1])
        elif short in ("bq", "bk"):
            a = a.reshape(DC, 128).T
        elif short == "WgT":
            a = a.T.reshape(DC, 128, NE).transpose(1, 0, 2)
        a = np.ascontiguousarray(a)
        arrays["in_" + short] = a
        dram[short] = nc.dram_tensor("in_" + short, a.shape, mybir.dt.from_np(a.dtype), kind="ExternalInput").ap()
    dram["out"] = nc.dram_tensor("out", (T, D), F32, kind="ExternalOutput").ap()
    for name, shape, dt in (("qk", (2, 2 * D, S), F16), ("m", (H, S), F16), ("x2", (T, D), F32),
                            ("xs", (TILES * SLOTS, 2 * D), F16), ("ys", (TILES * SLOTS, D), F32)):
        dram[name] = nc.dram_tensor("scratch_" + name, shape, dt).ap()
    decoder_layer(nc, dram)
    r = run_bass_kernel_spmd(nc, [arrays], core_ids=[0])
    return r.results[0]["out"].reshape(NB, S, D)
```

```python
import concourse.bass as bass
from concourse import mybir
from contextlib import ExitStack

F32 = mybir.dt.float32
F16 = mybir.dt.float16
I32 = mybir.dt.int32
U32 = mybir.dt.uint32
ALU = mybir.AluOpType
ACT = mybir.ActivationFunctionType
AX = mybir.AxisListType

NB, S, D = 4, 512, 256
T = NB * S
NQ = S // 128
NT = T // 128
DC = D // 128
H, HD = 16, 16
PAIRS = H // 2
GROUPS = H // 4
XH, XD, KV, DCOND = 16, 64, 64, 192
XA = XH * XD
NE, FF = 8, 1024
FM = FF // 128
SLOTS = 256
TILES = (2 * T + NE * (SLOTS - 1)) // SLOTS
EPS = 1e-5
WS = 64.0
XS = 16.0
QS = 4.0
NEG = -60000.0
STACK = 3 * HD


def max_items():
    items = []
    for t in range(NQ):
        pairs = max(1, 512 // (128 * (t + 1)))
        if PAIRS % pairs:
            pairs = 1
        items += [(t, par, p, pairs) for par in range(2) for p in range(0, PAIRS, pairs)]
    return items


MAXES = max_items()
UNITS = GROUPS * NQ


def project_steps(first):
    return ([("xT", 2 * first + n) for n in range(2)] + [("q", 4 * first + n) for n in range(4)]
            + [("v", 2 * first + n) for n in range(2)])


def prepare_steps():
    steps = project_steps(0) + [("cT", 0), ("cT", 1), ("W", 0), ("W", 1)]
    steps += [("kv", n) for n in range(4)] + project_steps(1)
    n = 0
    for step in [("A", n) for n in range(8)] + [("VW", n) for n in range(2 * NB)]:
        steps.append(step)
        steps += [("m", k) for k in range(n, min(n + 3, len(MAXES)))]
        n += 3
    return steps + [("mT", 0), ("mT", 1)]


def alpha_steps():
    steps, n = [("s", 0), ("s", 1)], 0
    for u in range(UNITS):
        gr, j = u // NQ, u % NQ
        upto = len(MAXES) * (gr * 10 + (4, 7, 9, 10)[j]) // (10 * GROUPS)
        half = (n + upto + 1) // 2
        if u + 1 < UNITS:
            steps.append(("s", 2 * u + 2))
        steps += [("m", k) for k in range(n, half)]
        if u + 1 < UNITS:
            steps.append(("s", 2 * u + 3))
        steps.append(("w", u))
        if j == 1 and gr > 0:
            steps.append(("ct", gr - 1))
        steps += [("m", k) for k in range(half, upto)]
        n = upto
    return steps + [("mT", 0), ("mT", 1)]


PREPARE = prepare_steps()
ALPHA = alpha_steps()
BETA = [("ct", 3), ("cx", 0), ("xT", 0), ("cx", 1), ("xT", 1), ("o", 0), ("o", 1), ("q", 0), ("q", 1), ("q", 2),
        ("q", 3), ("xa", 0), ("xa", 1), ("v", 0), ("S", 0), ("S", 1), ("v", 1), ("S", 2), ("T", 0), ("S", 3),
        ("O", 0), ("T", 1), ("O", 1), ("T", 2), ("O", 2), ("T", 3), ("O", 3)]
G_KINDS = ("xT", "q", "v", "cT", "m", "mT", "ct", "cx", "o", "xa", "O")
R_KINDS = ("W", "kv", "A", "VW", "s", "S", "T")


class Slots:

    def __init__(self, steps, kinds, banks, full, empty, start):
        self.uses = [step for step in steps if step[0] in kinds]
        self.banks, self.full, self.empty, self.start = banks, full, empty, start

    def at(self, i, kind, n):
        use, k = self.uses.index((kind, n)), len(self.banks)
        assert isinstance(i, int) or len(self.uses) % k == 0
        return use % k, i * (len(self.uses) // k) + use // k + self.start


def flat(ap):
    return ap.rearrange("p a b -> p (a b)")


def positive(eng, sem, value):
    if not isinstance(value, int) or value > 0:
        eng.wait_ge(sem, value)


class Projection:

    def __init__(self, nc, k, g, hi_count, s):
        self.nc, self.k, self.g, self.hi_count, self.s = nc, k, g, hi_count, s

    def pe_x(self, pe, i, n, loaded):
        slot, value = self.g.at(i, "xT", n)
        pe.wait_ge(self.s["x_in"], loaded)
        positive(pe, self.g.empty[slot], value)
        c = n % 2
        for t in range(NQ):
            last = self.nc.tensor.transpose(self.g.banks[slot][:, t * 128:t * 128 + 128],
                                            self.k["x_tok"][:, t, c * 128:c * 128 + 128], self.k["ident"][:, :])
        last.then_inc(self.g.full[slot], 1)

    def pe_q(self, pe, i, n):
        if n % 4 == 0:
            for c in range(2):
                slot, value = self.g.at(i, "xT", n // 4 * 2 + c)
                pe.wait_ge(self.g.empty[slot], value + 1)
        slot, value = self.g.at(i, "q", n)
        pe.wait_ge(self.g.empty[slot], value)
        w, m, w_hl, xT = n % 4 // 2, n % 2, self.k["w_hl"], self.k["xT"]
        three(self.nc, self.g.banks[slot][:, :], lambda hl, c: w_hl[:, hl, w, c, m * 128:m * 128 + 128],
              lambda hl, c: xT[:, hl, c, :], DC).then_inc(self.g.full[slot], 1)

    def pe_v(self, pe, i, n):
        slot, value = self.g.at(i, "v", n)
        pe.wait_ge(self.g.empty[slot], value)
        w_hl, xT = self.k["w_hl"], self.k["xT"]
        for t in range(2):
            at = (2 * (n % 2) + t) * 128
            last = three(self.nc, self.g.banks[slot][:, t * D:t * D + D], lambda hl, c: xT[:, hl, c, at:at + 128],
                         lambda hl, c: w_hl[:, hl, 2, c, :], DC)
        last.then_inc(self.g.full[slot], 1)

    def act_x(self, act, i, n):
        slot, value = self.g.at(i, "xT", n)
        act.wait_ge(self.g.full[slot], value + 1)
        self.nc.scalar.activation(self.k["xT"][:, 0, n % 2, :], self.g.banks[slot][:, :], ACT.Copy,
                                  scale=XS).then_inc(self.s["hi_done"], 1)

    def act_q(self, act, i, n, before, stored):
        A, qf, qk = self.nc.scalar, self.k["qf"], self.k["qk"]
        slot, value = self.g.at(i, "q", n)
        act.wait_ge(self.g.full[slot], value + 1)
        positive(act, self.s["qlo_done"], before + max(n - 1, 0))
        A.activation(qf[:, n % 2, :], self.g.banks[slot][:, :], ACT.Identity,
                     bias=self.k["qk_bias"][:, n % 4 // 2, n % 2:n % 2 + 1],
                     scale=QS / (WS * XS) * (HD ** -0.5 if n % 4 < 2 else 1.0)).then_inc(self.g.empty[slot], 1)
        if n % 4 == 0:
            positive(act, self.s["qk_stored"], stored)
        act.wait_ge(self.g.empty[slot], value + 1)
        A.activation(qk[:, 0, n % 4, :], qf[:, n % 2, :], ACT.Copy).then_inc(self.s["qhi_done"], 1)

    def dve_x(self, dve, i, n):
        slot, _ = self.g.at(i, "xT", n)
        xT = self.k["xT"]
        dve.wait_ge(self.s["hi_done"], self.hi_count(i, "xT", n))
        self.nc.vector.scalar_tensor_tensor(xT[:, 1, n % 2, :], self.g.banks[slot][:, :], XS, xT[:, 0, n % 2, :],
                                            ALU.mult, ALU.subtract).then_inc(self.g.empty[slot], 1)

    def dve_v(self, dve, i, n, copied):
        slot, value = self.g.at(i, "v", n)
        dve.wait_ge(self.g.full[slot], value + 1)
        positive(dve, self.s["v_copied"], copied)
        self.nc.vector.scalar_tensor_tensor(
            self.k["v_next"][:, 2 * (n % 2):2 * (n % 2) + 2, :], self.g.banks[slot][:, :]
            .rearrange("p (t d) -> p t d", t=2), 1.0 / (WS * XS),
            self.k["b_rows"][:, 1:2, :].to_broadcast([128, 2, D]), ALU.mult, ALU.add).then_inc(self.g.empty[slot], 1)

    def pool_q(self, pool, n, before):
        qf, qk = self.k["qf"], self.k["qk"]
        pool.wait_ge(self.s["qhi_done"], before + n + 1)
        self.nc.gpsimd.tensor_tensor(qk[:, 1, n % 4, :], qf[:, n % 2, :], qk[:, 0, n % 4, :],
                                     ALU.subtract).then_inc(self.s["qlo_done"], 1)

    def pool_v(self):
        self.nc.gpsimd.tensor_copy(self.k["v_aug"][:, :, :, 0:HD], self.k["v_next"][:, :, :]
                                   .rearrange("p t (h d) -> p t h d", h=H)).then_inc(self.s["v_copied"], 1)

    def sp_store(self, sp, b):
        for hl in range(2):
            sp.dma_start(self.k["dram"]["qk"][bass.ds(b * 4 * D + hl * 2 * D, 2 * D), :]
                         .rearrange("(m p) s -> p m s", p=128), self.k["qk"][:, hl, :, :]
                         ).then_inc(self.s["qk_stored"], 16)

    def sp_stack(self, sp, b, qs, ks, done):
        rows = self.k["dram"]["qk"][bass.ds(b * 4 * D, 4 * D), :].rearrange(
            "(l t p r d) s -> l t r d p s", l=2, t=2, r=2, d=HD)
        for t, (dst, parts) in enumerate(((qs, (0, 0, 1)), (ks, (0, 1, 0)))):
            for par in range(2):
                for n, hl in enumerate(parts):
                    row = 64 * par + n * HD
                    sp.dma_start(dst[row:row + HD, :, :], rows[hl, t, par, :, :, :]).then_inc(done, 16)


def three(nc, out, left, right, n):
    for k in range(n):
        for m, (a, b) in enumerate(((0, 0), (0, 1), (1, 0))):
            last = nc.tensor.matmul(out, left(a, k), right(b, k), start=(k == 0 and m == 0),
                                    stop=(k == n - 1 and m == 2))
    return last


def score_maxima(nc, k, bank, item, qs, ks):
    t, par, p0, pairs = item
    rows, wide = slice(64 * par, 64 * par + STACK), 128 * (t + 1)
    for n in range(pairs):
        nc.tensor.matmul(bank[:, n * wide:n * wide + wide], qs[rows, p0 + n, t * 128:t * 128 + 128],
                         ks[rows, p0 + n, 0:wide], start=True, stop=False)
        last = nc.tensor.matmul(bank[:, (n + 1) * wide - 128:(n + 1) * wide], k["ident16"][:, :], k["causal"][:, :],
                                start=False, stop=True)
    return last


def reduce_maxima(nc, k, bank, item):
    t, par, p0, pairs = item
    wide = 128 * (t + 1)
    return nc.vector.tensor_reduce(k["rowmax"][:, t, par * PAIRS + p0:par * PAIRS + p0 + pairs],
                                   bank[:, 0:pairs * wide].rearrange("p (n w) -> p n w", n=pairs), AX.X, ALU.max)


def prepare_block(nc, ctx, dram, keep):
    def sb(name, shape, dt=F32):
        return ctx.enter_context(nc.sbuf_tensor(name, shape, dt))

    def sem(name):
        return ctx.enter_context(nc.semaphore(name))

    ident, ident16, causal = keep["ident"], keep["ident16"], keep["causal"]
    w_hl, qk_bias, b_rows, power = keep["w_hl"], keep["qk_bias"], keep["b_rows"], keep["power"]
    w_f = sb("w_f", [128, 4, DC, D])
    wq_f = sb("wq_f", [128, DC, XA])
    wqT = sb("wqT", [128, 2, PAIRS, D], F16)
    wkv = sb("wkv", [128, 2, XA])
    wkv2 = sb("wkv2", [DCOND - 128, 2, XA])
    wout_f = sb("wout_f", [128, PAIRS, D])
    wout = sb("wout", [128, 2, PAIRS, D], F16)
    KT = NB * KV // 128
    cond = sb("cond", [128, KT, DCOND])
    cT = sb("cT", [128, 2, NB * KV])
    kvT = sb("kvT", [128, 2, 2, PAIRS, NB * KV], F16)
    stage = sb("stage", [128, 4, 2, 1024], F16)

    R = [ctx.enter_context(nc.psum_tensor(f"prR{i}", [128, 2, 512], F32)) for i in range(2)]
    G = [ctx.enter_context(nc.psum_tensor(f"prG{i}", [128, 512], F32)) for i in range(4)]
    r = Slots(PREPARE, R_KINDS, R, [sem(f"pr_full{i}") for i in range(2)], [sem(f"pr_empty{i}") for i in range(2)], 0)
    g = Slots(PREPARE, G_KINDS, G, [sem(f"pg_full{i}") for i in range(4)], [sem(f"pg_empty{i}") for i in range(4)], 0)
    HIS = [step for step in PREPARE if step[0] in ("xT", "W", "kv", "A", "VW")]

    def hi_count(i, kind, n):
        return HIS.index((kind, n)) + 1

    s = {name: sem("p_" + name) for name in ("x_in", "hi_done", "qlo_done", "qhi_done", "qk_stored", "v_copied")}
    hi_done = s["hi_done"]
    w_in, b_in, c_in, wkv_in, wq_in, wo_in = (sem("w_in"), sem("b_in"), sem("c_in"), sem("wkv_in"), sem("wq_in"),
                                              sem("wo_in"))
    const_step, consts = sem("const_step"), sem("consts")
    w_hi, w_lo, wout_hi, wout_lo = sem("w_hi"), sem("w_lo"), sem("wout_hi"), sem("wout_lo")
    bias_done, stack_in, next_in = sem("bias_done"), sem("stack_in"), sem("next_in")
    m_stored, m_in, xr_in = sem("pm_stored"), sem("pm_in"), sem("pxr_in")
    staged = [sem(f"staged{i}") for i in range(4)]
    project = Projection(nc, keep, g, hi_count, s)
    PIECES = [step for step in PREPARE if step[0] in ("A", "VW")]

    def piece(use, hl, par):
        return stage[:, use % 4, hl, :].rearrange("p (b r x k) -> p r x b k", b=NB, r=2, x=2)[:, par, :, :, :]

    block = ctx.enter_context(nc.Block())

    @block.sync
    def _(sp):
        def tokens(b, dst, done):
            sp.dma_start(dst[:, :, :], dram["x"][b * S:b * S + S, :]
                         .rearrange("(t p) d -> p t d", p=128)).then_inc(done, 16)

        tokens(0, keep["x_tok"], s["x_in"])
        for n, w in enumerate(("Wq", "Wk", "Wv", "Wo")):
            sp.dma_start(w_f[:, n, :, :], dram[w].rearrange("(c p) n -> p c n", p=128)).then_inc(w_in, 16)
        sp.dma_start(qk_bias[:, 0, :], dram["bq"]).then_inc(b_in, 16)
        sp.dma_start(qk_bias[:, 1, :], dram["bk"]).then_inc(b_in, 16)
        for n, b in enumerate(("bo", "bv", "b_out")):
            sp.dma_start(b_rows[:, n, :], dram[b].partition_broadcast(128)).then_inc(b_in, 16)
        sp.dma_start(cond[:, :, :], dram["cond"].rearrange("(t p) d -> p t d", p=128)).then_inc(c_in, 16)
        for n, w in enumerate(("w_k", "w_v")):
            sp.dma_start(wkv[:, n, :], dram[w][0:128, :]).then_inc(wkv_in, 16)
            sp.dma_start(wkv2[:, n, :], dram[w][128:DCOND, :]).then_inc(wkv_in, 16)
        tokens(0, keep["x_res"], xr_in)
        slot, value = g.at(0, "xT", 1)
        sp.wait_ge(g.full[slot], value + 1)
        tokens(1, keep["x_tok"], s["x_in"])
        sp.wait_ge(s["qlo_done"], 4)
        project.sp_store(sp, 0)
        sp.wait_ge(s["qk_stored"], 32)
        sp.wait_ge(consts, 1)
        project.sp_stack(sp, 0, keep["qs_e"], keep["ks_e"], stack_in)
        slot, value = g.at(0, "xT", 3)
        sp.wait_ge(g.full[slot], value + 1)
        tokens(2, keep["x_tok"], s["x_in"])
        sp.wait_ge(s["qlo_done"], 8)
        project.sp_store(sp, 1)
        sp.wait_ge(s["qk_stored"], 64)
        project.sp_stack(sp, 1, keep["qs_m"], keep["ks_m"], next_in)
        for n in range(2):
            slot, value = g.at(0, "mT", n)
            sp.wait_ge(g.empty[slot], value + 1)
        sp.dma_start(dram["m"], keep["neg_maxT"][:, :]).then_inc(m_stored, 16)
        sp.wait_ge(m_stored, 16)
        for par in range(2):
            row = 64 * par + STACK
            sp.dma_start(keep["qs_e"][row:row + 1, :, :], dram["m"][par * PAIRS:(par + 1) * PAIRS, :]
                         .unsqueeze(0)).then_inc(m_in, 16)
        sp.wait_ge(next_in, 12 * 16)
        sp.wait_ge(m_in, 32)
        sp.wait_ge(s["x_in"], 48)
        sp.wait_ge(xr_in, 16)

    @block.gpsimd
    def _(pool):
        P = nc.gpsimd
        P.memset(ident[:, :], 0.0).then_inc(const_step, 1)
        P.memset(causal[:, :], 0.0).then_inc(const_step, 1)
        pool.wait_ge(const_step, 2)
        P.affine_select(out=ident[:, :], in_=ident[:, :], compare_op=ALU.not_equal, fill=1.0, base=0,
                        pattern=[[-1, 128]], channel_multiplier=1).then_inc(const_step, 1)
        P.affine_select(out=causal[:, :], in_=causal[:, :], compare_op=ALU.is_ge, fill=NEG, base=0,
                        pattern=[[-1, 128]], channel_multiplier=1).then_inc(const_step, 1)
        P.memset(keep["ks_e"][:, :, :], 1.0).then_inc(const_step, 1)
        P.memset(keep["v_aug"][:, :, :, :], 1.0).then_inc(const_step, 1)
        P.memset(power[:, 0:NQ], EPS).then_inc(const_step, 1)
        P.memset(power[:, NQ:], -0.5).then_inc(const_step, 1)
        P.memset(keep["zeros"][:, :], 0.0).then_inc(const_step, 1)
        pool.wait_ge(const_step, 9)
        P.tensor_copy(ident16[:, :], ident[:, :]).then_inc(consts, 1)
        for n in range(4):
            project.pool_q(pool, n, 0)
        for n in range(2):
            slot, value = g.at(0, "v", n)
            pool.wait_ge(g.empty[slot], value + 1)
        project.pool_v()
        for n in range(4, 8):
            project.pool_q(pool, n, 0)
        for n, (kind, m) in enumerate(PIECES):
            slot, value = r.at(0, kind, m)
            pool.wait_ge(r.empty[slot], value + 1)
            if kind == "A":
                c, q = m // 4, m % 4
                dst = dram["ax"].rearrange("(b p) (l c n) -> p l b c n", p=128, l=2, c=DC)[:, :, :, c, q * 256:q * 256 + 256]
                src = stage[:, n % 4, :, :].rearrange("p l (b n) -> p l b n", b=NB)
            else:
                b, par = m // 2, m % 2
                dst = dram["vw"][b * 128:b * 128 + 128, :].rearrange("p (l q r n) -> p l q r n", l=2, q=4, r=2)[:, :, :, par, :]
                src = stage[:, n % 4, :, :].rearrange("p l (q n) -> p l q n", q=4)
            for hl in range(2):
                pool.dma_start(dst[:, hl, :, :], src[:, hl, :, :]).then_inc(staged[n % 4], 16)
        for n in range(4):
            pool.wait_ge(staged[n], len(PIECES) // 4 * 32)

    @block.scalar
    def _(act):
        A = nc.scalar
        act.dma_start(wq_f[:, :, :], dram["w_q"].rearrange("(c p) n -> p c n", p=128)).then_inc(wq_in, 16)
        act.dma_start(wout_f[:, :, :], dram["w_out"].rearrange("(k p) n -> p k n", p=128)).then_inc(wo_in, 16)

        def hi(out, bank, kind, n, scale):
            slot, value = r.at(0, kind, n)
            act.wait_ge(r.full[slot], value + 1)
            A.activation(out, bank(R[slot]), ACT.Copy, scale=scale).then_inc(hi_done, 1)

        for kind, n in PREPARE:
            if kind == "xT":
                project.act_x(act, 0, n)
                if n == 1:
                    act.wait_ge(w_in, 4 * 16)
                    A.activation(w_hl[:, 0, :, :, :].rearrange("p w c n -> p (w c n)"),
                                 w_f[:, :, :, :].rearrange("p w c n -> p (w c n)"), ACT.Copy, scale=WS
                                 ).then_inc(w_hi, 1)
                    act.wait_ge(bias_done, 2)
            elif kind == "q":
                project.act_q(act, 0, n, 0, n // 4 * 32)
            elif kind == "cT":
                slot, value = g.at(0, kind, n)
                act.wait_ge(g.full[slot], value + 1)
                rows = 128 if n == 0 else DCOND - 128
                A.activation(cT[0:rows, n, :], G[slot][0:rows, 0:NB * KV], ACT.Copy).then_inc(g.empty[slot], 1)
            elif kind == "W":
                hi(wqT[:, 0, n * 4:n * 4 + 4, :].rearrange("p k n -> p (k n)"), lambda b: flat(b[:, :, :]), kind, n, WS)
            elif kind == "kv":
                hi(kvT[:, 0, n // 2, n % 2 * 4:n % 2 * 4 + 4, :].rearrange("p k n -> p (k n)"),
                   lambda b: flat(b[:, :, :]), kind, n, XS)
                if n == 3:
                    act.wait_ge(wo_in, 16)
                    A.activation(wout[:, 0, :, :].rearrange("p k n -> p (k n)"), flat(wout_f[:, :, :]), ACT.Copy,
                                 scale=WS).then_inc(wout_hi, 1)
            elif kind in ("A", "VW"):
                use = PIECES.index((kind, n))
                if use >= 4:
                    act.wait_ge(staged[use % 4], use // 4 * 32)
                slot, value = r.at(0, kind, n)
                act.wait_ge(r.full[slot], value + 1)
                if kind == "A":
                    for par in range(2):
                        last = A.activation(piece(use, 0, par), R[slot][:, par, :]
                                            .rearrange("p (x b k) -> p x b k", x=2, b=NB), ACT.Copy, scale=1.0 / XS)
                else:
                    last = A.activation(stage[:, use % 4, 0, :], flat(R[slot][:, :, :]), ACT.Copy, scale=1.0 / XS)
                last.then_inc(hi_done, 1)
            elif kind == "mT":
                slot, value = g.at(0, kind, n)
                act.wait_ge(g.full[slot], value + 1)
                A.activation(keep["neg_maxT"][:, n * 256:n * 256 + 256], G[slot][0:H, 0:256], ACT.Copy, scale=-1.0
                             ).then_inc(g.empty[slot], 1)

    @block.vector
    def _(dve):
        V = nc.vector
        dve.wait_ge(b_in, 5 * 16)
        V.tensor_scalar(qk_bias[:, 0, :], qk_bias[:, 0, :], QS * HD ** -0.5, None, ALU.mult).then_inc(bias_done, 1)
        V.tensor_scalar(qk_bias[:, 1, :], qk_bias[:, 1, :], QS, None, ALU.mult).then_inc(bias_done, 1)

        def lo(out, bank, high, kind, n, scale):
            slot, _ = r.at(0, kind, n)
            dve.wait_ge(hi_done, hi_count(0, kind, n))
            V.scalar_tensor_tensor(out, bank(R[slot]), scale, high, ALU.mult, ALU.subtract).then_inc(r.empty[slot], 1)

        for kind, n in PREPARE:
            if kind == "xT":
                project.dve_x(dve, 0, n)
                if n == 1:
                    dve.wait_ge(w_hi, 1)
                    V.scalar_tensor_tensor(w_hl[:, 1, :, :, :].rearrange("p w c n -> p (w c n)"),
                                           w_f[:, :, :, :].rearrange("p w c n -> p (w c n)"), WS,
                                           w_hl[:, 0, :, :, :].rearrange("p w c n -> p (w c n)"),
                                           ALU.mult, ALU.subtract).then_inc(w_lo, 1)
            elif kind == "v":
                project.dve_v(dve, 0, n, n // 2)
            elif kind == "W":
                lo(wqT[:, 1, n * 4:n * 4 + 4, :].rearrange("p k n -> p (k n)"), lambda b: flat(b[:, :, :]),
                   wqT[:, 0, n * 4:n * 4 + 4, :].rearrange("p k n -> p (k n)"), kind, n, WS)
            elif kind == "kv":
                part = kvT[:, :, n // 2, n % 2 * 4:n % 2 * 4 + 4, :].rearrange("p l k n -> p l (k n)")
                lo(part[:, 1, :], lambda b: flat(b[:, :, :]), part[:, 0, :], kind, n, XS)
                if n == 3:
                    dve.wait_ge(wout_hi, 1)
                    V.scalar_tensor_tensor(wout[:, 1, :, :].rearrange("p k n -> p (k n)"), flat(wout_f[:, :, :]), WS,
                                           wout[:, 0, :, :].rearrange("p k n -> p (k n)"),
                                           ALU.mult, ALU.subtract).then_inc(wout_lo, 1)
            elif kind == "A":
                use = PIECES.index((kind, n))
                slot, _ = r.at(0, kind, n)
                dve.wait_ge(hi_done, hi_count(0, kind, n))
                for par in range(2):
                    for x in range(2):
                        last = V.scalar_tensor_tensor(piece(use, 1, par)[:, x, :, :],
                                                      R[slot][:, par, x * NB * KV:(x + 1) * NB * KV]
                                                      .rearrange("p (b k) -> p b k", b=NB), 1.0 / XS,
                                                      piece(use, 0, par)[:, x, :, :], ALU.mult, ALU.subtract)
                last.then_inc(r.empty[slot], 1)
            elif kind == "VW":
                use = PIECES.index((kind, n))
                lo(stage[:, use % 4, 1, :], lambda b: flat(b[:, :, :]), stage[:, use % 4, 0, :], kind, n, 1.0 / XS)
            elif kind == "m":
                slot, value = g.at(0, kind, n)
                dve.wait_ge(g.full[slot], value + 1)
                reduce_maxima(nc, keep, G[slot], MAXES[n]).then_inc(g.empty[slot], 1)

    @block.tensor
    def _(pe):
        M = nc.tensor

        def opened(slots, kind, n):
            slot, value = slots.at(0, kind, n)
            positive(pe, slots.empty[slot], value)
            return slots.banks[slot], slots.full[slot]

        def read(slots, kind, n):
            slot, value = slots.at(0, kind, n)
            pe.wait_ge(slots.empty[slot], value + 1)

        pe.wait_ge(consts, 1)
        for kind, n in PREPARE:
            if kind == "xT":
                project.pe_x(pe, 0, n, n // 2 * 16 + 16)
            elif kind == "q":
                if n == 0:
                    pe.wait_ge(w_lo, 1)
                project.pe_q(pe, 0, n)
            elif kind == "v":
                project.pe_v(pe, 0, n)
            elif kind == "cT":
                pe.wait_ge(c_in, 16)
                bank, full = opened(g, kind, n)
                rows = 128 if n == 0 else DCOND - 128
                for t in range(KT):
                    last = M.transpose(bank[0:rows, t * 128:t * 128 + 128], cond[:, t, n * 128:n * 128 + rows],
                                       ident[:, :])
                last.then_inc(full, 1)
            elif kind == "W":
                pe.wait_ge(wq_in, 16)
                bank, full = opened(r, kind, n)
                for k in range(4):
                    for c in range(DC):
                        at = k * D + c * 128
                        last = M.transpose(flat(bank[:, :, :])[:, at:at + 128],
                                           wq_f[:, c, (4 * n + k) * 128:(4 * n + k) * 128 + 128], ident[:, :])
                last.then_inc(full, 1)
            elif kind == "kv":
                pe.wait_ge(wkv_in, 4 * 16)
                if n == 0:
                    read(g, "cT", 0)
                    read(g, "cT", 1)
                bank, full = opened(r, kind, n)
                for k in range(4):
                    p = n % 2 * 4 + k
                    out = flat(bank[:, :, :])[:, k * NB * KV:(k + 1) * NB * KV]
                    M.matmul(out, wkv[:, n // 2, p * 128:p * 128 + 128], cT[:, 0, :], start=True, stop=False)
                    last = M.matmul(out, wkv2[:, n // 2, p * 128:p * 128 + 128], cT[0:DCOND - 128, 1, :],
                                    start=False, stop=True)
                last.then_inc(full, 1)
            elif kind == "A":
                if n == 0:
                    for m in range(2):
                        read(r, "W", m)
                        read(r, "kv", m)
                c, q = n // 4, n % 4
                bank, full = opened(r, kind, n)
                for x in range(2):
                    for par in range(2):
                        half, p = slice(64 * par, 64 * par + 64), 2 * q + x
                        last = three(nc, bank[:, par, x * NB * KV:(x + 1) * NB * KV],
                                     lambda hl, _: wqT[half, hl, p, c * 128:c * 128 + 128],
                                     lambda hl, _: kvT[half, hl, 0, p, :], 1)
                last.then_inc(full, 1)
            elif kind == "VW":
                if n == 0:
                    for m in range(2, 4):
                        read(r, "kv", m)
                    pe.wait_ge(wout_lo, 1)
                b, par = n // 2, n % 2
                rows = slice(64 * par, 64 * par + 64)
                bank, full = opened(r, kind, n)
                for p in range(PAIRS):
                    at = 64 * (p % 2)
                    last = three(nc, flat(bank[:, :, :])[at:at + 64, p // 2 * D:p // 2 * D + D],
                                 lambda hl, _: kvT[rows, hl, 1, p, b * KV:b * KV + KV],
                                 lambda hl, _: wout[rows, hl, p, :], 1)
                last.then_inc(full, 1)
            elif kind == "m":
                if n == 0:
                    pe.wait_ge(stack_in, 12 * 16)
                bank, full = opened(g, kind, n)
                score_maxima(nc, keep, bank, MAXES[n], keep["qs_e"], keep["ks_e"]).then_inc(full, 1)
            elif kind == "mT":
                if n == 0:
                    for m in range(len(MAXES) - 4, len(MAXES)):
                        read(g, "m", m)
                bank, full = opened(g, kind, n)
                for t in range(2):
                    last = M.transpose(bank[0:H, t * 128:t * 128 + 128], keep["rowmax"][:, 2 * n + t, :], ident[:, :])
                last.then_inc(full, 1)


def attention_block(nc, ctx, dram, keep):
    START = 1

    def sb(name, shape, dt=F32):
        return ctx.enter_context(nc.sbuf_tensor(name, shape, dt))

    def sem(name):
        return ctx.enter_context(nc.semaphore(name))

    ident, w_hl, b_rows, power = keep["ident"], keep["w_hl"], keep["b_rows"], keep["power"]
    xhl, x_res, v_aug = keep["xhl"], keep["x_res"], keep["v_aug"]
    qs_e, ks_e, qs_m, ks_m = keep["qs_e"], keep["ks_e"], keep["qs_m"], keep["ks_m"]
    probs = sb("probs", [128, 4, 2, S])
    cu = sb("cu", [128, 2, S])
    inv = sb("inv", [128, GROUPS, NQ, 4])
    ctx_tok = sb("ctx_tok", [128, NQ, D])
    ctxT = sb("ctxT", [128, 2, DC, S], F16)
    x1 = sb("x1", [128, NQ, D])
    x1_b = sb("x1_b", [128, NQ, D])
    x1T = sb("x1T", [128, 2, DC, S], F16)
    x2 = sb("x2", [128, NQ, D])
    stats = sb("stats", [128, 2 * NQ, 6])
    meanvar = sb("meanvar", [128, 2 * NQ, 2])
    rstd = sb("rstd", [128, 2 * NQ])
    e_x = sb("e_x", [128, NQ, XA])
    xmax = sb("xmax", [128, NQ, XH])
    xsum = sb("xsum", [128, NQ, XH])
    xinv = sb("xinv", [128, NQ, XH])
    pT = sb("pT", [128, 2, 2, PAIRS, 128], F16)
    a_x = sb("a_x", [128, 2, DC, XA], F16)
    vw = sb("vw", [128, 2, PAIRS, D], F16)

    R = [ctx.enter_context(nc.psum_tensor(f"R{i}", [128, 2, 512], F32)) for i in range(2)]
    PV = [ctx.enter_context(nc.psum_tensor(f"PV{i}", [128, 512], F32)) for i in range(2)]
    G = [ctx.enter_context(nc.psum_tensor(f"G{i}", [128, 512], F32)) for i in range(2)]
    r = Slots(ALPHA + BETA, R_KINDS, R, [sem(f"r_full{i}") for i in range(2)], [sem(f"r_empty{i}") for i in range(2)],
              START)
    g = Slots(ALPHA + BETA, G_KINDS, G, [sem(f"g_full{i}") for i in range(2)], [sem(f"g_empty{i}") for i in range(2)],
              START)
    pv_empty = [sem(f"pv_empty{i}") for i in range(2)]
    HIS = [("cx", 0), ("xT", 0), ("cx", 1), ("xT", 1), ("xa", 0), ("xa", 1), ("T", 0), ("T", 1), ("T", 2), ("T", 3)]

    def hi_count(i, kind, n):
        return i * len(HIS) + HIS.index((kind, n)) + 1

    s = {name: sem(name) for name in ("x_in", "hi_done", "qlo_done", "qhi_done", "qk_stored", "v_copied")}
    hi_done, x_in, v_copied, qk_stored, qlo_done = (s["hi_done"], s["x_in"], s["v_copied"], s["qk_stored"],
                                                    s["qlo_done"])
    z_out, ax_in, vw_in, xr_in = sem("z_out"), sem("ax_in"), sem("vw_in"), sem("xr_in")
    stack_e, stack_m, m_stored = sem("stack_e"), sem("stack_m"), sem("m_stored")
    probs_ready, probs_used, exp_seen = sem("probs_ready"), sem("probs_used"), sem("exp_seen")
    stats_seen = sem("stats_seen")
    xb_done, x1b_done, x1_ready, x2_ready = sem("xb_done"), sem("x1b_done"), sem("x1_ready"), sem("x2_ready")
    var_done, rstd_done, pool_step, dve_step = sem("var_done"), sem("rstd_done"), sem("pool_step"), sem("dve_step")
    e_exp, e_inv, e_prob, x2_stored = sem("e_exp"), sem("e_inv"), sem("e_prob"), sem("x2_stored")
    project = Projection(nc, keep, g, hi_count, s)
    SCORES = 2 * UNITS

    block = ctx.enter_context(nc.Block())

    @block.sync
    def _(sp):
        for free in (g.full[0], g.full[1], g.empty[0], g.empty[1], r.full[0], r.full[1], r.empty[0], r.empty[1],
                     pv_empty[0], pv_empty[1], probs_used, stack_e, stack_m, qk_stored, qlo_done, m_stored, x2_stored,
                     x_in, xr_in, v_copied):
            sp.sem_inc(free, START)

        def load_ax(b):
            sp.dma_start(a_x[:, :, :, :].rearrange("p l c n -> p (l c n)"),
                         dram["ax"][bass.ds(b * 128, 128), :]).then_inc(ax_in, 16)

        def load_vw(b):
            sp.dma_start(vw[:, :, :, :].rearrange("p l k n -> p (l k n)"),
                         dram["vw"][bass.ds(b * 128, 128), :]).then_inc(vw_in, 16)

        load_ax(0)
        load_vw(0)
        with nc.sync.Fori(0, NB) as i:
            slot, value = g.at(i, "mT", 1)
            sp.wait_ge(g.empty[slot], value + 1)
            sp.dma_start(dram["m"], keep["neg_maxT"][:, :]).then_inc(m_stored, 16)
            sp.wait_ge(probs_used, i * UNITS + UNITS + START)
            project.sp_stack(sp, (i + 1) % NB, qs_e, ks_e, stack_e)
            sp.wait_ge(m_stored, i * 16 + 16 + START)
            for par in range(2):
                row = 64 * par + STACK
                sp.dma_start(qs_e[row:row + 1, :, :], dram["m"][par * PAIRS:(par + 1) * PAIRS, :]
                             .unsqueeze(0)).then_inc(stack_e, 16)
            slot, value = g.at(i, "xT", 1)
            sp.wait_ge(g.full[slot], value + 1)
            sp.dma_start(keep["x_tok"][:, :, :], dram["x"][bass.ds((i + 3) % NB * S, S), :]
                         .rearrange("(t p) d -> p t d", p=128)).then_inc(x_in, 16)
            slot, value = g.at(i, "o", 1)
            sp.wait_ge(g.empty[slot], value + 1)
            sp.dma_start(x_res[:, :, :], dram["x"][bass.ds((i + 1) % NB * S, S), :]
                         .rearrange("(t p) d -> p t d", p=128)).then_inc(xr_in, 16)
            sp.wait_ge(qlo_done, i * 4 + 4 + START)
            project.sp_store(sp, (i + 2) % NB)
            sp.wait_ge(qk_stored, i * 32 + 32 + START)
            project.sp_stack(sp, (i + 2) % NB, qs_m, ks_m, stack_m)
            slot, value = r.at(i, "S", 3)
            sp.wait_ge(r.full[slot], value + 1)
            load_ax((i + 1) % NB)
            slot, value = g.at(i, "O", 3)
            sp.wait_ge(g.full[slot], value + 1)
            load_vw((i + 1) % NB)
            sp.wait_ge(x2_ready, i * 2 + 2)
            sp.dma_start(dram["x2"][bass.ds(i * S, S), :].rearrange("(t p) d -> p t d", p=128),
                         x2[:, :, :]).then_inc(x2_stored, 16)
        for done, count in ((x2_stored, NB * 16 + START), (x_in, NB * 16 + START), (xr_in, NB * 16 + START),
                            (stack_m, NB * 12 * 16 + START), (stack_e, NB * 14 * 16 + START),
                            (ax_in, NB * 16 + 16), (vw_in, NB * 16 + 16), (z_out, 16)):
            sp.wait_ge(done, count)

    @block.gpsimd
    def _(pool):
        P = nc.gpsimd
        pool.dma_start(dram["xs"].rearrange("(n p) d -> p n d", p=128),
                       keep["zeros"][:, :].unsqueeze(1).to_broadcast([128, TILES * SLOTS // 128, 2 * D])
                       ).then_inc(z_out, 16)

        def root(i, n):
            pool.wait_ge(var_done, i * 4 + n + 1)
            P.tensor_tensor(rstd[:, 2 * n:2 * n + 2], meanvar[:, 2 * n:2 * n + 2, 1], power[:, 0:2],
                            ALU.add).then_inc(pool_step, 1)
            pool.wait_ge(pool_step, i * 4 + n + 1)
            P.tensor_tensor(rstd[:, 2 * n:2 * n + 2], rstd[:, 2 * n:2 * n + 2], power[:, NQ:NQ + 2],
                            ALU.pow).then_inc(rstd_done, 1)

        with nc.gpsimd.Fori(0, NB) as i:
            for n in range(SCORES):
                slot, value = r.at(i, "s", n)
                pool.wait_ge(r.empty[slot], value + 1)
                pool.sem_inc(exp_seen, 1)
                diag = probs[:, n % 4, :, 0:128]
                P.affine_select(out=diag, in_=diag, compare_op=ALU.is_ge, fill=0.0, base=0,
                                pattern=[[0, 2], [1, 128]], channel_multiplier=-1).then_inc(probs_ready, 1)
                if n == SCORES // 2:
                    pool.wait_ge(xr_in, i * 16 + START)
                    P.tensor_tensor(x_res[:, :, :], x_res[:, :, :],
                                    b_rows[:, 0:1, :].to_broadcast([128, NQ, D]), ALU.add).then_inc(xb_done, 1)
            pool.wait_ge(probs_used, i * UNITS + UNITS + START)
            pool.sem_inc(exp_seen, 1)
            project.pool_v()
            root(i, 0)
            root(i, 1)
            for n in range(4):
                project.pool_q(pool, n, i * 4)
            pool.wait_ge(x1_ready, i * 2 + 2)
            P.tensor_tensor(x1_b[:, :, :], x1[:, :, :],
                            b_rows[:, 2:3, :].to_broadcast([128, NQ, D]), ALU.add).then_inc(x1b_done, 1)
            for t in range(NQ):
                pool.wait_ge(e_inv, i * NQ + t + 1)
                e3 = e_x[:, t, :].rearrange("p (h k) -> p h k", h=XH)
                P.tensor_tensor(e3, e3, xinv[:, t, :].unsqueeze(2).to_broadcast([128, XH, KV]),
                                ALU.mult).then_inc(e_prob, 1)
            root(i, 2)
            root(i, 3)

    @block.scalar
    def _(act):
        A = nc.scalar

        def hi(i, kind, n, out, slots, bank, scale):
            slot, value = slots.at(i, kind, n)
            act.wait_ge(slots.full[slot], value + 1)
            A.activation(out, bank(slots.banks[slot]), ACT.Copy, scale=scale).then_inc(hi_done, 1)

        with nc.scalar.Fori(0, NB) as i:
            def pv_out(gr):
                act.wait_ge(probs_used, i * UNITS + NQ * (gr + 1) + START)
                A.activation(cu[:, gr % 2, :], PV[gr % 2][:, :], ACT.Copy).then_inc(pv_empty[gr % 2], 1)

            for n in range(SCORES):
                u = n // 2
                gr, j = u // NQ, u % NQ
                slot, value = r.at(i, "s", n)
                act.wait_ge(r.full[slot], value + 1)
                act.wait_ge(probs_used, i * UNITS + max(u - 1, 0) + START)
                A.activation(probs[:, n % 4, :, 0:S - 128 * j], R[slot][:, :, 0:S - 128 * j], ACT.Exp,
                             scale=1.0 / (QS * QS)).then_inc(r.empty[slot], 1)
                if j == 0 and n % 2 == 1 and gr > 0:
                    pv_out(gr - 1)
            pv_out(GROUPS - 1)
            act.wait_ge(m_stored, i * 16 + START)
            for n in range(2):
                slot, value = g.at(i, "mT", n)
                act.wait_ge(g.full[slot], value + 1)
                A.activation(keep["neg_maxT"][:, n * 256:n * 256 + 256], G[slot][0:H, 0:256], ACT.Copy, scale=-1.0
                             ).then_inc(g.empty[slot], 1)
            for c in range(DC):
                hi(i, "cx", c, ctxT[:, 0, c, :], g, lambda b: b[:, :], XS)
                project.act_x(act, i, c)
            for n in range(4):
                project.act_q(act, i, n, i * 4 + START, i * 32 + START)
            for c in range(DC):
                hi(i, "xa", c, x1T[:, 0, c, :], g, lambda b: b[:, :], XS)

            def x_exp(t):
                slot, value = r.at(i, "S", t)
                act.wait_ge(r.empty[slot], value + 1)
                A.activation(e_x[:, t, :], e_x[:, t, :], ACT.Exp,
                             scale=XD ** -0.5 / (WS * XS)).then_inc(e_exp, 1)

            def p_hi(t):
                hi(i, "T", t, pT[:, t % 2, 0, :, :].rearrange("p k q -> p (k q)"), r, lambda b: flat(b[:, :, :]), WS)

            x_exp(0)
            x_exp(1)
            p_hi(0)
            x_exp(2)
            p_hi(1)
            x_exp(3)
            p_hi(2)
            p_hi(3)

    @block.vector
    def _(dve):
        V = nc.vector
        STEPS_DVE = GROUPS + 4 + 2 * NQ + 1
        count = [0]

        with nc.vector.Fori(0, NB) as i:
            def after(ins):
                count[0] += 1
                ins.then_inc(dve_step, 1)
                dve.wait_ge(dve_step, i * STEPS_DVE + count[0])

            def lo(kind, n, out, slots, bank, high, scale):
                slot, _ = slots.at(i, kind, n)
                dve.wait_ge(hi_done, hi_count(i, kind, n))
                V.scalar_tensor_tensor(out, bank(slots.banks[slot]), scale, high, ALU.mult, ALU.subtract
                                       ).then_inc(slots.empty[slot], 1)

            def normalize(gr):
                slot, value = g.at(i, "ct", gr)
                dve.wait_ge(g.full[slot], value + 1)
                bank = G[slot][:, :].rearrange("p (t h d) -> p t h d", t=NQ, h=4)
                after(V.reciprocal(inv[:, gr, :, :], bank[:, :, :, HD]))
                V.tensor_tensor(ctx_tok[:, :, gr * 64:gr * 64 + 64].rearrange("p t (h d) -> p t h d", h=4),
                                bank[:, :, :, 0:HD], inv[:, gr, :, :].unsqueeze(3).to_broadcast([128, NQ, 4, HD]),
                                ALU.mult).then_inc(g.empty[slot], 1)

            def moments(n, buf):
                tiles = range(n % 2 * 2, n % 2 * 2 + 2)
                for t in tiles:
                    last = V.bn_stats(stats[:, n // 2 * NQ + t, :], buf[:, t, :])
                after(last)
                dve.sem_inc(stats_seen, 1)
                for t in tiles:
                    last = V.bn_aggr(meanvar[:, n // 2 * NQ + t, :], stats[:, n // 2 * NQ + t, :])
                last.then_inc(var_done, 1)

            def scaled(n, buf, done):
                dve.wait_ge(rstd_done, i * 4 + n + 1)
                for t in range(n % 2 * 2, n % 2 * 2 + 2):
                    at = n // 2 * NQ + t
                    last = V.tensor_scalar(buf[:, t, :], buf[:, t, :], meanvar[:, at, 0:1], rstd[:, at:at + 1],
                                           ALU.subtract, ALU.mult)
                last.then_inc(done, 1)

            for kind, n in ALPHA:
                if kind == "m":
                    slot, value = g.at(i, kind, n)
                    dve.wait_ge(g.full[slot], value + 1)
                    reduce_maxima(nc, keep, G[slot], MAXES[n]).then_inc(g.empty[slot], 1)
                elif kind == "ct":
                    normalize(n)
            normalize(GROUPS - 1)
            for c in range(DC):
                lo("cx", c, ctxT[:, 1, c, :], g, lambda b: b[:, :], ctxT[:, 0, c, :], XS)
                project.dve_x(dve, i, c)
            dve.wait_ge(xb_done, i + 1)
            for n in range(2):
                slot, value = g.at(i, "o", n)
                dve.wait_ge(g.full[slot], value + 1)
                V.scalar_tensor_tensor(x1[:, 2 * n:2 * n + 2, :],
                                       G[slot][:, :].rearrange("p (t d) -> p t d", t=2), 1.0 / (WS * XS),
                                       x_res[:, 2 * n:2 * n + 2, :], ALU.mult, ALU.add).then_inc(g.empty[slot], 1)
                dve.wait_ge(g.empty[slot], value + 1)
                moments(n, x1)
            for n in range(2):
                scaled(n, x1, x1_ready)
            for c in range(DC):
                lo("xa", c, x1T[:, 1, c, :], g, lambda b: b[:, :], x1T[:, 0, c, :], XS)

            def x_shift(t):
                slot, value = r.at(i, "S", t)
                dve.wait_ge(r.full[slot], value + 1)
                s3 = flat(R[slot][:, :, :]).rearrange("p (h k) -> p h k", h=XH)
                after(V.tensor_reduce(xmax[:, t, :], s3, AX.X, ALU.max))
                V.tensor_tensor(e_x[:, t, :].rearrange("p (h k) -> p h k", h=XH), s3,
                                xmax[:, t, :].unsqueeze(2).to_broadcast([128, XH, KV]),
                                ALU.subtract).then_inc(r.empty[slot], 1)

            def x_sum(t):
                dve.wait_ge(e_exp, i * NQ + t + 1)
                after(V.tensor_reduce(xsum[:, t, :], e_x[:, t, :].rearrange("p (h k) -> p h k", h=XH),
                                      AX.X, ALU.add))
                V.reciprocal(xinv[:, t, :], xsum[:, t, :]).then_inc(e_inv, 1)

            def p_lo(t):
                high = pT[:, t % 2, 0, :, :].rearrange("p k q -> p (k q)")
                lo("T", t, pT[:, t % 2, 1, :, :].rearrange("p k q -> p (k q)"), r, lambda b: flat(b[:, :, :]), high, WS)

            def x_out(t):
                slot, value = g.at(i, "O", t)
                dve.wait_ge(g.full[slot], value + 1)
                V.scalar_tensor_tensor(x2[:, t, :], G[slot][:, 0:D], 1.0 / (WS * WS), x1_b[:, t, :],
                                       ALU.mult, ALU.add).then_inc(g.empty[slot], 1)
                if t % 2 == 1:
                    dve.wait_ge(g.empty[slot], value + 1)

            project.dve_v(dve, i, 0, i + 1 + START)
            x_shift(0)
            x_shift(1)
            x_sum(0)
            x_sum(1)
            project.dve_v(dve, i, 1, i + 1 + START)
            x_shift(2)
            p_lo(0)
            x_sum(2)
            x_shift(3)
            p_lo(1)
            x_sum(3)
            dve.wait_ge(x2_stored, i * 16 + START)
            dve.wait_ge(x1b_done, i + 1)
            x_out(0)
            p_lo(2)
            x_out(1)
            moments(2, x2)
            p_lo(3)
            x_out(2)
            scaled(2, x2, x2_ready)
            x_out(3)
            moments(3, x2)
            scaled(3, x2, x2_ready)
            dve.wait_ge(x2_ready, i * 2 + 2)
            tiles = bass.ds(i * NQ, NQ)
            after(V.tensor_scalar(xhl[:, tiles, 0:D], x2[:, :, :], XS, None, ALU.mult))
            V.scalar_tensor_tensor(xhl[:, tiles, D:2 * D], x2[:, :, :], XS, xhl[:, tiles, 0:D],
                                   ALU.mult, ALU.subtract)
            assert count[0] == STEPS_DVE, count

    @block.tensor
    def _(pe):
        M = nc.tensor

        with nc.tensor.Fori(0, NB) as i:
            def opened(slots, kind, n):
                slot, value = slots.at(i, kind, n)
                pe.wait_ge(slots.empty[slot], value)
                return slots.banks[slot], slots.full[slot]

            def read(slots, kind, n):
                slot, value = slots.at(i, kind, n)
                pe.wait_ge(slots.empty[slot], value + 1)

            def transposed(kind, c, src):
                bank, full = opened(g, kind, c)
                for t in range(NQ):
                    last = M.transpose(bank[:, t * 128:t * 128 + 128], src[:, t, c * 128:c * 128 + 128], ident[:, :])
                last.then_inc(full, 1)

            def score(n):
                gr, j, k = n // 2 // NQ, n // 2 % NQ, n % 2
                bank, full = opened(r, "s", n)
                p = 2 * gr + k
                for par in range(2):
                    rows = slice(64 * par, 64 * par + STACK + 1)
                    last = M.matmul(bank[:, par, 0:S - 128 * j], ks_e[rows, p, 128 * j:128 * j + 128],
                                    qs_e[rows, p, 128 * j:S], start=True, stop=True)
                last.then_inc(full, 1)

            def weigh(u):
                gr, j = u // NQ, u % NQ
                if j == 0:
                    pe.wait_ge(pv_empty[gr % 2], i * 2 + gr // 2 + START)
                pe.wait_ge(probs_ready, i * SCORES + 2 * u + 2)
                for hd in range(4):
                    last = M.matmul(PV[gr % 2][32 * hd:32 * hd + 32, 128 * j:S], v_aug[:, j, 4 * gr + hd, :],
                                    probs[:, (2 * u + hd // 2) % 4, hd % 2, 0:S - 128 * j],
                                    start=(j == 0), stop=(j == NQ - 1))
                last.then_inc(probs_used, 1)

            def tokens(gr):
                pe.wait_ge(pv_empty[gr % 2], i * 2 + gr // 2 + 1 + START)
                bank, full = opened(g, "ct", gr)
                for t in range(NQ):
                    last = M.transpose(bank[:, t * 128:t * 128 + 128], cu[:, gr % 2, t * 128:t * 128 + 128], ident[:, :])
                last.then_inc(full, 1)

            pe.wait_ge(v_copied, i + START)
            pe.wait_ge(stack_e, i * 14 * 16 + START)
            pe.wait_ge(stack_m, i * 12 * 16 + START)
            for kind, n in ALPHA:
                if kind == "s":
                    score(n)
                elif kind == "w":
                    weigh(n)
                elif kind == "ct":
                    tokens(n)
                elif kind == "m":
                    bank, full = opened(g, kind, n)
                    score_maxima(nc, keep, bank, MAXES[n], qs_m, ks_m).then_inc(full, 1)
                elif kind == "mT":
                    if n == 0:
                        read(g, "m", len(MAXES) - 2)
                        read(g, "m", len(MAXES) - 1)
                    bank, full = opened(g, kind, n)
                    for t in range(2):
                        last = M.transpose(bank[0:H, t * 128:t * 128 + 128], keep["rowmax"][:, 2 * n + t, :],
                                           ident[:, :])
                    last.then_inc(full, 1)
            for kind, n in BETA:
                if kind == "ct":
                    tokens(n)
                elif kind == "cx":
                    for gr in (2 * n, 2 * n + 1):
                        read(g, "ct", gr)
                    transposed(kind, n, ctx_tok)
                elif kind == "xT":
                    project.pe_x(pe, i, n, i * 16 + START)
                elif kind == "q":
                    project.pe_q(pe, i, n)
                elif kind == "v":
                    project.pe_v(pe, i, n)
                elif kind == "o":
                    if n == 0:
                        for c in range(DC):
                            read(g, "cx", c)
                    bank, full = opened(g, kind, n)
                    for t in range(2):
                        at = (2 * n + t) * 128
                        last = three(nc, bank[:, t * D:t * D + D], lambda hl, c: ctxT[:, hl, c, at:at + 128],
                                     lambda hl, c: w_hl[:, hl, 3, c, :], DC)
                    last.then_inc(full, 1)
                elif kind == "xa":
                    pe.wait_ge(x1_ready, i * 2 + 2)
                    transposed(kind, n, x1)
                elif kind == "S":
                    if n == 0:
                        pe.wait_ge(ax_in, i * 16 + 16)
                        for c in range(DC):
                            read(g, "xa", c)
                    bank, full = opened(r, kind, n)
                    for half in range(2):
                        last = three(nc, bank[:, half, :], lambda hl, c: x1T[:, hl, c, n * 128:n * 128 + 128],
                                     lambda hl, c: a_x[:, hl, c, half * 512:half * 512 + 512], DC)
                    last.then_inc(full, 1)
                elif kind == "T":
                    pe.wait_ge(e_prob, i * NQ + n + 1)
                    bank, full = opened(r, kind, n)
                    for k in range(PAIRS):
                        last = M.transpose(flat(bank[:, :, :])[:, k * 128:k * 128 + 128],
                                           e_x[:, n, k * 128:k * 128 + 128], ident[:, :])
                    last.then_inc(full, 1)
                elif kind == "O":
                    if n == 0:
                        pe.wait_ge(vw_in, i * 16 + 16)
                    read(r, "T", n)
                    bank, full = opened(g, kind, n)
                    three(nc, bank[:, 0:D], lambda hl, k: pT[:, n % 2, hl, k, :],
                          lambda hl, k: vw[:, hl, k, :], PAIRS).then_inc(full, 1)


def expert_block(nc, ctx, dram, keep):
    ident, ident16, xhl = keep["ident"], keep["ident16"], keep["xhl"]

    def sb(name, shape, dt=F32):
        return ctx.enter_context(nc.sbuf_tensor(name, shape, dt))

    def sem(name):
        return ctx.enter_context(nc.semaphore(name))

    before = sb("before", [128, 128], F16)
    ones16 = sb("ones16", [128, 128], F16)
    w_scale = sb("w_scale", [128, 1])
    iota_e = sb("iota_e", [128, NE])
    iota_s = sb("iota_s", [128, NE])
    iota_t = sb("iota_t", [128, TILES])
    wg_f = sb("wg_f", [128, DC, NE])
    wg = sb("wg", [128, 2, DC, NE], F16)
    logits = sb("logits", [128, NT * NE])
    top = sb("top", [128, NT, 8])
    topi = sb("topi", [128, NT, 8], U32)
    topf = sb("topf", [128, NT, 2])
    gap = sb("gap", [128, NT])
    gate = sb("gate", [128, 2, NT])
    hot = sb("hot", [128, 2, NT, NE])
    hot16 = sb("hot16", [128, NT, NE], F16)
    run = sb("run", [128, 2, NT, NE])
    fits = sb("fits", [128, NE, NE])
    tiles_e = sb("tiles_e", [128, NE])
    upto = sb("upto", [128, 2, NE])
    pos = sb("pos", [128, NT, NE])
    pick = sb("pick", [128, 2, NT, NE])
    slot_f = sb("slot_f", [128, 2, NT])
    slot = sb("slot", [128, 2, NT], I32)
    below = sb("below", [128, TILES, NE])
    eid_f = sb("eid_f", [128, TILES])
    eid = sb("eid", [128, TILES], I32)
    b1r = sb("b1r", [NE * FM, 128])
    b1T = sb("b1T", [128, NE * FM])
    b1 = sb("b1", [128, 2, FM])
    w1f = sb("w1f", [128, 2, DC, FF])
    w2f = sb("w2f", [128, 2, FM, D])
    w1 = sb("w1", [128, 2, 2, DC, FF], F16)
    w2 = sb("w2", [128, 2, 2, FM, D], F16)
    xg = sb("xg", [128, 2, 2, 2 * D], F16)
    xT = sb("xT2", [128, 2, 2 * DC, SLOTS], F16)
    hf = sb("hf", [128, FM, SLOTS])
    h = sb("h", [128, 2, 2, FM, SLOTS], F16)
    b2_rows = sb("b2_rows", [128, NE * D])
    b2 = sb("b2", [128, 2, D])
    y = sb("y", [128, 2, 2, D])
    power = sb("power2", [128, 2 * NQ])
    parts = sb("parts", [128, NT, 2, D])
    z = sb("z", [128, NT, D])
    stats = sb("stats2", [128, NQ, 6])
    meanvar = sb("meanvar2", [128, NQ, 2])
    rstd = sb("rstd2", [128, NQ])

    HB = [ctx.enter_context(nc.psum_tensor(f"HB{i}", [128, 2, SLOTS], F32)) for i in range(4)]
    YB = [ctx.enter_context(nc.psum_tensor(f"YB{i}", [128, 2, D], F32)) for i in range(2)]
    XBS = [ctx.enter_context(nc.psum_tensor(f"XB{i}", [128, 2 * DC, SLOTS], F16)) for i in range(2)]
    XB = XBS[0]
    LB, rank, total, b1B = HB[2][:, 0, 0:NT * NE], HB[3][:, 0, 0:128], HB[3][:, 0, 128:256], HB[3][:, 1, 0:NE * FM]

    const_step, consts, rt_step, ranks = sem("ec_step"), sem("ec_done"), sem("rt_step"), sem("ranks")
    gap_done, gexp_done, slot_done, eid_done, b1_in = (
        sem("gap_done"), sem("gexp_done"), sem("slot_done"), sem("eid_done"), sem("b1_in"))
    scattered = sem("scattered")
    w1_in = [sem(f"w1_in{i}") for i in range(2)]
    w2_in = [sem(f"w2_in{i}") for i in range(2)]
    xg_in = [sem(f"xg_in{i}") for i in range(2)]
    b2_in, b2_done = sem("b2_in"), sem("b2_done")
    w2_scaled = sem("w2_scaled")
    w1_hi, w2_hi, w1_split, w2_split = sem("w1_hi"), sem("w2_hi"), sem("w1_split"), sem("w2_split")
    xt_full, xt_done, b1_done = sem("xt_full"), sem("xt_done"), sem("b1_done")
    h_full, h_gelu, h_hi, h_split = sem("h_full"), sem("h_gelu"), sem("h_hi"), sem("h_split")
    y_full, y_done = sem("y_full"), sem("y_done")
    y_out = [sem(f"y_out{i}") for i in range(2)]
    wg_in, wg_hi, wg_lo = sem("wg_in"), sem("wg_hi"), sem("wg_lo")
    lt_full, lt_act, lt_dve, lg_done = sem("lt_full"), sem("lt_act"), sem("lt_dve"), sem("lg_done")
    hot_done, x2_in = sem("hot_done"), sem("x2_in")
    parts_in = [sem(f"parts_in{i}") for i in range(NT // NQ)]
    var_done, pool_step, rstd_done = sem("var2_done"), sem("pool2_step"), sem("rstd2_done")
    z_done, stored = sem("z_done"), sem("stored")

    TRIPS = (TILES - 3) // 2
    assert TILES % 2 == 1 and NT // NQ * NQ == NT and T // SLOTS <= NE

    def run_steps(eng, step):
        step(0, 0, 0)
        step(1, 0, 1)
        with eng.Fori(0, TRIPS) as i:
            step(2 * i + 2, i + 1, 0)
            step(2 * i + 3, i + 1, 1)
        step(TILES - 1, TILES // 2, 0)

    def is_int(n, *values):
        return isinstance(n, int) and n in values

    def following(n, j, q):
        return n + 1, j + q, 1 - q

    block = ctx.enter_context(nc.Block())

    @block.sync
    def _(sp):
        sp.dma_start(wg_f[:, :, :], dram["WgT"]).then_inc(wg_in, 16)
        sp.dma_start(b1r[:, :], dram["b1"].rearrange("e (m p) -> (e m) p", p=128)).then_inc(b1_in, 16)
        sp.dma_start(b2_rows[:, :], dram["b2"].rearrange("e d -> (e d)")
                     .partition_broadcast(128)).then_inc(b2_in, 16)
        sp.wait_ge(eid_done, 1)

        def load(n, j, q):
            old = not is_int(n, 0, 1)
            e = nc.sync.value_load(eid[0:1, bass.ds(n, 1)], min_val=0, max_val=NE - 1)
            if old:
                sp.wait_ge(xt_full, n - 1)
            else:
                sp.wait_ge(scattered, 2 * NT * 16)
            sp.dma_start(xg[:, q, :, :], dram["xs"][bass.ds(n * SLOTS, SLOTS), :]
                         .rearrange("(t p) d -> p t d", p=128)).then_inc(xg_in[q], 16)
            if old:
                sp.wait_ge(w1_split, n - 1)
            sp.dma_start(w1f[:, q, :, :], dram["W1"][bass.ds(e * D, D), :]
                         .rearrange("(c p) f -> p c f", p=128)).then_inc(w1_in[q], 16)
            if old:
                sp.wait_ge(w2_split, n - 1)
            sp.dma_start(w2f[:, q, :, :], dram["W2"][bass.ds(e * FF, FF), :]
                         .rearrange("(m p) d -> p m d", p=128)).then_inc(w2_in[q], 16)

        run_steps(nc.sync, load)
        sp.dma_start(z[:, :, :], dram["x2"].rearrange("(t p) d -> p t d", p=128)).then_inc(x2_in, 16)
        for k in range(NT // NQ):
            sp.wait_ge(z_done, k + 1)
            sp.dma_start(dram["out"][k * S:(k + 1) * S, :].rearrange("(t p) d -> p t d", p=128),
                         z[:, k * NQ:(k + 1) * NQ, :]).then_inc(stored, 16)
        sp.wait_ge(stored, NT // NQ * 16)

    @block.gpsimd
    def _(pool):
        P = nc.gpsimd
        P.memset(before[:, :], 0.0).then_inc(const_step, 1)
        P.memset(ones16[:, :], 1.0).then_inc(const_step, 1)
        P.iota(topi[:, 0, :], pattern=[[1, NE]], base=0, channel_multiplier=0).then_inc(const_step, 1)
        P.iota(eid[:, :], pattern=[[1, TILES]], base=0, channel_multiplier=0).then_inc(const_step, 1)
        P.memset(power[:, 0:NQ], EPS).then_inc(const_step, 1)
        P.memset(power[:, NQ:], -0.5).then_inc(const_step, 1)
        P.memset(w_scale[:, :], WS).then_inc(const_step, 1)
        pool.wait_ge(const_step, 7)
        P.affine_select(out=before[:, :], in_=before[:, :], compare_op=ALU.is_ge, fill=1.0, base=0,
                        pattern=[[-1, 128]], channel_multiplier=1).then_inc(consts, 1)
        P.tensor_copy(iota_e[:, :], topi[:, 0, :]).then_inc(consts, 1)
        P.tensor_copy(iota_t[:, :], eid[:, :]).then_inc(consts, 1)
        pool.wait_ge(slot_done, 1)
        for t in range(NT):
            for c in range(2):
                pool.indirect_dma_start(out=dram["xs"], out_offset=bass.IndirectOffsetOnAxis(slot[:, c, t:t + 1], 0),
                                        in_=xhl[:, t, :], in_offset=None).then_inc(scattered, 16)

        def split(n, j, q):
            pool.wait_ge(w2_in[q], j * 16 + 16)
            scaled = w2f[:, q, :, :].rearrange("p m d -> p (m d)")
            P.tensor_tensor(scaled, scaled, w_scale[:, :].to_broadcast([128, FM * D]), ALU.mult).then_inc(w2_scaled, 1)
            pool.wait_ge(w2_hi, n + 1)
            P.tensor_tensor(w2[:, q, 1, :, :].rearrange("p m d -> p (m d)"), scaled,
                            w2[:, q, 0, :, :].rearrange("p m d -> p (m d)"), ALU.subtract).then_inc(w2_split, 1)

        run_steps(nc.gpsimd, split)
        pool.wait_ge(y_out[0], (TILES + 1) // 2 * 16)
        pool.wait_ge(y_out[1], TILES // 2 * 16)

        def gather(k):
            for t in range(k * NQ, (k + 1) * NQ):
                for c in range(2):
                    pool.indirect_dma_start(out=parts[:, t, c, :], out_offset=None, in_=dram["ys"],
                                            in_offset=bass.IndirectOffsetOnAxis(slot[:, c, t:t + 1], 0)
                                            ).then_inc(parts_in[k], 16)

        def root(k):
            pool.wait_ge(var_done, k + 1)
            P.tensor_tensor(rstd[:, :], meanvar[:, :, 1], power[:, 0:NQ], ALU.add).then_inc(pool_step, 1)
            pool.wait_ge(pool_step, k + 1)
            P.tensor_tensor(rstd[:, :], rstd[:, :], power[:, NQ:], ALU.pow).then_inc(rstd_done, 1)

        gather(0)
        for k in range(1, NT // NQ):
            gather(k)
            root(k - 1)
        root(NT // NQ - 1)

    @block.scalar
    def _(act):
        A = nc.scalar
        act.wait_ge(wg_in, 16)
        A.activation(wg[:, 0, :, :], wg_f[:, :, :], ACT.Copy, scale=WS).then_inc(wg_hi, 1)
        for n in range(1, NT // 2, 2):
            act.wait_ge(lt_full, n + 1)
            if n >= 2:
                act.wait_ge(lg_done, n - 1)
            A.activation(xT[:, 1, :, :], XBS[1][:, :, :], ACT.Copy).then_inc(lt_act, 1)
        act.wait_ge(gap_done, 1)
        A.activation(gate[:, 1, :], gap[:, :], ACT.Exp).then_inc(gexp_done, 1)

        def w1_high(n, j, q):
            act.wait_ge(w1_in[q], j * 16 + 16)
            if not is_int(n, 0, 1):
                act.wait_ge(h_full, 4 * n - 4)
            A.activation(w1[:, q, 0, :, :].rearrange("p c f -> p (c f)"),
                         w1f[:, q, :, :].rearrange("p c f -> p (c f)"), ACT.Copy, scale=WS).then_inc(w1_hi, 1)

        def store(n, q):
            act.wait_ge(y_done, n + 1)
            act.dma_start(dram["ys"][bass.ds(n * SLOTS, SLOTS), :].rearrange("(t p) d -> p t d", p=128),
                          y[:, q, :, :]).then_inc(y_out[q], 16)

        def step(n, j, q):
            act.wait_ge(b1_done, n + 1)
            for b in range(4):
                act.wait_ge(h_full, 4 * n + b + 1)
                if not is_int(n, 0):
                    act.wait_ge(h_split, 4 * n - 3 + b)
                for m in range(2):
                    last = A.activation(hf[:, 2 * b + m, :], HB[b][:, m, :], ACT.Gelu,
                                        bias=b1[:, q, 2 * b + m:2 * b + m + 1], scale=1.0 / (WS * XS))
                last.then_inc(h_gelu, 1)
            if not is_int(n, TILES - 1):
                w1_high(*following(n, j, q))
            act.wait_ge(w2_scaled, n + 1)
            if not is_int(n, 0, 1):
                act.wait_ge(y_full, n - 1)
            A.activation(w2[:, q, 0, :, :].rearrange("p m d -> p (m d)"),
                         w2f[:, q, :, :].rearrange("p m d -> p (m d)"), ACT.Copy).then_inc(w2_hi, 1)
            if not is_int(n, 0, 1):
                store(n - 2, q)

        w1_high(0, 0, 0)
        run_steps(nc.scalar, step)
        store(TILES - 2, 1)
        store(TILES - 1, 0)

    @block.vector
    def _(dve):
        V = nc.vector
        count = [0]

        def after(ins):
            count[0] += 1
            ins.then_inc(rt_step, 1)
            dve.wait_ge(rt_step, count[0])

        def wide(ap, *shape):
            return ap.to_broadcast([128, *shape])

        dve.wait_ge(wg_hi, 1)
        V.scalar_tensor_tensor(wg[:, 1, :, :], wg_f[:, :, :], WS, wg[:, 0, :, :], ALU.mult,
                               ALU.subtract).then_inc(wg_lo, 1)
        for n in range(0, NT // 2, 2):
            dve.wait_ge(lt_full, n + 1)
            if n >= 2:
                dve.wait_ge(lg_done, n - 1)
            V.tensor_copy(xT[:, 0, :, :], XBS[0][:, :, :]).then_inc(lt_dve, 1)
        dve.wait_ge(lg_done, NT // 2)
        after(V.tensor_scalar(logits[:, :], LB, 1.0 / (WS * XS), None, ALU.mult))
        dve.wait_ge(consts, 3)
        for t in range(NT):
            last = V.max(top[:, t, :], logits[:, t * NE:t * NE + NE])
        after(last)
        V.tensor_tensor(gap[:, :], top[:, :, 1], top[:, :, 0], ALU.subtract).then_inc(gap_done, 1)
        for t in range(NT):
            last = V.max_index(topi[:, t, :], top[:, t, :], logits[:, t * NE:t * NE + NE])
        after(last)
        after(V.tensor_copy(topf[:, :, :], topi[:, :, 0:2]))
        for c in range(2):
            last = V.tensor_tensor(hot[:, c, :, :], wide(topf[:, :, c:c + 1], NT, NE),
                                   wide(iota_e[:, :].unsqueeze(1), NT, NE), ALU.is_equal)
        after(last)
        V.tensor_tensor(hot16[:, :, :], hot[:, 0, :, :], hot[:, 1, :, :], ALU.add).then_inc(hot_done, 1)
        V.tensor_scalar(iota_s[:, :], iota_e[:, :], float(SLOTS), None, ALU.mult)
        dve.wait_ge(ranks, 1)
        V.tensor_copy(b1T[:, :], b1B)
        after(V.tensor_copy(run[:, 0, :, :], total.rearrange("p (t e) -> p t e", e=NE)))
        cur = 0
        for k in (1, 2, 4, 8):
            V.tensor_copy(run[:, 1 - cur, 0:k, :], run[:, cur, 0:k, :])
            after(V.tensor_tensor(run[:, 1 - cur, k:, :], run[:, cur, k:, :], run[:, cur, 0:NT - k, :], ALU.add))
            cur = 1 - cur
        after(V.tensor_tensor(fits[:, :, :], wide(run[:, cur, NT - 1, :].unsqueeze(2), NE, NE),
                              wide(iota_s[:, :].unsqueeze(1), NE, NE), ALU.is_gt))
        after(V.tensor_reduce(tiles_e[:, :], fits[:, :, :], AX.X, ALU.add))
        after(V.tensor_copy(upto[:, 0, :], tiles_e[:, :]))
        at = 0
        for k in (1, 2, 4):
            V.tensor_copy(upto[:, 1 - at, 0:k], upto[:, at, 0:k])
            after(V.tensor_tensor(upto[:, 1 - at, k:], upto[:, at, k:], upto[:, at, 0:NE - k], ALU.add))
            at = 1 - at
        after(V.tensor_tensor(below[:, :, :], wide(upto[:, at, :].unsqueeze(1), TILES, NE),
                              wide(iota_t[:, :].unsqueeze(2), TILES, NE), ALU.is_le))
        after(V.tensor_reduce(eid_f[:, :], below[:, :, :], AX.X, ALU.add))
        V.tensor_scalar(eid[:, :], eid_f[:, :], NE - 1.0, None, ALU.min).then_inc(eid_done, 1)
        V.tensor_tensor(upto[:, 1 - at, :], upto[:, at, :], tiles_e[:, :], ALU.subtract)
        after(V.tensor_tensor(run[:, 1 - cur, :, :], run[:, cur, :, :],
                              total.rearrange("p (t e) -> p t e", e=NE), ALU.subtract))
        after(V.tensor_tensor(run[:, cur, :, :], run[:, 1 - cur, :, :],
                              rank.rearrange("p (t e) -> p t e", e=NE), ALU.add))
        after(V.scalar_tensor_tensor(pos[:, :, :], wide(upto[:, 1 - at, :].unsqueeze(1), NT, NE), float(SLOTS),
                                     run[:, cur, :, :], ALU.mult, ALU.add))
        after(V.tensor_tensor(pick[:, :, :, :], hot[:, :, :, :], wide(pos[:, :, :].unsqueeze(1), 2, NT, NE), ALU.mult))
        after(V.tensor_reduce(slot_f[:, :, :], pick[:, :, :, :], AX.X, ALU.add))
        V.tensor_copy(slot[:, :, :], slot_f[:, :, :]).then_inc(slot_done, 1)
        dve.wait_ge(gexp_done, 1)
        after(V.tensor_scalar(gap[:, :], gate[:, 1, :], 1.0, None, ALU.add))
        after(V.reciprocal(gate[:, 0, :], gap[:, :]))
        after(V.tensor_tensor(gate[:, 1, :], gate[:, 1, :], gate[:, 0, :], ALU.mult))
        dve.wait_ge(eid_done, 1)

        def ready(n, j, q):
            e = nc.vector.value_load(eid[0:1, bass.ds(n, 1)], min_val=0, max_val=NE - 1)
            V.tensor_copy(b1[:, q, :], b1T[:, bass.ds(e * FM, FM)]).then_inc(b1_done, 1)
            dve.wait_ge(xt_full, n + 1)
            V.tensor_copy(xT[:, q, :, :], XB[:, :, :]).then_inc(xt_done, 1)
            dve.wait_ge(w1_hi, n + 1)
            V.scalar_tensor_tensor(w1[:, q, 1, :, :].rearrange("p c f -> p (c f)"),
                                   w1f[:, q, :, :].rearrange("p c f -> p (c f)"), WS,
                                   w1[:, q, 0, :, :].rearrange("p c f -> p (c f)"),
                                   ALU.mult, ALU.subtract).then_inc(w1_split, 1)

        def output(n, j, q):
            e = nc.vector.value_load(eid[0:1, bass.ds(n, 1)], min_val=0, max_val=NE - 1)
            V.tensor_copy(b2[:, q, :], b2_rows[:, bass.ds(e * D, D)]).then_inc(b2_done, 1)
            dve.wait_ge(b2_done, n + 1)
            dve.wait_ge(y_full, n + 1)
            if not is_int(n, 0, 1):
                dve.wait_ge(y_out[q], j * 16)
            V.scalar_tensor_tensor(y[:, q, :, :], YB[q][:, :, :], 1.0 / (WS * XS),
                                   wide(b2[:, q, :].unsqueeze(1), 2, D), ALU.mult, ALU.add).then_inc(y_done, 1)

        def step(n, j, q):
            if not is_int(n, 0, 1):
                dve.wait_ge(y_full, n - 1)
            for b in range(4):
                pair = slice(2 * b, 2 * b + 2)
                dve.wait_ge(h_gelu, 4 * n + b + 1)
                V.tensor_scalar(h[:, q, 0, pair, :], hf[:, pair, :], XS, None, ALU.mult).then_inc(h_hi, 1)
                dve.wait_ge(h_hi, 4 * n + b + 1)
                V.scalar_tensor_tensor(h[:, q, 1, pair, :], hf[:, pair, :], XS, h[:, q, 0, pair, :],
                                       ALU.mult, ALU.subtract).then_inc(h_split, 1)
            if not is_int(n, TILES - 1):
                ready(*following(n, j, q))
            if not is_int(n, 0):
                output(n - 1, j - 1 + q, 1 - q)

        dve.wait_ge(b2_in, 16)
        ready(0, 0, 0)
        run_steps(nc.vector, step)
        output(TILES - 1, TILES // 2, 0)

        dve.wait_ge(x2_in, 16)
        for k in range(NT // NQ):
            dve.wait_ge(parts_in[k], 2 * NQ * 16)
            tiles = range(k * NQ, (k + 1) * NQ)
            for c in range(2):
                for t in tiles:
                    last = V.scalar_tensor_tensor(z[:, t, :], parts[:, t, c, :], gate[:, c, t:t + 1], z[:, t, :],
                                                  ALU.mult, ALU.add)
                after(last)
            for t in tiles:
                last = V.bn_stats(stats[:, t % NQ, :], z[:, t, :])
            after(last)
            for t in tiles:
                last = V.bn_aggr(meanvar[:, t % NQ, :], stats[:, t % NQ, :])
            last.then_inc(var_done, 1)
            dve.wait_ge(rstd_done, k + 1)
            for t in tiles:
                last = V.tensor_scalar(z[:, t, :], z[:, t, :], meanvar[:, t % NQ, 0:1], rstd[:, t % NQ:t % NQ + 1],
                                       ALU.subtract, ALU.mult)
            last.then_inc(z_done, 1)

    @block.tensor
    def _(pe):
        M = nc.tensor

        def router(n):
            if n % 2 == 0:
                pe.wait_ge(lt_dve, n // 2 + 1)
            else:
                pe.wait_ge(lt_act, n // 2 + 1)
            for t in range(2):
                at = (2 * n + t) * NE
                last = three(nc, LB[:, at:at + NE], lambda hl, c: xT[:, n % 2, hl * DC + c, t * 128:t * 128 + 128],
                             lambda hl, c: wg[:, hl, c, :], DC)
            last.then_inc(lg_done, 1)

        for n in range(NT // 2):
            if n >= 2:
                pe.wait_ge(lg_done, n - 1)
            for k in range(2 * DC):
                for t in range(2):
                    last = M.transpose(XBS[n % 2][:, k, t * 128:t * 128 + 128],
                                       xhl[:, 2 * n + t, k * 128:k * 128 + 128], ident16[:, :])
            last.then_inc(lt_full, 1)
            if n == 0:
                pe.wait_ge(wg_lo, 1)
            else:
                router(n - 1)
        router(NT // 2 - 1)
        pe.wait_ge(consts, 3)
        pe.wait_ge(b1_in, 16)
        M.transpose(b1B, b1r[:, :], ident[0:NE * FM, 0:NE * FM])
        pe.wait_ge(hot_done, 1)
        hot2 = hot16[:, :, :].rearrange("p t e -> p (t e)")
        M.matmul(rank, before[:, :], hot2, start=True, stop=True)
        M.matmul(total, ones16[:, :], hot2, start=True, stop=True).then_inc(ranks, 1)

        def transposes(n, j, q):
            pe.wait_ge(xg_in[q], j * 16 + 16)
            if not is_int(n, 0):
                pe.wait_ge(xt_done, n)
            for k in range(2 * DC):
                for t in range(2):
                    last = M.transpose(XB[:, k, t * 128:t * 128 + 128], xg[:, q, t, k * 128:k * 128 + 128],
                                       ident16[:, :])
            last.then_inc(xt_full, 1)

        def second(n, j, q):
            pe.wait_ge(h_split, 4 * n + 4)
            pe.wait_ge(w2_split, n + 1)
            if not is_int(n, 0, 1):
                pe.wait_ge(y_done, n - 1)
            for t in range(2):
                last = three(nc, YB[q][:, t, :], lambda hl, m: h[:, q, hl, m, t * 128:t * 128 + 128],
                             lambda hl, m: w2[:, q, hl, m, :], FM)
            last.then_inc(y_full, 1)

        def step(n, j, q):
            pe.wait_ge(xt_done, n + 1)
            pe.wait_ge(w1_split, n + 1)
            for b in range(4):
                if not is_int(n, 0):
                    pe.wait_ge(h_gelu, 4 * n - 3 + b)
                for m in range(2):
                    at = (2 * b + m) * 128
                    last = three(nc, HB[b][:, m, :], lambda hl, c: w1[:, q, hl, c, at:at + 128],
                                 lambda hl, c: xT[:, q, hl * DC + c, :], DC)
                last.then_inc(h_full, 1)
            if not is_int(n, TILES - 1):
                transposes(*following(n, j, q))
            if not is_int(n, 0):
                second(n - 1, j - 1 + q, 1 - q)

        transposes(0, 0, 0)
        run_steps(nc.tensor, step)
        second(TILES - 1, TILES // 2, 0)


def decoder_layer(nc, dram):
    def buffers(ctx, keep, *names):
        for name, shape, dt in names:
            keep[name] = ctx.enter_context(nc.sbuf_tensor(name, shape, dt))

    with ExitStack() as outer:
        keep = {"dram": dram}
        buffers(outer, keep, ("ident", [128, 128], F32), ("ident16", [128, 128], F16), ("xhl", [128, NT, 2 * D], F16))
        with ExitStack() as attention:
            buffers(attention, keep,
                    ("causal", [128, 128], F16), ("zeros", [128, 2 * D], F16), ("power", [128, 2 * NQ], F32),
                    ("x_tok", [128, NQ, D], F32), ("x_res", [128, NQ, D], F32),
                    ("xT", [128, 2, DC, S], F16),
                    ("qf", [128, 2, S], F32),
                    ("qk", [128, 2, 4, S], F16),
                    ("qs_m", [128, PAIRS, S], F16), ("ks_m", [128, PAIRS, S], F16),
                    ("qs_e", [128, PAIRS, S], F16), ("ks_e", [128, PAIRS, S], F16),
                    ("v_next", [128, NQ, D], F32), ("v_aug", [128, NQ, H, 32], F32),
                    ("rowmax", [128, NQ, H], F32), ("neg_maxT", [H, S], F16),
                    ("w_hl", [128, 2, 4, DC, D], F16),
                    ("qk_bias", [128, 2, 2], F32), ("b_rows", [128, 3, D], F32))
            with ExitStack() as ctx:
                prepare_block(nc, ctx, dram, keep)
            with ExitStack() as ctx:
                attention_block(nc, ctx, dram, keep)
        with ExitStack() as ctx:
            expert_block(nc, ctx, dram, keep)


_INS = {"x": "x", "ctx_768": "cond", "L0_attn_Wq": "Wq", "L0_attn_bq": "bq", "L0_attn_Wk": "Wk", "L0_attn_bk": "bk",
        "L0_attn_Wv": "Wv", "L0_attn_bv": "bv", "L0_attn_Wo": "Wo", "L0_attn_bo": "bo",
        "L0_xattn_w_q": "w_q", "L0_xattn_w_k": "w_k", "L0_xattn_w_v": "w_v", "L0_xattn_w_out": "w_out",
        "L0_xattn_b_out": "b_out", "L0_ffn_Wg": "WgT", "L0_ffn_W1": "W1", "L0_ffn_b1": "b1",
        "L0_ffn_W2": "W2", "L0_ffn_b2": "b2"}


def kernel(**inputs):
    import numpy as np
    import concourse.bacc as bacc
    from concourse.bass_utils import run_bass_kernel_spmd

    nc = bacc.Bacc("TRN2", target_bir_lowering=False, num_devices=1)
    arrays, dram = {}, {}
    for name, short in _INS.items():
        a = np.asarray(inputs[name])
        if short == "x" or short == "cond" or short in ("W1", "W2"):
            a = a.reshape(-1, a.shape[-1])
        elif short in ("bq", "bk"):
            a = a.reshape(DC, 128).T
        elif short == "WgT":
            a = a.T.reshape(DC, 128, NE).transpose(1, 0, 2)
        a = np.ascontiguousarray(a)
        arrays["in_" + short] = a
        dram[short] = nc.dram_tensor("in_" + short, a.shape, mybir.dt.from_np(a.dtype), kind="ExternalInput").ap()
    dram["out"] = nc.dram_tensor("out", (T, D), F32, kind="ExternalOutput").ap()
    for name, shape, dt in (("qk", (NB * 4 * D, S), F16), ("m", (H, S), F16), ("x2", (T, D), F32), ("ax", (NB * 128, 2 * DC * XA), F16),
                            ("vw", (NB * 128, 2 * PAIRS * D), F16),
                            ("xs", (TILES * SLOTS, 2 * D), F16), ("ys", (TILES * SLOTS, D), F32)):
        dram[name] = nc.dram_tensor("scratch_" + name, shape, dt).ap()
    decoder_layer(nc, dram)
    r = run_bass_kernel_spmd(nc, [arrays], core_ids=[0])
    return r.results[0]["out"].reshape(NB, S, D)
```

```python
import concourse.bass as bass
from concourse import mybir
from contextlib import ExitStack

F32 = mybir.dt.float32
F16 = mybir.dt.float16
I32 = mybir.dt.int32
U32 = mybir.dt.uint32
ALU = mybir.AluOpType
ACT = mybir.ActivationFunctionType
AX = mybir.AxisListType

NB, S, D = 4, 512, 256
T = NB * S
NQ = S // 128
NT = T // 128
DC = D // 128
H, HD = 16, 16
PAIRS = H // 2
GROUPS = H // 4
XH, XD, KV, DCOND = 16, 64, 64, 192
XA = XH * XD
NE, FF = 8, 1024
FM = FF // 128
SLOTS = 256
TILES = (2 * T + NE * (SLOTS - 1)) // SLOTS
HALVES = SLOTS // 128
EPS = 1e-5
WS = 64.0
XS = 16.0
QS = 4.0
NEG = -60000.0
STACK = 3 * HD
ROWS = 64


def max_items():
    items = []
    for t in range(NQ):
        pairs = max(1, 512 // (128 * (t + 1)))
        if PAIRS % pairs:
            pairs = 1
        items += [(t, par, p, pairs) for par in range(2) for p in range(0, PAIRS, pairs)]
    return items


MAXES = max_items()
UNITS = GROUPS * NQ


def project_steps(first):
    return ([("xT", 2 * first + n) for n in range(2)] + [("q", 4 * first + n) for n in range(4)]
            + [("v", 2 * first + n) for n in range(2)])


def prepare_steps():
    second = project_steps(1)
    steps = project_steps(0) + [("cT", 0), ("cT", 1), ("W", 0), ("W", 1)] + second[0:2]
    work = [(kind, n, k) for kind, n in [("kv", n) for n in range(4)] for k in range(4)]
    work += [(kind, n, None) for kind, n in second[2:]]
    work += [(kind, n, k) for n in range(2 * NB) for kind in ("A", "VW") for k in range(4)]
    first, last, m = 6, 6 + 16 + 6 + 30, 0
    for at, (kind, n, k) in enumerate(work):
        steps.append((kind + "+", 4 * n + k) if k is not None and k < 3 else (kind, n))
        upto = len(MAXES) * min(max(at - first, 0), last - first) // (last - first)
        if at == last + 1:
            steps += [("mT", 0), ("mT", 1)]
        steps += [("m", k) for k in range(m, upto)]
        m = upto
    return steps


def alpha_steps():
    steps, n = [("s", 0), ("s", 1)], 0
    for u in range(UNITS):
        gr, j = u // NQ, u % NQ
        upto = len(MAXES) * (gr * 10 + (3, 5, 6, 10)[j]) // (10 * GROUPS)
        half = (n + upto + 1) // 2
        if u + 1 < UNITS:
            steps.append(("s", 2 * u + 2))
        steps += [("m", k) for k in range(n, half)]
        if u + 1 < UNITS:
            steps.append(("s", 2 * u + 3))
        if u + 1 < UNITS:
            steps += [("m", k) for k in range(half, upto)]
        steps.append(("w", u))
        if j == 1 and gr > 0:
            steps.append(("ct", gr - 1))
        if u + 1 == UNITS:
            steps += [("m", k) for k in range(half, upto)]
        if u == UNITS - 2:
            steps.append(("cx", 0))
        n = upto
    return steps + [("ct", GROUPS - 1), ("mT", 0), ("mT", 1)]


PREPARE = prepare_steps()
ALPHA = alpha_steps()
PROJECT, MAXIMA = ("xT", "q", "v"), ("m", "mT")
BETA = [("xT", 0), ("cx", 1), ("xT", 1), ("o", 0), ("o", 1), ("q", 0), ("q", 1), ("q", 2), ("q", 3), ("xa", 0),
        ("xa", 1), ("v", 0), ("S", 0), ("S", 1), ("v", 1), ("S", 2), ("S", 3), ("Tp", 0), ("T", 1), ("O", 0),
        ("Tp", 2), ("O", 1), ("T", 3), ("O", 2), ("O", 3)]
LOOP = NB - 2


EARLY = (NB - 1) * NQ // 2
assert 2 * EARLY < UNITS


def trip_steps(i):
    if later(i, 1):
        skipped = PROJECT if isinstance(i, int) else ()
        return [step for step in ALPHA + BETA if step[0] not in skipped]
    steps = []
    for step in ALPHA + BETA:
        if step[0] not in PROJECT + MAXIMA:
            steps.append(step)
        if step[0] == "w" and 1 <= step[1] <= 2 * EARLY:
            steps.append(("rt" if step[1] % 2 else "lg", (step[1] - 1) // 2))
    return steps


def later(i, n):
    return not isinstance(i, int) or i + n < NB


def run_trips(eng, trip):
    with eng.Fori(0, LOOP) as i:
        trip(i)
    for i in range(LOOP, NB):
        trip(i)


G_KINDS = ("xT", "q", "v", "cT", "m", "mT", "ct", "cx", "o", "xa", "O", "rt", "lg")
R_KINDS = ("W", "kv", "A", "VW", "s", "S", "T")
P_KINDS = ("Tp",)


class Slots:

    def __init__(self, steps, kinds, banks, full, empty, start):
        self.steps, self.kinds = steps, kinds
        self.banks, self.full, self.empty, self.start = banks, full, empty, start

    def uses(self, i):
        return [step for step in self.steps(i) if step[0] in self.kinds]

    def at(self, i, kind, n):
        use, k = self.uses(i).index((kind, n)), len(self.banks)
        if isinstance(i, int):
            use += sum(len(self.uses(None if j < LOOP else j)) for j in range(i))
            return use % k, use // k + self.start
        assert len(self.uses(i)) % k == 0
        return use % k, i * (len(self.uses(i)) // k) + use // k + self.start


def flat(ap):
    return ap.rearrange("p a b -> p (a b)")


def positive(eng, sem, value):
    if not isinstance(value, int) or value > 0:
        eng.wait_ge(sem, value)


class Projection:

    def __init__(self, nc, k, g, hi_count, s):
        self.nc, self.k, self.g, self.hi_count, self.s = nc, k, g, hi_count, s

    def pe_x(self, pe, i, n, loaded):
        slot, value = self.g.at(i, "xT", n)
        pe.wait_ge(self.s["x_in"], loaded)
        positive(pe, self.g.empty[slot], value)
        c = n % 2
        for t in range(NQ):
            last = self.nc.tensor.transpose(self.g.banks[slot][:, t * 128:t * 128 + 128],
                                            self.k["x_tok"][:, t, c * 128:c * 128 + 128], self.k["ident"][:, :])
        last.then_inc(self.g.full[slot], 1)

    def pe_q(self, pe, i, n):
        if n % 4 == 0:
            for c in range(2):
                slot, value = self.g.at(i, "xT", n // 4 * 2 + c)
                pe.wait_ge(self.g.empty[slot], value + 1)
        slot, value = self.g.at(i, "q", n)
        pe.wait_ge(self.g.empty[slot], value)
        w, m, w_hl, xT = n % 4 // 2, n % 2, self.k["w_hl"], self.k["xT"]
        three(self.nc, self.g.banks[slot][:, :], lambda hl, c: w_hl[:, hl, w, c, m * 128:m * 128 + 128],
              lambda hl, c: xT[:, hl, c, :], DC).then_inc(self.g.full[slot], 1)

    def pe_v(self, pe, i, n):
        slot, value = self.g.at(i, "v", n)
        pe.wait_ge(self.g.empty[slot], value)
        w_hl, xT = self.k["w_hl"], self.k["xT"]
        for t in range(2):
            at = (2 * (n % 2) + t) * 128
            last = three(self.nc, self.g.banks[slot][:, t * D:t * D + D], lambda hl, c: xT[:, hl, c, at:at + 128],
                         lambda hl, c: w_hl[:, hl, 2, c, :], DC)
        last.then_inc(self.g.full[slot], 1)

    def act_x(self, act, i, n):
        slot, value = self.g.at(i, "xT", n)
        act.wait_ge(self.g.full[slot], value + 1)
        self.nc.scalar.activation(self.k["xT"][:, 0, n % 2, :], self.g.banks[slot][:, :], ACT.Copy,
                                  scale=XS).then_inc(self.s["hi_done"], 1)

    def act_q(self, act, i, n, before, stored):
        qf = self.k["qf"]
        slot, value = self.g.at(i, "q", n)
        if n % 4 == 0:
            positive(act, self.s["qk_stored"], stored)
        act.wait_ge(self.g.full[slot], value + 1)
        positive(act, self.s["qlo_done"], before + max(n - 1, 0))
        for out in (self.k["qk"][:, 0, n % 4, :], qf[:, n % 2, :]):
            last = self.nc.scalar.activation(out, self.g.banks[slot][:, :], ACT.Identity,
                                             bias=self.k["qk_bias"][:, n % 4 // 2, n % 2:n % 2 + 1],
                                             scale=QS / (WS * XS) * (HD ** -0.5 if n % 4 < 2 else 1.0))
        last.then_inc(self.g.empty[slot], 1)

    def act_v(self, act, i, n, copied):
        slot, value = self.g.at(i, "v", n)
        act.wait_ge(self.g.full[slot], value + 1)
        positive(act, self.s["v_copied"], copied)
        self.nc.scalar.activation(self.k["v_next"][:, 2 * (n % 2):2 * (n % 2) + 2, :], self.g.banks[slot][:, :]
                                  .rearrange("p (t d) -> p t d", t=2), ACT.Copy, scale=1.0 / (WS * XS)
                                  ).then_inc(self.g.empty[slot], 1)

    def dve_x(self, dve, i, n):
        slot, _ = self.g.at(i, "xT", n)
        xT = self.k["xT"]
        dve.wait_ge(self.s["hi_done"], self.hi_count(i, "xT", n))
        self.nc.vector.scalar_tensor_tensor(xT[:, 1, n % 2, :], self.g.banks[slot][:, :], XS, xT[:, 0, n % 2, :],
                                            ALU.mult, ALU.subtract).then_inc(self.g.empty[slot], 1)

    def pool_q(self, pool, i, n):
        qf, qk = self.k["qf"], self.k["qk"]
        slot, value = self.g.at(i, "q", n)
        pool.wait_ge(self.g.empty[slot], value + 1)
        self.nc.gpsimd.tensor_tensor(qk[:, 1, n % 4, :], qf[:, n % 2, :], qk[:, 0, n % 4, :],
                                     ALU.subtract).then_inc(self.s["qlo_done"], 1)

    def pool_v(self):
        for t in range(NQ):
            last = self.nc.gpsimd.tensor_tensor(
                self.k["v_aug"][:, t, :, 0:HD], self.k["v_next"][:, t, :].rearrange("p (h d) -> p h d", h=H),
                self.k["b_rows"][:, 1, :].rearrange("p (h d) -> p h d", h=H), ALU.add)
        last.then_inc(self.s["v_copied"], 1)

    def sp_store(self, sp, b):
        for hl in range(2):
            sp.dma_start(self.k["dram"]["qk"][bass.ds(b * 4 * D + hl * 2 * D, 2 * D), :]
                         .rearrange("(m p) s -> p m s", p=128), self.k["qk"][:, hl, :, :]
                         ).then_inc(self.s["qk_stored"], 16)

    def sp_stack(self, sp, b, qs, ks, done):
        rows = self.k["dram"]["qk"][bass.ds(b * 4 * D, 4 * D), :].rearrange(
            "(l t p r d) s -> l t r d p s", l=2, t=2, r=2, d=HD)
        for t, (dst, parts) in enumerate(((qs, (0, 0, 1)), (ks, (0, 1, 0)))):
            for par in range(2):
                for n, hl in enumerate(parts):
                    row = 64 * par + n * HD
                    sp.dma_start(dst[row:row + HD, :, :], rows[hl, t, par, :, :, :]).then_inc(done, 16)


def three(nc, out, left, right, n):
    for k in range(n):
        for m, (a, b) in enumerate(((0, 0), (0, 1), (1, 0))):
            last = nc.tensor.matmul(out, left(a, k), right(b, k), start=(k == 0 and m == 0),
                                    stop=(k == n - 1 and m == 2))
    return last


def score_maxima(nc, k, bank, item, qs, ks):
    t, par, p0, pairs = item
    rows, wide = slice(64 * par, 64 * par + ROWS), 128 * (t + 1)
    for n in range(pairs):
        nc.tensor.matmul(bank[:, n * wide:n * wide + wide], qs[rows, p0 + n, t * 128:t * 128 + 128],
                         ks[rows, p0 + n, 0:wide], start=True, stop=False)
        last = nc.tensor.matmul(bank[:, (n + 1) * wide - 128:(n + 1) * wide], k["ident16"][:, :], k["causal"][:, :],
                                start=False, stop=True)
    return last


def reduce_maxima(nc, k, bank, item):
    t, par, p0, pairs = item
    wide = 128 * (t + 1)
    return nc.vector.tensor_reduce(k["rowmax"][:, t, par * PAIRS + p0:par * PAIRS + p0 + pairs],
                                   bank[:, 0:pairs * wide].rearrange("p (n w) -> p n w", n=pairs), AX.X, ALU.max)


def prepare_block(nc, ctx, dram, keep):
    def sb(name, shape, dt=F32):
        return ctx.enter_context(nc.sbuf_tensor(name, shape, dt))

    def sem(name):
        return ctx.enter_context(nc.semaphore(name))

    ident, ident16, causal = keep["ident"], keep["ident16"], keep["causal"]
    w_hl, qk_bias, b_rows, power = keep["w_hl"], keep["qk_bias"], keep["b_rows"], keep["power"]
    w_f = sb("w_f", [128, 4, DC, D])
    wq_f = sb("wq_f", [128, DC, XA])
    wqT = sb("wqT", [128, 2, PAIRS, D], F16)
    wkv = sb("wkv", [128, 2, XA])
    wkv2 = sb("wkv2", [128, 2, XA])
    wout_f = sb("wout_f", [128, PAIRS, D])
    wout = sb("wout", [128, 2, PAIRS, D], F16)
    KT = NB * KV // 128
    cond = sb("cond", [128, KT, DCOND])
    wg, wg_f = keep["wg"], sb("wg_f", [128, DC, NE])
    cT = sb("cT", [128, 2, NB * KV])
    k_diag = sb("k_diag", [128, 2, PAIRS, 2, NB * KV], F16)
    v_diag = sb("v_diag", [128, 2, PAIRS, NB, 2, KV], F16)
    stage = sb("stage", [128, 4, 2, 1024], F16)
    stage_f = w_f[:, :, :, :].rearrange("p w c n -> p (w c n)").rearrange("p (t n) -> p t n", t=2)

    R = [ctx.enter_context(nc.psum_tensor(f"prR{i}", [128, 2, 512], F32)) for i in range(2)]
    G = [ctx.enter_context(nc.psum_tensor(f"prG{i}", [128, 512], F32)) for i in range(4)]
    r = Slots(lambda _: PREPARE, R_KINDS, R, [sem(f"pr_full{i}") for i in range(2)], [sem(f"pr_empty{i}") for i in range(2)], 0)
    g = Slots(lambda _: PREPARE, G_KINDS, G, [sem(f"pg_full{i}") for i in range(4)], [sem(f"pg_empty{i}") for i in range(4)], 0)
    HIS = [step for step in PREPARE if step[0] in ("xT", "W", "kv", "A", "VW")]

    def hi_count(i, kind, n):
        return HIS.index((kind, n)) + 1

    s = {name: sem("p_" + name) for name in ("x_in", "hi_done", "qlo_done", "qk_stored", "v_copied")}
    hi_done = s["hi_done"]
    w_in = [sem(f"w_in{i}") for i in range(2)]
    wkv_in = [sem(f"wkv_in{i}") for i in range(2)]
    b_in, r_in, c_in, wq_in, wo_in = sem("b_in"), sem("r_in"), sem("c_in"), sem("wq_in"), sem("wo_in")
    const_step, consts = sem("const_step"), sem("consts")
    w_hi, w_lo, wout_hi, wout_lo = sem("w_hi"), sem("w_lo"), sem("wout_hi"), sem("wout_lo")
    stack_set, pad_set, diag_set, a_lo = sem("stack_set"), sem("pad_set"), sem("diag_set"), sem("a_lo")
    wg_in, wg_hi, wg_lo = sem("wg_in"), sem("wg_hi"), sem("wg_lo")
    bias_done, stack_in, next_in = sem("bias_done"), sem("stack_in"), sem("next_in")
    m_stored, m_in, xr_in = sem("pm_stored"), sem("pm_in"), sem("pxr_in")
    staged = [sem(f"staged{i}") for i in range(4)]
    project = Projection(nc, keep, g, hi_count, s)
    PIECES = [step for step in PREPARE if step[0] in ("A", "VW")]

    def piece(row, par):
        return row.rearrange("p (b x r k) -> p r x b k", b=NB, r=2, x=2)[:, par, :, :, :]

    def diagonal(n, hl, par):
        rows, pairs = slice(64 * par, 64 * par + 64), slice(n % 2 * 4, n % 2 * 4 + 4)
        if n < 2:
            return rows, k_diag[rows, hl, pairs, par, :]
        return rows, v_diag[rows, hl, pairs, :, par, :].rearrange("p k b n -> p (k b) n")

    def diagonal_in(n, slot, rows):
        return flat(R[slot][rows, :, :]).rearrange("p (k n) -> p k n", n=NB * KV if n < 2 else KV)

    block = ctx.enter_context(nc.Block())

    @block.sync
    def _(sp):
        def tokens(b, dst, done):
            sp.dma_start(dst[:, :, :], dram["x"][b * S:b * S + S, :]
                         .rearrange("(t p) d -> p t d", p=128)).then_inc(done, 16)

        def store(pieces):
            for kind, m in pieces:
                n = PIECES.index((kind, m))
                if kind == "A":
                    sp.wait_ge(a_lo, m + 1)
                else:
                    slot, value = r.at(0, kind, m)
                    sp.wait_ge(r.empty[slot], value + 1)
                if kind == "A":
                    c, q = m // 4, m % 4
                    dst = dram["ax"].rearrange("(b p) (l c n) -> p l b c n", p=128, l=2, c=DC)[
                        :, :, :, c, q * 256:q * 256 + 256]
                    src = stage[:, n % 4, :, :].rearrange("p l (b n) -> p l b n", b=NB)
                else:
                    b, half = m // 2, m % 2
                    dst = dram["vw"][b * 128:b * 128 + 128, :].rearrange("p (l h n) -> p l h n", l=2, h=2)[
                        :, :, half:half + 1, :]
                    src = stage[:, n % 4, :, :].rearrange("p l (h n) -> p l h n", h=1)
                for hl in range(2):
                    sp.dma_start(dst[:, hl, :, :], src[:, hl, :, :]).then_inc(staged[n % 4], 16)

        tokens(0, keep["x_tok"], s["x_in"])
        for n, w in enumerate(("Wq", "Wk", "Wv", "Wo")):
            sp.dma_start(w_f[:, n, :, :], dram[w].rearrange("(c p) n -> p c n", p=128)).then_inc(w_in[n // 2], 16)
            if n == 1:
                sp.dma_start(qk_bias[:, 0, :], dram["bq"]).then_inc(b_in, 16)
                sp.dma_start(qk_bias[:, 1, :], dram["bk"]).then_inc(b_in, 16)
        sp.dma_start(cond[:, :, :], dram["cond"].rearrange("(t p) d -> p t d", p=128)).then_inc(c_in, 16)
        sp.dma_start(wq_f[:, :, :], dram["w_q"].rearrange("(c p) n -> p c n", p=128)).then_inc(wq_in, 16)
        for n, w in enumerate(("w_k", "w_v")):
            sp.dma_start(wkv[:, n, :], dram[w][0:128, :]).then_inc(wkv_in[n], 16)
            sp.dma_start(wkv2[0:DCOND - 128, n, :], dram[w][128:DCOND, :]).then_inc(wkv_in[n], 16)
        for n, b in enumerate(("bo", "bv", "b_out")):
            sp.dma_start(b_rows[:, n, :], dram[b].partition_broadcast(128)).then_inc(r_in, 16)
        sp.dma_start(wout_f[:, :, :], dram["w_out"].rearrange("(k p) n -> p k n", p=128)).then_inc(wo_in, 16)
        sp.dma_start(wg_f[:, :, :], dram["WgT"]).then_inc(wg_in, 16)
        tokens(0, keep["x_res"], xr_in)
        slot, value = g.at(0, "xT", 1)
        sp.wait_ge(g.full[slot], value + 1)
        tokens(1, keep["x_tok"], s["x_in"])
        sp.wait_ge(s["qlo_done"], 4)
        project.sp_store(sp, 0)
        sp.wait_ge(s["qk_stored"], 32)
        sp.wait_ge(stack_set, 4)
        project.sp_stack(sp, 0, keep["qs_e"], keep["ks_e"], stack_in)
        slot, value = g.at(0, "xT", 3)
        sp.wait_ge(g.full[slot], value + 1)
        tokens(2, keep["x_tok"], s["x_in"])
        sp.wait_ge(s["qlo_done"], 8)
        project.sp_store(sp, 1)
        sp.wait_ge(s["qk_stored"], 64)
        project.sp_stack(sp, 1, keep["qs_m"], keep["ks_m"], next_in)
        before = PREPARE.index(("mT", 1))
        store([step for step in PIECES if PREPARE.index(step) < before])
        for n in range(2):
            slot, value = g.at(0, "mT", n)
            sp.wait_ge(g.empty[slot], value + 1)
        sp.dma_start(dram["m"], keep["neg_maxT"][:, :]).then_inc(m_stored, 16)
        sp.wait_ge(m_stored, 16)
        for par in range(2):
            row = 64 * par + STACK
            sp.dma_start(keep["qs_e"][row:row + 1, :, :], dram["m"][par * PAIRS:(par + 1) * PAIRS, :]
                         .unsqueeze(0)).then_inc(m_in, 16)
        store([step for step in PIECES if PREPARE.index(step) > before])
        sp.wait_ge(next_in, 12 * 16)
        sp.wait_ge(m_in, 32)
        for n in range(4):
            sp.wait_ge(staged[n], len(PIECES) // 4 * 32)
        sp.wait_ge(wg_lo, 1)
        sp.wait_ge(s["x_in"], 48)
        sp.wait_ge(xr_in, 16)

    @block.gpsimd
    def _(pool):
        P = nc.gpsimd
        P.memset(ident[:, :], 0.0).then_inc(const_step, 1)
        P.memset(causal[:, :], 0.0).then_inc(const_step, 1)
        pool.wait_ge(const_step, 2)
        P.affine_select(out=ident[:, :], in_=ident[:, :], compare_op=ALU.not_equal, fill=1.0, base=0,
                        pattern=[[-1, 128]], channel_multiplier=1).then_inc(const_step, 1)
        P.affine_select(out=causal[:, :], in_=causal[:, :], compare_op=ALU.is_ge, fill=NEG, base=0,
                        pattern=[[-1, 128]], channel_multiplier=1).then_inc(const_step, 1)
        pool.wait_ge(const_step, 4)
        P.tensor_copy(ident16[:, :], ident[:, :]).then_inc(consts, 1)
        P.memset(keep["qs_e"][:, :, :], 0.0).then_inc(stack_set, 1)
        P.memset(keep["ks_e"][:, :, :], 1.0).then_inc(stack_set, 1)
        P.memset(keep["v_aug"][:, :, :, :], 1.0).then_inc(const_step, 1)
        P.memset(power[:, 0:NQ], EPS).then_inc(const_step, 1)
        P.memset(power[:, NQ:], -0.5).then_inc(const_step, 1)
        pool.wait_ge(const_step, 7)
        P.memset(keep["qs_m"][:, :, :], 0.0).then_inc(stack_set, 1)
        P.memset(keep["ks_m"][:, :, :], 1.0).then_inc(stack_set, 1)
        for n in range(4):
            project.pool_q(pool, 0, n)
        for n in range(2):
            slot, value = g.at(0, "v", n)
            pool.wait_ge(g.empty[slot], value + 1)
        pool.wait_ge(r_in, 3 * 16)
        project.pool_v()
        for n in range(4, 8):
            project.pool_q(pool, 0, n)
        for n in range(2 * NB):
            slot, value = r.at(0, "A", n)
            pool.wait_ge(r.empty[slot], value + 1)
            use = PIECES.index(("A", n))
            P.tensor_tensor(stage[:, use % 4, 1, :], stage_f[:, n % 2, :], stage[:, use % 4, 0, :],
                            ALU.subtract).then_inc(a_lo, 1)

    @block.scalar
    def _(act):
        A = nc.scalar
        def hi(out, bank, kind, n, scale):
            slot, value = r.at(0, kind, n)
            act.wait_ge(r.full[slot], value + 1)
            A.activation(out, bank(R[slot]), ACT.Copy, scale=scale).then_inc(hi_done, 1)

        for kind, n in PREPARE:
            if kind == "xT":
                project.act_x(act, 0, n)
                if n == 1:
                    for w in range(2):
                        act.wait_ge(w_in[w], 2 * 16)
                        A.activation(w_hl[:, 0, 2 * w:2 * w + 2, :, :].rearrange("p w c n -> p (w c n)"),
                                     w_f[:, 2 * w:2 * w + 2, :, :].rearrange("p w c n -> p (w c n)"), ACT.Copy,
                                     scale=WS).then_inc(w_hi, 1)
                    act.wait_ge(bias_done, 2)
            elif kind == "q":
                project.act_q(act, 0, n, 0, n // 4 * 32)
            elif kind == "v":
                project.act_v(act, 0, n, n // 2)
            elif kind == "cT":
                slot, value = g.at(0, kind, n)
                act.wait_ge(g.full[slot], value + 1)
                rows = 128 if n == 0 else DCOND - 128
                A.activation(cT[0:rows, n, :], G[slot][0:rows, 0:NB * KV], ACT.Copy).then_inc(g.empty[slot], 1)
            elif kind == "W":
                hi(wqT[:, 0, n * 4:n * 4 + 4, :].rearrange("p k n -> p (k n)"), lambda b: flat(b[:, :, :]), kind, n, WS)
            elif kind == "kv":
                slot, value = r.at(0, kind, n)
                act.wait_ge(diag_set, 4)
                act.wait_ge(r.full[slot], value + 1)
                for par in range(2):
                    rows, out = diagonal(n, 0, par)
                    last = A.activation(out, diagonal_in(n, slot, rows), ACT.Copy, scale=XS)
                last.then_inc(hi_done, 1)
                if n == 3:
                    act.wait_ge(wg_in, 16)
                    A.activation(wg[:, 0, :, :], wg_f[:, :, :], ACT.Copy, scale=WS).then_inc(wg_hi, 1)
                if n == 1:
                    act.wait_ge(wo_in, 16)
                    A.activation(wout[:, 0, :, :].rearrange("p k n -> p (k n)"), flat(wout_f[:, :, :]), ACT.Copy,
                                 scale=WS).then_inc(wout_hi, 1)
            elif kind in ("A", "VW"):
                use = PIECES.index((kind, n))
                if use >= 4:
                    act.wait_ge(staged[use % 4], use // 4 * 32)
                slot, value = r.at(0, kind, n)
                act.wait_ge(r.full[slot], value + 1)
                if kind == "A":
                    positive(act, a_lo, n - 1)
                    for out, done in ((stage[:, use % 4, 0, :], hi_done), (stage_f[:, n % 2, :], r.empty[slot])):
                        for par in range(2):
                            last = A.activation(piece(out, par), R[slot][:, par, :]
                                                .rearrange("p (x b k) -> p x b k", x=2, b=NB), ACT.Copy, scale=1.0 / XS)
                        last.then_inc(done, 1)
                else:
                    A.activation(stage[:, use % 4, 0, :], flat(R[slot][:, :, :]), ACT.Copy,
                                 scale=1.0 / XS).then_inc(hi_done, 1)
            elif kind == "mT":
                slot, value = g.at(0, kind, n)
                act.wait_ge(g.full[slot], value + 1)
                A.activation(keep["neg_maxT"][:, n * 256:n * 256 + 256], G[slot][0:H, 0:256], ACT.Copy, scale=-1.0
                             ).then_inc(g.empty[slot], 1)

    @block.vector
    def _(dve):
        V = nc.vector
        V.memset(cT[DCOND - 128:, 1, :], 0.0).then_inc(pad_set, 1)
        V.memset(wkv2[DCOND - 128:, :, :], 0.0).then_inc(pad_set, 1)
        for hl in range(2):
            V.memset(v_diag[:, hl, :, :, :, :].rearrange("p k b r n -> p (k b r n)"), 0.0).then_inc(diag_set, 1)
        dve.wait_ge(b_in, 2 * 16)
        V.tensor_scalar(qk_bias[:, 0, :], qk_bias[:, 0, :], QS * HD ** -0.5, None, ALU.mult).then_inc(bias_done, 1)
        V.tensor_scalar(qk_bias[:, 1, :], qk_bias[:, 1, :], QS, None, ALU.mult).then_inc(bias_done, 1)

        def lo(out, bank, high, kind, n, scale):
            slot, _ = r.at(0, kind, n)
            dve.wait_ge(hi_done, hi_count(0, kind, n))
            V.scalar_tensor_tensor(out, bank(R[slot]), scale, high, ALU.mult, ALU.subtract).then_inc(r.empty[slot], 1)

        for kind, n in PREPARE:
            if kind == "xT":
                project.dve_x(dve, 0, n)
                if n == 1:
                    for w in range(2):
                        part = slice(2 * w, 2 * w + 2)
                        dve.wait_ge(w_hi, w + 1)
                        V.scalar_tensor_tensor(w_hl[:, 1, part, :, :].rearrange("p w c n -> p (w c n)"),
                                               w_f[:, part, :, :].rearrange("p w c n -> p (w c n)"), WS,
                                               w_hl[:, 0, part, :, :].rearrange("p w c n -> p (w c n)"),
                                               ALU.mult, ALU.subtract).then_inc(w_lo, 1)
            elif kind == "q":
                if n == 1:
                    for hl in range(2):
                        V.memset(k_diag[:, hl, :, :, :].rearrange("p k r n -> p (k r n)"), 0.0).then_inc(diag_set, 1)
            elif kind == "W":
                lo(wqT[:, 1, n * 4:n * 4 + 4, :].rearrange("p k n -> p (k n)"), lambda b: flat(b[:, :, :]),
                   wqT[:, 0, n * 4:n * 4 + 4, :].rearrange("p k n -> p (k n)"), kind, n, WS)
            elif kind == "kv":
                slot, _ = r.at(0, kind, n)
                dve.wait_ge(hi_done, hi_count(0, kind, n))
                for par in range(2):
                    rows, out = diagonal(n, 1, par)
                    last = V.scalar_tensor_tensor(out, diagonal_in(n, slot, rows), XS, diagonal(n, 0, par)[1],
                                                  ALU.mult, ALU.subtract)
                last.then_inc(r.empty[slot], 1)
                if n == 3:
                    dve.wait_ge(wg_hi, 1)
                    V.scalar_tensor_tensor(wg[:, 1, :, :], wg_f[:, :, :], WS, wg[:, 0, :, :], ALU.mult,
                                           ALU.subtract).then_inc(wg_lo, 1)
                if n == 1:
                    dve.wait_ge(wout_hi, 1)
                    V.scalar_tensor_tensor(wout[:, 1, :, :].rearrange("p k n -> p (k n)"), flat(wout_f[:, :, :]), WS,
                                           wout[:, 0, :, :].rearrange("p k n -> p (k n)"),
                                           ALU.mult, ALU.subtract).then_inc(wout_lo, 1)
            elif kind == "VW":
                use = PIECES.index((kind, n))
                lo(stage[:, use % 4, 1, :], lambda b: flat(b[:, :, :]), stage[:, use % 4, 0, :], kind, n, 1.0 / XS)
            elif kind == "m":
                slot, value = g.at(0, kind, n)
                dve.wait_ge(g.full[slot], value + 1)
                reduce_maxima(nc, keep, G[slot], MAXES[n]).then_inc(g.empty[slot], 1)

    @block.tensor
    def _(pe):
        M = nc.tensor

        def opened(slots, kind, n):
            slot, value = slots.at(0, kind, n)
            positive(pe, slots.empty[slot], value)
            return slots.banks[slot], slots.full[slot]

        def read(slots, kind, n):
            slot, value = slots.at(0, kind, n)
            pe.wait_ge(slots.empty[slot], value + 1)

        pe.wait_ge(consts, 1)
        for kind, n in PREPARE:
            if kind == "xT":
                project.pe_x(pe, 0, n, n // 2 * 16 + 16)
            elif kind == "q":
                if n == 0:
                    pe.wait_ge(w_lo, 1)
                project.pe_q(pe, 0, n)
            elif kind == "v":
                if n == 0:
                    pe.wait_ge(w_lo, 2)
                project.pe_v(pe, 0, n)
            elif kind == "cT":
                pe.wait_ge(c_in, 16)
                bank, full = opened(g, kind, n)
                rows = 128 if n == 0 else DCOND - 128
                for t in range(KT):
                    last = M.transpose(bank[0:rows, t * 128:t * 128 + 128], cond[:, t, n * 128:n * 128 + rows],
                                       ident[:, :])
                last.then_inc(full, 1)
            elif kind == "W":
                pe.wait_ge(wq_in, 16)
                bank, full = opened(r, kind, n)
                for k in range(4):
                    for c in range(DC):
                        at = k * D + c * 128
                        last = M.transpose(flat(bank[:, :, :])[:, at:at + 128],
                                           wq_f[:, c, (4 * n + k) * 128:(4 * n + k) * 128 + 128], ident[:, :])
                last.then_inc(full, 1)
            elif kind in ("kv", "kv+"):
                n, k = (n, 3) if kind == "kv" else (n // 4, n % 4)
                if k == 0:
                    pe.wait_ge(wkv_in[n // 2], 2 * 16)
                    if n == 0:
                        read(g, "cT", 0)
                        read(g, "cT", 1)
                        pe.wait_ge(pad_set, 2)
                    opened(r, "kv", n)
                p, slot = n % 2 * 4 + k, r.at(0, "kv", n)[0]
                out = flat(R[slot][:, :, :])[:, k * NB * KV:(k + 1) * NB * KV]
                M.matmul(out, wkv[:, n // 2, p * 128:p * 128 + 128], cT[:, 0, :], start=True, stop=False)
                last = M.matmul(out, wkv2[:, n // 2, p * 128:p * 128 + 128], cT[:, 1, :],
                                start=False, stop=True)
                if k == 3:
                    last.then_inc(r.full[slot], 1)
            elif kind in ("A", "A+"):
                n, k = (n, 3) if kind == "A" else (n // 4, n % 4)
                if n == 0 and k == 0:
                    for m in range(2):
                        read(r, "W", m)
                        read(r, "kv", m)
                if k == 0:
                    opened(r, "A", n)
                c, q, x, par = n // 4, n % 4, k // 2, k % 2
                p = 2 * q + x
                last = three(nc, R[r.at(0, "A", n)[0]][:, par, x * NB * KV:(x + 1) * NB * KV],
                             lambda hl, _: wqT[:, hl, p, c * 128:c * 128 + 128],
                             lambda hl, _: k_diag[:, hl, p, par, :], 1)
                if k == 3:
                    last.then_inc(r.full[r.at(0, "A", n)[0]], 1)
            elif kind in ("VW", "VW+"):
                n, k = (n, 3) if kind == "VW" else (n // 4, n % 4)
                if n == 0 and k == 0:
                    for m in range(2, 4):
                        read(r, "kv", m)
                    pe.wait_ge(wout_lo, 1)
                if k == 0:
                    opened(r, "VW", n)
                b, p = n // 2, n % 2 * 4 + k
                last = three(nc, flat(R[r.at(0, "VW", n)[0]][:, :, :])[:, k * D:k * D + D],
                             lambda hl, _: v_diag[:, hl, p, b, :, :].rearrange("p r n -> p (r n)"),
                             lambda hl, _: wout[:, hl, p, :], 1)
                if k == 3:
                    last.then_inc(r.full[r.at(0, "VW", n)[0]], 1)
            elif kind == "m":
                if n == 0:
                    pe.wait_ge(stack_in, 12 * 16)
                bank, full = opened(g, kind, n)
                score_maxima(nc, keep, bank, MAXES[n], keep["qs_e"], keep["ks_e"]).then_inc(full, 1)
            elif kind == "mT":
                if n == 0:
                    for m in range(len(MAXES) - 4, len(MAXES)):
                        read(g, "m", m)
                bank, full = opened(g, kind, n)
                for t in range(2):
                    last = M.transpose(bank[0:H, t * 128:t * 128 + 128], keep["rowmax"][:, 2 * n + t, :], ident[:, :])
                last.then_inc(full, 1)


def attention_block(nc, ctx, dram, keep):
    START = 1

    def sb(name, shape, dt=F32):
        return ctx.enter_context(nc.sbuf_tensor(name, shape, dt))

    def sem(name):
        return ctx.enter_context(nc.semaphore(name))

    ident, w_hl, b_rows, power = keep["ident"], keep["w_hl"], keep["b_rows"], keep["power"]
    x2_all, x_res, v_aug = keep["x2_all"], keep["x_res"], keep["v_aug"]
    qs_e, ks_e, qs_m, ks_m = keep["qs_e"], keep["ks_e"], keep["qs_m"], keep["ks_m"]
    probs = sb("probs", [128, 4, 2, S])
    cu = sb("cu", [128, 2, S])
    inv = sb("inv", [128, GROUPS, NQ, 4])
    ctx_tok = sb("ctx_tok", [128, NQ, D])
    ctxT = sb("ctxT", [128, 2, DC, S], F16)
    x1 = sb("x1", [128, NQ, D])
    x1_b = sb("x1_b", [128, NQ, D])
    x1T = sb("x1T", [128, 2, DC, S], F16)
    x2 = sb("x2", [128, NQ, D])
    stats = sb("stats", [128, 2 * NQ, 6])
    meanvar = sb("meanvar", [128, 2 * NQ, 2])
    rstd = sb("rstd", [128, 2 * NQ])
    e_x = sb("e_x", [128, NQ, XA])
    xmax = sb("xmax", [128, NQ, XH])
    xsum = sb("xsum", [128, NQ, XH])
    xinv = sb("xinv", [128, NQ, XH])
    pT = sb("pT", [128, 2, 2, PAIRS, 128], F16)
    a_x = sb("a_x", [128, 2, DC, XA], F16)
    vw = sb("vw", [128, 2, PAIRS, D], F16)

    R = [ctx.enter_context(nc.psum_tensor(f"R{i}", [128, 2, 512], F32)) for i in range(2)]
    PV = ctx.enter_context(nc.psum_tensor("PV", [128, 2, 512], F32))
    G = [ctx.enter_context(nc.psum_tensor(f"G{i}", [128, 512], F32)) for i in range(2)]
    r = Slots(trip_steps, R_KINDS, R, [sem(f"r_full{i}") for i in range(2)], [sem(f"r_empty{i}") for i in range(2)],
              START)
    g = Slots(trip_steps, G_KINDS, G, [sem(f"g_full{i}") for i in range(2)], [sem(f"g_empty{i}") for i in range(2)],
              START)
    pt = Slots(trip_steps, P_KINDS, [PV], [sem("pt_full")], [sem("pt_empty")], START)
    pv_empty = [sem(f"pv_empty{i}") for i in range(2)]

    def turned(t):
        return (pt, "Tp") if t % 2 == 0 else (r, "T")

    HIS = [("cx", 0), ("xT", 0), ("cx", 1), ("xT", 1), ("xa", 0), ("xa", 1), ("Tp", 0), ("T", 1), ("Tp", 2), ("T", 3)]

    def hi_count(i, kind, n):
        if not isinstance(i, int):
            return i * len(HIS) + HIS.index((kind, n)) + 1
        here = [step for step in HIS if step[0] not in PROJECT]
        return LOOP * len(HIS) + (i - LOOP) * len(here) + here.index((kind, n)) + 1

    s = {name: sem(name) for name in ("x_in", "hi_done", "qlo_done", "qk_stored", "v_copied")}
    hi_done, x_in, v_copied, qk_stored, qlo_done = (s["hi_done"], s["x_in"], s["v_copied"], s["qk_stored"],
                                                    s["qlo_done"])
    ax_in, vw_in, xr_in = sem("ax_in"), sem("vw_in"), sem("xr_in")
    stack_e, stack_m, m_stored = sem("stack_e"), sem("stack_m"), sem("m_stored")
    probs_ready, probs_used, exp_seen = sem("probs_ready"), sem("probs_used"), sem("exp_seen")
    stats_seen = sem("stats_seen")
    xb_done, x1b_done, x1_ready, x2_ready = sem("xb_done"), sem("x1b_done"), sem("x1_ready"), sem("x2_ready")
    var_done, rstd_done, pool_step, dve_step = sem("var_done"), sem("rstd_done"), sem("pool_step"), sem("dve_step")
    e_exp, e_inv, e_prob = sem("e_exp"), sem("e_inv"), sem("e_prob")
    xmax_done, x_shifted = sem("xmax_done"), sem("x_shifted")
    project = Projection(nc, keep, g, hi_count, s)
    SCORES = 2 * UNITS

    block = ctx.enter_context(nc.Block())

    @block.sync
    def _(sp):
        for free in (g.full[0], g.full[1], g.empty[0], g.empty[1], r.full[0], r.full[1], r.empty[0], r.empty[1],
                     pt.full[0], pt.empty[0],
                     pv_empty[0], pv_empty[1], probs_used, stack_e, stack_m, qk_stored, qlo_done, m_stored, x2_ready,
                     x_in, xr_in, v_copied):
            sp.sem_inc(free, START)

        def load_ax(b):
            sp.dma_start(a_x[:, :, :, :].rearrange("p l c n -> p (l c n)"),
                         dram["ax"][bass.ds(b * 128, 128), :]).then_inc(ax_in, 16)

        def load_vw(b):
            sp.dma_start(vw[:, :, :, :].rearrange("p l k n -> p (l k n)"),
                         dram["vw"][bass.ds(b * 128, 128), :]).then_inc(vw_in, 16)

        load_ax(0)
        load_vw(0)

        def trip(i):
            if not later(i, 1):
                return
            slot, value = g.at(i, "mT", 1)
            sp.wait_ge(g.empty[slot], value + 1)
            sp.dma_start(dram["m"], keep["neg_maxT"][:, :]).then_inc(m_stored, 16)
            sp.wait_ge(probs_used, i * UNITS + UNITS + START)
            project.sp_stack(sp, i + 1, qs_e, ks_e, stack_e)
            sp.wait_ge(m_stored, i * 16 + 16 + START)
            for par in range(2):
                row = 64 * par + STACK
                sp.dma_start(qs_e[row:row + 1, :, :], dram["m"][par * PAIRS:(par + 1) * PAIRS, :]
                             .unsqueeze(0)).then_inc(stack_e, 16)
            if later(i, 2):
                slot, value = g.at(i, "xT", 1)
                sp.wait_ge(g.full[slot], value + 1)
                sp.dma_start(keep["x_tok"][:, :, :], dram["x"][bass.ds((i + 3) % NB * S, S), :]
                             .rearrange("(t p) d -> p t d", p=128)).then_inc(x_in, 16)
            slot, value = g.at(i, "o", 1)
            sp.wait_ge(g.empty[slot], value + 1)
            sp.dma_start(x_res[:, :, :], dram["x"][bass.ds((i + 1) * S, S), :]
                         .rearrange("(t p) d -> p t d", p=128)).then_inc(xr_in, 16)
            if later(i, 2):
                sp.wait_ge(qlo_done, i * 4 + 4 + START)
                project.sp_store(sp, i + 2)
                sp.wait_ge(qk_stored, i * 32 + 32 + START)
                project.sp_stack(sp, i + 2, qs_m, ks_m, stack_m)
            slot, value = r.at(i, "S", 3)
            sp.wait_ge(r.full[slot], value + 1)
            load_ax(i + 1)
            slot, value = g.at(i, "O", 3)
            sp.wait_ge(g.full[slot], value + 1)
            load_vw(i + 1)

        run_trips(nc.sync, trip)
        for done, count in ((x_in, LOOP * 16 + START), (xr_in, (NB - 1) * 16 + START),
                            (stack_m, LOOP * 12 * 16 + START), (stack_e, (NB - 1) * 14 * 16 + START),
                            (ax_in, NB * 16), (vw_in, NB * 16)):
            sp.wait_ge(done, count)

    @block.gpsimd
    def _(pool):
        P = nc.gpsimd

        def root(i, n):
            pool.wait_ge(var_done, i * 4 + n + 1)
            P.tensor_tensor(rstd[:, 2 * n:2 * n + 2], meanvar[:, 2 * n:2 * n + 2, 1], power[:, 0:2],
                            ALU.add).then_inc(pool_step, 1)
            pool.wait_ge(pool_step, i * 4 + n + 1)
            P.tensor_tensor(rstd[:, 2 * n:2 * n + 2], rstd[:, 2 * n:2 * n + 2], power[:, NQ:NQ + 2],
                            ALU.pow).then_inc(rstd_done, 1)

        def trip(i):
            for n in range(SCORES):
                slot, value = r.at(i, "s", n)
                pool.wait_ge(r.empty[slot], value + 1)
                pool.sem_inc(exp_seen, 1)
                diag = probs[:, n % 4, :, 0:128]
                P.affine_select(out=diag, in_=diag, compare_op=ALU.is_ge, fill=0.0, base=0,
                                pattern=[[0, 2], [1, 128]], channel_multiplier=-1).then_inc(probs_ready, 1)
                if n == SCORES // 2:
                    pool.wait_ge(xr_in, i * 16 + START)
                    P.tensor_tensor(x_res[:, :, :], x_res[:, :, :],
                                    b_rows[:, 0:1, :].to_broadcast([128, NQ, D]), ALU.add).then_inc(xb_done, 1)
            if later(i, 1):
                pool.wait_ge(probs_used, i * UNITS + UNITS + START)
                pool.sem_inc(exp_seen, 1)
                project.pool_v()
            root(i, 0)
            root(i, 1)
            if later(i, 2):
                for n in range(4):
                    project.pool_q(pool, i, n)
            pool.wait_ge(x1_ready, i * 2 + 2)
            P.tensor_tensor(x1_b[:, :, :], x1[:, :, :],
                            b_rows[:, 2:3, :].to_broadcast([128, NQ, D]), ALU.add).then_inc(x1b_done, 1)
            for t in range(NQ):
                if t == 2:
                    pool.wait_ge(xmax_done, i + 1)
                    P.tensor_tensor(e_x[:, NQ - 1, :].rearrange("p (h k) -> p h k", h=XH),
                                    e_x[:, NQ - 1, :].rearrange("p (h k) -> p h k", h=XH),
                                    xmax[:, NQ - 1, :].unsqueeze(2).to_broadcast([128, XH, KV]),
                                    ALU.subtract).then_inc(x_shifted, 1)
                pool.wait_ge(e_inv, i * NQ + t + 1)
                e3 = e_x[:, t, :].rearrange("p (h k) -> p h k", h=XH)
                P.tensor_tensor(e3, e3, xinv[:, t, :].unsqueeze(2).to_broadcast([128, XH, KV]),
                                ALU.mult).then_inc(e_prob, 1)
            root(i, 2)
            root(i, 3)

        run_trips(nc.gpsimd, trip)

    @block.scalar
    def _(act):
        A = nc.scalar

        def hi(i, kind, n, out, slots, bank, scale):
            slot, value = slots.at(i, kind, n)
            act.wait_ge(slots.full[slot], value + 1)
            A.activation(out, bank(slots.banks[slot]), ACT.Copy, scale=scale).then_inc(hi_done, 1)

        def trip(i):
            def pv_out(gr):
                act.wait_ge(probs_used, i * UNITS + NQ * (gr + 1) + START)
                A.activation(cu[:, gr % 2, :], PV[:, gr % 2, :], ACT.Copy).then_inc(pv_empty[gr % 2], 1)

            for n in range(SCORES):
                u = n // 2
                gr, j = u // NQ, u % NQ
                slot, value = r.at(i, "s", n)
                act.wait_ge(r.full[slot], value + 1)
                act.wait_ge(probs_used, i * UNITS + max(u - 1, 0) + START)
                A.activation(probs[:, n % 4, :, 0:S - 128 * j], R[slot][:, :, 0:S - 128 * j], ACT.Exp,
                             scale=1.0 / (QS * QS)).then_inc(r.empty[slot], 1)
                if j == 0 and n % 2 == 1 and gr > 0:
                    pv_out(gr - 1)
            hi(i, "cx", 0, ctxT[:, 0, 0, :], g, lambda b: b[:, :], XS)
            pv_out(GROUPS - 1)
            if later(i, 1):
                act.wait_ge(m_stored, i * 16 + START)
                for n in range(2):
                    slot, value = g.at(i, "mT", n)
                    act.wait_ge(g.full[slot], value + 1)
                    A.activation(keep["neg_maxT"][:, n * 256:n * 256 + 256], G[slot][0:H, 0:256], ACT.Copy,
                                 scale=-1.0).then_inc(g.empty[slot], 1)
            if later(i, 2):
                project.act_x(act, i, 0)
            hi(i, "cx", 1, ctxT[:, 0, 1, :], g, lambda b: b[:, :], XS)
            if later(i, 2):
                project.act_x(act, i, 1)
                for n in range(4):
                    project.act_q(act, i, n, i * 4 + START, i * 32 + START)
            for c in range(DC):
                hi(i, "xa", c, x1T[:, 0, c, :], g, lambda b: b[:, :], XS)

            def x_copy(t):
                slot, value = r.at(i, "S", t)
                act.wait_ge(r.full[slot], value + 1)
                A.activation(e_x[:, t, :], flat(R[slot][:, :, :]), ACT.Copy).then_inc(r.empty[slot], 1)

            def x_exp(t):
                slot, value = r.at(i, "S", t)
                if t == NQ - 1:
                    act.wait_ge(x_shifted, i + 1)
                else:
                    act.wait_ge(r.empty[slot], value + 1)
                A.activation(e_x[:, t, :], e_x[:, t, :], ACT.Exp,
                             scale=XD ** -0.5 / (WS * XS)).then_inc(e_exp, 1)

            def p_hi(t):
                slots, kind = turned(t)
                hi(i, kind, t, pT[:, t % 2, 0, :, :].rearrange("p k q -> p (k q)"), slots, lambda b: flat(b[:, :, :]), WS)

            if later(i, 2):
                project.act_v(act, i, 0, i + 1 + START)
            x_exp(0)
            if later(i, 2):
                project.act_v(act, i, 1, i + 1 + START)
            x_exp(1)
            x_copy(3)
            p_hi(0)
            x_exp(2)
            x_exp(3)
            p_hi(1)
            p_hi(2)
            p_hi(3)

        run_trips(nc.scalar, trip)

    @block.vector
    def _(dve):
        V = nc.vector
        STEPS_DVE = GROUPS + 4 + 2 * NQ - 1

        def trip(i):
            count = [0]

            def after(ins):
                count[0] += 1
                ins.then_inc(dve_step, 1)
                dve.wait_ge(dve_step, i * STEPS_DVE + count[0])

            def lo(kind, n, out, slots, bank, high, scale):
                slot, _ = slots.at(i, kind, n)
                dve.wait_ge(hi_done, hi_count(i, kind, n))
                V.scalar_tensor_tensor(out, bank(slots.banks[slot]), scale, high, ALU.mult, ALU.subtract
                                       ).then_inc(slots.empty[slot], 1)

            def normalize(gr):
                slot, value = g.at(i, "ct", gr)
                dve.wait_ge(g.full[slot], value + 1)
                bank = G[slot][:, :].rearrange("p (t h d) -> p t h d", t=NQ, h=4)
                after(V.reciprocal(inv[:, gr, :, :], bank[:, :, :, HD]))
                V.tensor_tensor(ctx_tok[:, :, gr * 64:gr * 64 + 64].rearrange("p t (h d) -> p t h d", h=4),
                                bank[:, :, :, 0:HD], inv[:, gr, :, :].unsqueeze(3).to_broadcast([128, NQ, 4, HD]),
                                ALU.mult).then_inc(g.empty[slot], 1)

            def moments(n, buf):
                tiles = range(n % 2 * 2, n % 2 * 2 + 2)
                for t in tiles:
                    last = V.bn_stats(stats[:, n // 2 * NQ + t, :], buf[:, t, :])
                after(last)
                dve.sem_inc(stats_seen, 1)
                for t in tiles:
                    last = V.bn_aggr(meanvar[:, n // 2 * NQ + t, :], stats[:, n // 2 * NQ + t, :])
                last.then_inc(var_done, 1)

            def scaled(n, out, buf, done):
                dve.wait_ge(rstd_done, i * 4 + n + 1)
                for t in range(n % 2 * 2, n % 2 * 2 + 2):
                    at = n // 2 * NQ + t
                    dst = out[:, t:t + 1, :] if out is buf else out[:, bass.ds(i * NQ + t, 1), :]
                    last = V.tensor_scalar(dst, buf[:, t:t + 1, :], meanvar[:, at, 0:1], rstd[:, at:at + 1],
                                           ALU.subtract, ALU.mult)
                last.then_inc(done, 1)

            for kind, n in trip_steps(i):
                if kind == "m":
                    slot, value = g.at(i, kind, n)
                    dve.wait_ge(g.full[slot], value + 1)
                    reduce_maxima(nc, keep, G[slot], MAXES[n]).then_inc(g.empty[slot], 1)
                elif kind == "ct":
                    normalize(n)
                elif kind == "cx":
                    lo("cx", n, ctxT[:, 1, n, :], g, lambda b: b[:, :], ctxT[:, 0, n, :], XS)
                elif kind == "xT":
                    project.dve_x(dve, i, n)
                elif kind == "rt":
                    slot, value = g.at(i, kind, n)
                    dve.wait_ge(g.full[slot], value + 1)
                    high, low = (keep["xT"][:, hl, :, n % 2 * 256:n % 2 * 256 + 256] for hl in range(2))
                    bank = G[slot][:, :].rearrange("p (c q) -> p c q", c=DC)
                    after(V.tensor_scalar(high, bank, XS, None, ALU.mult))
                    V.scalar_tensor_tensor(low, bank, XS, high, ALU.mult, ALU.subtract).then_inc(g.empty[slot], 1)
                elif kind == "lg":
                    slot, value = g.at(i, kind, n)
                    dve.wait_ge(g.full[slot], value + 1)
                    V.tensor_scalar(keep["logits"][:, n * 2 * NE:(n + 1) * 2 * NE], G[slot][:, 0:2 * NE],
                                    1.0 / (WS * XS), None, ALU.mult).then_inc(g.empty[slot], 1)
            dve.wait_ge(xb_done, i + 1)
            for n in range(2):
                slot, value = g.at(i, "o", n)
                dve.wait_ge(g.full[slot], value + 1)
                V.scalar_tensor_tensor(x1[:, 2 * n:2 * n + 2, :],
                                       G[slot][:, :].rearrange("p (t d) -> p t d", t=2), 1.0 / (WS * XS),
                                       x_res[:, 2 * n:2 * n + 2, :], ALU.mult, ALU.add).then_inc(g.empty[slot], 1)
                dve.wait_ge(g.empty[slot], value + 1)
                moments(n, x1)
            for n in range(2):
                scaled(n, x1, x1, x1_ready)
            for c in range(DC):
                lo("xa", c, x1T[:, 1, c, :], g, lambda b: b[:, :], x1T[:, 0, c, :], XS)

            def x_shift(t):
                slot, value = r.at(i, "S", t)
                dve.wait_ge(r.full[slot], value + 1)
                s3 = flat(R[slot][:, :, :]).rearrange("p (h k) -> p h k", h=XH)
                after(V.tensor_reduce(xmax[:, t, :], s3, AX.X, ALU.max))
                V.tensor_tensor(e_x[:, t, :].rearrange("p (h k) -> p h k", h=XH), s3,
                                xmax[:, t, :].unsqueeze(2).to_broadcast([128, XH, KV]),
                                ALU.subtract).then_inc(r.empty[slot], 1)

            def x_max(t):
                slot, value = r.at(i, "S", t)
                dve.wait_ge(r.empty[slot], value + 1)
                V.tensor_reduce(xmax[:, t, :], e_x[:, t, :].rearrange("p (h k) -> p h k", h=XH), AX.X,
                                ALU.max).then_inc(xmax_done, 1)

            def x_sum(t):
                dve.wait_ge(e_exp, i * NQ + t + 1)
                after(V.tensor_reduce(xsum[:, t, :], e_x[:, t, :].rearrange("p (h k) -> p h k", h=XH),
                                      AX.X, ALU.add))
                V.reciprocal(xinv[:, t, :], xsum[:, t, :]).then_inc(e_inv, 1)

            def p_lo(t):
                high = pT[:, t % 2, 0, :, :].rearrange("p k q -> p (k q)")
                slots, kind = turned(t)
                lo(kind, t, pT[:, t % 2, 1, :, :].rearrange("p k q -> p (k q)"), slots, lambda b: flat(b[:, :, :]), high, WS)

            def x_out(t):
                slot, value = g.at(i, "O", t)
                dve.wait_ge(g.full[slot], value + 1)
                V.scalar_tensor_tensor(x2[:, t, :], G[slot][:, 0:D], 1.0 / (WS * WS), x1_b[:, t, :],
                                       ALU.mult, ALU.add).then_inc(g.empty[slot], 1)
                if t % 2 == 1:
                    dve.wait_ge(g.empty[slot], value + 1)

            x_shift(0)
            x_shift(1)
            x_sum(0)
            x_sum(1)
            x_shift(2)
            x_max(3)
            p_lo(0)
            x_sum(2)
            p_lo(1)
            x_sum(3)
            dve.wait_ge(x2_ready, i * 2 + START)
            dve.wait_ge(x1b_done, i + 1)
            x_out(0)
            p_lo(2)
            x_out(1)
            moments(2, x2)
            p_lo(3)
            scaled(2, x2_all, x2, x2_ready)
            x_out(2)
            x_out(3)
            moments(3, x2)
            scaled(3, x2_all, x2, x2_ready)
            assert count[0] == STEPS_DVE + (0 if later(i, 1) else EARLY), count

        run_trips(nc.vector, trip)

    @block.tensor
    def _(pe):
        M = nc.tensor

        def trip(i):
            def opened(slots, kind, n):
                slot, value = slots.at(i, kind, n)
                pe.wait_ge(slots.empty[slot], value)
                return slots.banks[slot], slots.full[slot]

            def read(slots, kind, n):
                slot, value = slots.at(i, kind, n)
                pe.wait_ge(slots.empty[slot], value + 1)

            def transposed(kind, c, src):
                bank, full = opened(g, kind, c)
                for t in range(NQ):
                    last = M.transpose(bank[:, t * 128:t * 128 + 128], src[:, t, c * 128:c * 128 + 128], ident[:, :])
                last.then_inc(full, 1)

            def score(n):
                gr, j, k = n // 2 // NQ, n // 2 % NQ, n % 2
                bank, full = opened(r, "s", n)
                p = 2 * gr + k
                for par in range(2):
                    rows = slice(64 * par, 64 * par + ROWS)
                    last = M.matmul(bank[:, par, 0:S - 128 * j], ks_e[rows, p, 128 * j:128 * j + 128],
                                    qs_e[rows, p, 128 * j:S], start=True, stop=True)
                last.then_inc(full, 1)

            def weigh(u):
                gr, j = u // NQ, u % NQ
                if j == 0:
                    pe.wait_ge(pv_empty[gr % 2], i * 2 + gr // 2 + START)
                pe.wait_ge(probs_ready, i * SCORES + 2 * u + 2)
                for hd in range(4):
                    last = M.matmul(PV[32 * hd:32 * hd + 32, gr % 2, 128 * j:S], v_aug[:, j, 4 * gr + hd, :],
                                    probs[:, (2 * u + hd // 2) % 4, hd % 2, 0:S - 128 * j],
                                    start=(j == 0), stop=(j == NQ - 1))
                last.then_inc(probs_used, 1)

            def tokens(gr):
                pe.wait_ge(pv_empty[gr % 2], i * 2 + gr // 2 + 1 + START)
                bank, full = opened(g, "ct", gr)
                for t in range(NQ):
                    last = M.transpose(bank[:, t * 128:t * 128 + 128], cu[:, gr % 2, t * 128:t * 128 + 128], ident[:, :])
                last.then_inc(full, 1)

            pe.wait_ge(v_copied, i + START)
            pe.wait_ge(stack_e, i * 14 * 16 + START)
            if later(i, 1):
                pe.wait_ge(stack_m, i * 12 * 16 + START)
            for kind, n in trip_steps(i):
                if kind == "s":
                    score(n)
                elif kind == "w":
                    weigh(n)
                elif kind == "ct":
                    tokens(n)
                elif kind == "cx":
                    for gr in (2 * n, 2 * n + 1):
                        read(g, "ct", gr)
                    transposed(kind, n, ctx_tok)
                elif kind == "m":
                    bank, full = opened(g, kind, n)
                    score_maxima(nc, keep, bank, MAXES[n], qs_m, ks_m).then_inc(full, 1)
                elif kind == "mT":
                    if n == 0:
                        read(g, "m", len(MAXES) - 2)
                        read(g, "m", len(MAXES) - 1)
                    bank, full = opened(g, kind, n)
                    for t in range(2):
                        last = M.transpose(bank[0:H, t * 128:t * 128 + 128], keep["rowmax"][:, 2 * n + t, :],
                                           ident[:, :])
                    last.then_inc(full, 1)
                elif kind == "xT":
                    project.pe_x(pe, i, n, i * 16 + START)
                elif kind == "rt":
                    if n == 0:
                        pe.wait_ge(x2_ready, (NB - 1) * 2 + START)
                    bank, full = opened(g, kind, n)
                    for c in range(DC):
                        for t in range(2):
                            at = (2 * c + t) * 128
                            last = M.transpose(bank[:, at:at + 128], x2_all[:, 2 * n + t, c * 128:c * 128 + 128],
                                               ident[:, :])
                    last.then_inc(full, 1)
                elif kind == "lg":
                    read(g, "rt", n)
                    bank, full = opened(g, kind, n)
                    for t in range(2):
                        at = n % 2 * 256 + t * 128
                        last = three(nc, bank[:, t * NE:t * NE + NE],
                                     lambda hl, c: keep["xT"][:, hl, c, at:at + 128],
                                     lambda hl, c: keep["wg"][:, hl, c, :], DC)
                    last.then_inc(full, 1)
                elif kind == "q":
                    project.pe_q(pe, i, n)
                elif kind == "v":
                    project.pe_v(pe, i, n)
                elif kind == "o":
                    if n == 0:
                        for c in range(DC):
                            read(g, "cx", c)
                    bank, full = opened(g, kind, n)
                    for t in range(2):
                        at = (2 * n + t) * 128
                        last = three(nc, bank[:, t * D:t * D + D], lambda hl, c: ctxT[:, hl, c, at:at + 128],
                                     lambda hl, c: w_hl[:, hl, 3, c, :], DC)
                    last.then_inc(full, 1)
                elif kind == "xa":
                    pe.wait_ge(x1_ready, i * 2 + 2)
                    transposed(kind, n, x1)
                elif kind == "S":
                    if n == 0:
                        pe.wait_ge(ax_in, i * 16 + 16)
                        for c in range(DC):
                            read(g, "xa", c)
                    bank, full = opened(r, kind, n)
                    for half in range(2):
                        last = three(nc, bank[:, half, :], lambda hl, c: x1T[:, hl, c, n * 128:n * 128 + 128],
                                     lambda hl, c: a_x[:, hl, c, half * 512:half * 512 + 512], DC)
                    last.then_inc(full, 1)
                elif kind in ("T", "Tp"):
                    pe.wait_ge(e_prob, i * NQ + n + 1)
                    bank, full = opened(turned(n)[0], kind, n)
                    for k in range(PAIRS):
                        last = M.transpose(flat(bank[:, :, :])[:, k * 128:k * 128 + 128],
                                           e_x[:, n, k * 128:k * 128 + 128], ident[:, :])
                    last.then_inc(full, 1)
                elif kind == "O":
                    if n == 0:
                        pe.wait_ge(vw_in, i * 16 + 16)
                    slots, name = turned(n)
                    read(slots, name, n)
                    bank, full = opened(g, kind, n)
                    three(nc, bank[:, 0:D], lambda hl, k: pT[:, n % 2, hl, k, :],
                          lambda hl, k: vw[:, hl, k, :], PAIRS).then_inc(full, 1)

        run_trips(nc.tensor, trip)


def expert_block(nc, ctx, dram, keep):
    ident, ident16, z = keep["ident"], keep["ident16"], keep["x2_all"]

    def sb(name, shape, dt=F32):
        return ctx.enter_context(nc.sbuf_tensor(name, shape, dt))

    def sem(name):
        return ctx.enter_context(nc.semaphore(name))

    before = sb("before", [128, 128], F16)
    ones16 = sb("ones16", [128, 128], F16)
    iota_e = sb("iota_e", [128, NE])
    iota_s = sb("iota_s", [128, NE])
    iota_t = sb("iota_t", [128, TILES])
    iota_h = sb("iota_h", [128, TILES * HALVES])
    wg, logits = keep["wg"], keep["logits"]
    top = sb("top", [128, NT, 8])
    topi = sb("topi", [128, NT, 8], U32)
    topf = sb("topf", [128, NT, 2])
    gap = sb("gap", [128, NT])
    table = sb("table", [128, 1])
    gate = sb("gate", [128, 2, NT])
    hot = sb("hot", [128, 2, NT, NE])
    hot16 = sb("hot16", [128, NT, NE], F16)
    run = sb("run", [128, 2, NT, NE])
    fits = sb("fits", [128, NE, NE])
    tiles_e = sb("tiles_e", [128, NE])
    upto = sb("upto", [128, 2, NE])
    pos = sb("pos", [128, NT, NE])
    pick = sb("pick", [128, 2, NT, NE])
    slot_f = sb("slot_f", [128, 2, NT])
    slot = sb("slot", [128, 2, NT], I32)
    half_i = sb("half_i", [128, 2, NT], I32)
    half_f = sb("half_f", [128, 2 * NT])
    row_f = sb("row_f", [128, 2, NT])
    iota_i = sb("iota_i", [128, 128], I32)
    iota_r = sb("iota_r", [128, 128], F16)
    token_i = sb("token_i", [128, NT], I32)
    token_f = sb("token_f", [128, 2, NT])
    own_i = sb("own_i", [128, TILES * HALVES], I32)
    own_f = sb("own_f", [128, TILES * HALVES])
    in_row = sb("in_row", [128, 2 * NT, 128], F16)
    in_half = sb("in_half", [128, 2, 2 * NT, TILES * HALVES], F16)
    src_f = sb("src_f", [128, (TILES + 1) * HALVES])
    dst_f = sb("dst_f", [128, TILES * HALVES])
    spare_f = sb("spare_f", [128, TILES * HALVES])
    src = sb("src", [128, 2, HALVES], I32)
    dst = sb("dst", [128, 2, HALVES], I32)
    below = sb("below", [128, TILES, NE])
    eid_f = sb("eid_f", [128, TILES])
    eid = sb("eid", [128, TILES], I32)
    b1r = sb("b1r", [NE * FM, 128])
    b1T = sb("b1T", [128, NE * FM])
    b1 = sb("b1", [128, 2, FM])
    w1f = sb("w1f", [128, 2, DC, FF])
    w2f = sb("w2f", [128, 2, FM, D])
    w1 = sb("w1", [128, 2, 2, DC, FF], F16)
    w2 = sb("w2", [128, 2, 2, FM, D], F16)
    xg = sb("xg", [128, 2, HALVES, D])
    xT = sb("xT2", [128, 2, 2 * DC, SLOTS], F16)
    hf = sb("hf", [128, FM, SLOTS])
    h = sb("h", [128, 2, 2, FM, SLOTS], F16)
    b2_rows = sb("b2_rows", [128, NE * D])
    b2 = sb("b2", [128, 2, D])
    y = sb("y", [128, 2, 2, D])
    power = sb("power2", [128, 3 * NQ])
    shift = sb("shift", [128, 2, NQ])
    parts = sb("parts", [128, NT, 2, D])
    stats = sb("stats2", [128, NQ, 6])
    meanvar = sb("meanvar2", [128, 2, NQ, 2])
    rstd = sb("rstd2", [128, 2, NQ])

    HB = [ctx.enter_context(nc.psum_tensor(f"HB{i}", [128, 2, SLOTS], F32)) for i in range(4)]
    YB = [ctx.enter_context(nc.psum_tensor(f"YB{i}", [128, 2, D], F32)) for i in range(2)]
    XBS = [ctx.enter_context(nc.psum_tensor(f"XB{i}", [128, DC, SLOTS], F32)) for i in range(2)]
    XB = XBS[0]
    LATE = NT // 2 - EARLY
    slot_map = YB[0][:, :, 0:TILES * HALVES]
    LB, rank, total, b1B = HB[2][:, 0, 0:LATE * 2 * NE], HB[3][:, 0, 0:128], HB[3][:, 0, 128:256], HB[3][:, 1, 0:NE * FM]

    const_step, consts, rt_step, ranks = sem("ec_step"), sem("ec_done"), sem("rt_step"), sem("ranks")
    gap_done, gexp_done, slot_done, eid_done, b1_in = (
        sem("gap_done"), sem("gexp_done"), sem("slot_done"), sem("eid_done"), sem("b1_in"))
    gather_seen, scatter_seen = sem("gather_seen"), sem("scatter_seen")
    x_stored, placed, mapped, src_done, dst_done = (
        sem("x_stored"), sem("placed"), sem("mapped"), sem("src_done"), sem("dst_done"))
    halves_found, halves_set = sem("halves_found"), sem("halves_set")
    w1_in = [sem(f"w1_in{i}") for i in range(2)]
    w2_in = [sem(f"w2_in{i}") for i in range(2)]
    xg_in = [sem(f"xg_in{i}") for i in range(2)]
    b2_in, b2_done = sem("b2_in"), sem("b2_done")
    w1_hi, w2_hi, w1_split, w2_split = sem("w1_hi"), sem("w2_hi"), sem("w1_split"), sem("w2_split")
    xt_full, xt_hi, xt_done, b1_done = sem("xt_full"), sem("xt_hi"), sem("xt_done"), sem("b1_done")
    h_full, h_gelu, h_hi, h_split = sem("h_full"), sem("h_gelu"), sem("h_hi"), sem("h_split")
    y_full, y_done = sem("y_full"), sem("y_done")
    y_out = [sem(f"y_out{i}") for i in range(2)]
    lt_full, lt_hi, lt_lo, lg_done = sem("lt_full"), sem("lt_hi"), sem("lt_lo"), sem("lg_done")
    hot_done = sem("hot_done")
    parts_in = [sem(f"parts_in{i}") for i in range(NT // NQ)]
    part_done, part_added = sem("part_done"), sem("part_added")
    var_done, pool_step, rstd_done = sem("var2_done"), sem("pool2_step"), sem("rstd2_done")
    z_done, stored = sem("z_done"), sem("stored")

    TRIPS = (TILES - 3) // 2
    assert TILES % 2 == 1 and NT // NQ * NQ == NT and T // SLOTS <= NE

    def run_steps(eng, step):
        step(0, 0, 0)
        step(1, 0, 1)
        with eng.Fori(0, TRIPS) as i:
            step(2 * i + 2, i + 1, 0)
            step(2 * i + 3, i + 1, 1)
        step(TILES - 1, TILES // 2, 0)

    def is_int(n, *values):
        return isinstance(n, int) and n in values

    def following(n, j, q):
        return n + 1, j + q, 1 - q

    block = ctx.enter_context(nc.Block())

    @block.sync
    def _(sp):
        sp.dma_start(b1r[:, :], dram["b1"].rearrange("e (m p) -> (e m) p", p=128)).then_inc(b1_in, 16)
        sp.dma_start(b2_rows[:, :], dram["b2"].rearrange("e d -> (e d)")
                     .partition_broadcast(128)).then_inc(b2_in, 16)
        for k in range(NT // NQ):
            sp.dma_start(dram["xs"][k * S:(k + 1) * S, :].rearrange("(t p) d -> p t d", p=128),
                         z[:, k * NQ:(k + 1) * NQ, :]).then_inc(x_stored, 16)
        sp.wait_ge(eid_done, 1)

        def load(n, j, q):
            old = not is_int(n, 0, 1)
            e = nc.sync.value_load(eid[0:1, bass.ds(n, 1)], min_val=0, max_val=NE - 1)
            if old:
                sp.wait_ge(w1_split, n - 1)
            sp.dma_start(w1f[:, q, :, :], dram["W1"][bass.ds(e * D, D), :]
                         .rearrange("(c p) f -> p c f", p=128)).then_inc(w1_in[q], 16)
            if old:
                sp.wait_ge(w2_split, n - 1)
            sp.dma_start(w2f[:, q, :, :], dram["W2"][bass.ds(e * FF, FF), :]
                         .rearrange("(m p) d -> p m d", p=128)).then_inc(w2_in[q], 16)

        run_steps(nc.sync, load)
        sp.wait_ge(y_out[0], (TILES + 1) // 2 * HALVES * 16)
        sp.wait_ge(y_out[1], TILES // 2 * HALVES * 16)
        for k in range(NT // NQ):
            for c in range(2):
                sp.dma_start(parts[:, k * NQ:(k + 1) * NQ, c, :], dram["ys"][c * T + k * S:c * T + (k + 1) * S, :]
                             .rearrange("(t p) d -> p t d", p=128)).then_inc(parts_in[k], 16)
        for k in range(NT // NQ):
            sp.wait_ge(z_done, k + 1)
            sp.dma_start(dram["out"][k * S:(k + 1) * S, :].rearrange("(t p) d -> p t d", p=128),
                         z[:, k * NQ:(k + 1) * NQ, :]).then_inc(stored, 16)
        sp.wait_ge(stored, NT // NQ * 16)

    @block.gpsimd
    def _(pool):
        P = nc.gpsimd
        P.memset(before[:, :], 0.0).then_inc(const_step, 1)
        P.memset(ones16[:, :], 1.0).then_inc(const_step, 1)
        P.iota(topi[:, 0, :], pattern=[[1, NE]], base=0, channel_multiplier=0).then_inc(const_step, 1)
        P.iota(eid[:, :], pattern=[[1, TILES]], base=0, channel_multiplier=0).then_inc(const_step, 1)
        P.memset(power[:, 0:NQ], EPS).then_inc(const_step, 1)
        P.memset(power[:, NQ:2 * NQ], -0.5).then_inc(const_step, 1)
        P.memset(power[:, 2 * NQ:], -1.0).then_inc(const_step, 1)
        P.iota(iota_i[:, :], pattern=[[1, 128]], base=0, channel_multiplier=0).then_inc(const_step, 1)
        P.iota(token_i[:, :], pattern=[[128, NT]], base=0, channel_multiplier=1).then_inc(const_step, 1)
        P.iota(own_i[:, :], pattern=[[128, TILES * HALVES]], base=0, channel_multiplier=1).then_inc(const_step, 1)
        pool.wait_ge(const_step, 10)
        P.affine_select(out=before[:, :], in_=before[:, :], compare_op=ALU.is_ge, fill=1.0, base=0,
                        pattern=[[-1, 128]], channel_multiplier=1).then_inc(consts, 1)
        P.tensor_copy(iota_e[:, :], topi[:, 0, :]).then_inc(consts, 1)
        P.tensor_copy(iota_t[:, :], eid[:, :]).then_inc(consts, 1)
        P.tensor_copy(iota_r[:, :], iota_i[:, :]).then_inc(consts, 1)
        P.tensor_copy(token_f[:, 1, :], token_i[:, :]).then_inc(consts, 1)
        P.tensor_copy(own_f[:, :], own_i[:, :]).then_inc(consts, 1)
        P.tensor_copy(iota_h[:, :], iota_i[:, 0:TILES * HALVES]).then_inc(consts, 1)
        pool.wait_ge(consts, 7)
        P.tensor_scalar(token_f[:, 0, :], token_f[:, 1, :], 0.5, None, ALU.mult).then_inc(consts, 1)
        pool.wait_ge(consts, 8)
        pool.wait_ge(halves_found, 1)
        for c in range(2):
            ct = slice(c * NT, c * NT + NT)
            P.tensor_tensor(in_half[:, 0, ct, :], in_half[:, 1, ct, :],
                            token_f[:, c, :].unsqueeze(2).to_broadcast([128, NT, TILES * HALVES]),
                            ALU.mult).then_inc(halves_set, 1)
        pool.wait_ge(x_stored, NT // NQ * 16)

        def gather(n, q):
            pool.wait_ge(src_done, n + 1)
            if not is_int(n, 0, 1):
                pool.wait_ge(xt_full, n - 1)
            pool.sem_inc(gather_seen, 1)
            for t in range(HALVES):
                pool.indirect_dma_start(out=xg[:, q, t, :], out_offset=None, in_=dram["xs"],
                                        in_offset=bass.IndirectOffsetOnAxis(src[:, q, t:t + 1], 0)
                                        ).then_inc(xg_in[q], 16)

        def scatter(n, q):
            pool.wait_ge(dst_done, n + 1)
            pool.wait_ge(y_done, n + 1)
            pool.sem_inc(scatter_seen, 1)
            for t in range(HALVES):
                pool.indirect_dma_start(out=dram["ys"], in_=y[:, q, t, :], in_offset=None,
                                        out_offset=bass.IndirectOffsetOnAxis(dst[:, q, t:t + 1], 0)
                                        ).then_inc(y_out[q], 16)

        def step(n, j, q):
            if not is_int(n, TILES - 1):
                gather(n + 1, 1 - q)
            if not is_int(n, 0, 1):
                scatter(n - 2, q)

        gather(0, 0)
        run_steps(nc.gpsimd, step)
        scatter(TILES - 2, 1)
        scatter(TILES - 1, 0)

        def add_part(k):
            rows = slice(k * NQ, (k + 1) * NQ)
            pool.wait_ge(part_done, k)
            P.tensor_tensor(z[:, rows, :], z[:, rows, :], parts[:, rows, 1, :], ALU.add).then_inc(part_added, 1)

        def root(k):
            pool.wait_ge(var_done, k + 1)
            P.tensor_tensor(rstd[:, k % 2, :], meanvar[:, k % 2, :, 1], power[:, 0:NQ], ALU.add).then_inc(pool_step, 1)
            pool.wait_ge(pool_step, 3 * k + 1)
            P.tensor_tensor(rstd[:, k % 2, :], rstd[:, k % 2, :], power[:, NQ:2 * NQ], ALU.pow).then_inc(pool_step, 1)
            pool.wait_ge(pool_step, 3 * k + 2)
            P.tensor_tensor(shift[:, k % 2, :], rstd[:, k % 2, :], meanvar[:, k % 2, :, 0], ALU.mult).then_inc(pool_step, 1)
            pool.wait_ge(pool_step, 3 * k + 3)
            P.tensor_tensor(shift[:, k % 2, :], shift[:, k % 2, :], power[:, 2 * NQ:], ALU.mult).then_inc(rstd_done, 1)

        for k in range(1, NT // NQ):
            add_part(k)
            root(k - 1)
        root(NT // NQ - 1)

    @block.scalar
    def _(act):
        A = nc.scalar
        for n in range(LATE):
            act.wait_ge(lt_full, n + 1)
            if n >= 2:
                act.wait_ge(lg_done, n - 1)
            A.activation(xT[:, n % 2, 0:DC, :], XBS[n % 2][:, :, :], ACT.Copy, scale=XS).then_inc(lt_hi, 1)
        act.wait_ge(gap_done, 1)
        A.activation(gate[:, 1, :], gap[:, :], ACT.Exp).then_inc(gexp_done, 1)
        act.wait_ge(consts, 7)
        A.activation(table[:, :], iota_e[:, 0:1], ACT.Gelu)

        def x_high(n, q):
            act.wait_ge(xt_full, n + 1)
            A.activation(xT[:, q, 0:DC, :], XB[:, :, :], ACT.Copy, scale=XS).then_inc(xt_hi, 1)

        def w1_high(n, j, q):
            act.wait_ge(w1_in[q], j * 16 + 16)
            if not is_int(n, 0, 1):
                act.wait_ge(h_full, 4 * n - 4)
            A.activation(w1[:, q, 0, :, :].rearrange("p c f -> p (c f)"),
                         w1f[:, q, :, :].rearrange("p c f -> p (c f)"), ACT.Copy, scale=WS).then_inc(w1_hi, 1)

        def step(n, j, q):
            if not is_int(n, TILES - 1):
                w1_high(*following(n, j, q))
            act.wait_ge(b1_done, n + 1)
            for b in range(4):
                act.wait_ge(h_full, 4 * n + b + 1)
                if not is_int(n, 0):
                    act.wait_ge(h_split, 4 * n - 3 + b)
                for m in range(2):
                    last = A.activation(hf[:, 2 * b + m, :], HB[b][:, m, :], ACT.Gelu,
                                        bias=b1[:, q, 2 * b + m:2 * b + m + 1], scale=1.0 / (WS * XS))
                last.then_inc(h_gelu, 1)
            if not is_int(n, TILES - 1):
                x_high(n + 1, 1 - q)
            act.wait_ge(w2_in[q], j * 16 + 16)
            if not is_int(n, 0, 1):
                act.wait_ge(y_full, n - 1)
            A.activation(w2[:, q, 0, :, :].rearrange("p m d -> p (m d)"),
                         w2f[:, q, :, :].rearrange("p m d -> p (m d)"), ACT.Copy, scale=WS).then_inc(w2_hi, 1)

        w1_high(0, 0, 0)
        x_high(0, 0)
        run_steps(nc.scalar, step)

        def weigh(k):
            act.wait_ge(parts_in[k], 2 * 16)
            for t in range(k * NQ, (k + 1) * NQ):
                last = A.activation(parts[:, t, 1, :], parts[:, t, 1, :], ACT.Copy, scale=gate[:, 1, t:t + 1])
            last.then_inc(part_done, 1)

        def normalize(k):
            act.wait_ge(rstd_done, k + 1)
            for t in range(k * NQ, (k + 1) * NQ):
                last = A.activation(z[:, t, :], z[:, t, :], ACT.Identity, bias=shift[:, k % 2, t % NQ:t % NQ + 1],
                                    scale=rstd[:, k % 2, t % NQ:t % NQ + 1])
            last.then_inc(z_done, 1)

        for k in range(1, NT // NQ):
            weigh(k)
        for k in range(NT // NQ):
            normalize(k)

    @block.vector
    def _(dve):
        V = nc.vector
        count = [0]

        def after(ins):
            count[0] += 1
            ins.then_inc(rt_step, 1)
            dve.wait_ge(rt_step, count[0])

        def wide(ap, *shape):
            return ap.to_broadcast([128, *shape])

        V.memset(src_f[:, TILES * HALVES:], 0.0)
        for n in range(LATE):
            dve.wait_ge(lt_hi, n + 1)
            V.scalar_tensor_tensor(xT[:, n % 2, DC:, :], XBS[n % 2][:, :, :], XS, xT[:, n % 2, 0:DC, :],
                                   ALU.mult, ALU.subtract).then_inc(lt_lo, 1)
        dve.wait_ge(lg_done, LATE)
        after(V.tensor_scalar(logits[:, EARLY * 2 * NE:], LB, 1.0 / (WS * XS), None, ALU.mult))
        dve.wait_ge(consts, 7)
        for t in range(NT):
            last = V.max(top[:, t, :], logits[:, t * NE:t * NE + NE])
        after(last)
        V.tensor_tensor(gap[:, :], top[:, :, 1], top[:, :, 0], ALU.subtract).then_inc(gap_done, 1)
        for t in range(NT):
            last = V.max_index(topi[:, t, :], top[:, t, :], logits[:, t * NE:t * NE + NE])
        after(last)
        after(V.tensor_copy(topf[:, :, :], topi[:, :, 0:2]))
        for c in range(2):
            last = V.tensor_tensor(hot[:, c, :, :], wide(topf[:, :, c:c + 1], NT, NE),
                                   wide(iota_e[:, :].unsqueeze(1), NT, NE), ALU.is_equal)
        after(last)
        V.tensor_tensor(hot16[:, :, :], hot[:, 0, :, :], hot[:, 1, :, :], ALU.add).then_inc(hot_done, 1)
        V.tensor_scalar(iota_s[:, :], iota_e[:, :], float(SLOTS), None, ALU.mult)
        dve.wait_ge(ranks, 1)
        V.tensor_copy(b1T[:, :], b1B)
        after(V.tensor_copy(run[:, 0, :, :], total.rearrange("p (t e) -> p t e", e=NE)))
        cur = 0
        for k in (1, 2, 4, 8):
            V.tensor_copy(run[:, 1 - cur, 0:k, :], run[:, cur, 0:k, :])
            after(V.tensor_tensor(run[:, 1 - cur, k:, :], run[:, cur, k:, :], run[:, cur, 0:NT - k, :], ALU.add))
            cur = 1 - cur
        after(V.tensor_tensor(fits[:, :, :], wide(run[:, cur, NT - 1, :].unsqueeze(2), NE, NE),
                              wide(iota_s[:, :].unsqueeze(1), NE, NE), ALU.is_gt))
        after(V.tensor_reduce(tiles_e[:, :], fits[:, :, :], AX.X, ALU.add))
        after(V.tensor_copy(upto[:, 0, :], tiles_e[:, :]))
        at = 0
        for k in (1, 2, 4):
            V.tensor_copy(upto[:, 1 - at, 0:k], upto[:, at, 0:k])
            after(V.tensor_tensor(upto[:, 1 - at, k:], upto[:, at, k:], upto[:, at, 0:NE - k], ALU.add))
            at = 1 - at
        after(V.tensor_tensor(below[:, :, :], wide(upto[:, at, :].unsqueeze(1), TILES, NE),
                              wide(iota_t[:, :].unsqueeze(2), TILES, NE), ALU.is_le))
        after(V.tensor_reduce(eid_f[:, :], below[:, :, :], AX.X, ALU.add))
        V.tensor_scalar(eid[:, :], eid_f[:, :], NE - 1.0, None, ALU.min).then_inc(eid_done, 1)
        V.tensor_tensor(upto[:, 1 - at, :], upto[:, at, :], tiles_e[:, :], ALU.subtract)
        after(V.tensor_tensor(run[:, 1 - cur, :, :], run[:, cur, :, :],
                              total.rearrange("p (t e) -> p t e", e=NE), ALU.subtract))
        after(V.tensor_tensor(run[:, cur, :, :], run[:, 1 - cur, :, :],
                              rank.rearrange("p (t e) -> p t e", e=NE), ALU.add))
        after(V.scalar_tensor_tensor(pos[:, :, :], wide(upto[:, 1 - at, :].unsqueeze(1), NT, NE), float(SLOTS),
                                     run[:, cur, :, :], ALU.mult, ALU.add))
        after(V.tensor_tensor(pick[:, :, :, :], hot[:, :, :, :], wide(pos[:, :, :].unsqueeze(1), 2, NT, NE), ALU.mult))
        after(V.tensor_reduce(slot_f[:, :, :], pick[:, :, :, :], AX.X, ALU.add))
        after(V.tensor_copy(slot[:, :, :], slot_f[:, :, :]))
        after(V.tensor_scalar(half_i[:, :, :], slot[:, :, :], 7, None, ALU.logical_shift_right))
        after(V.tensor_copy(half_f[:, :], half_i[:, :, :].rearrange("p c t -> p (c t)")))
        V.scalar_tensor_tensor(row_f[:, :, :], half_f[:, :].rearrange("p (c t) -> p c t", t=NT), -128.0,
                               slot_f[:, :, :], ALU.mult, ALU.add)
        after(V.tensor_tensor(in_half[:, 1, :, :], wide(half_f[:, :].unsqueeze(2), 2 * NT, TILES * HALVES),
                              wide(iota_h[:, :].unsqueeze(1), 2 * NT, TILES * HALVES), ALU.is_equal))
        V.tensor_scalar(in_half[:, 1, 0:NT, :], in_half[:, 1, 0:NT, :], 2.0, None, ALU.mult).then_inc(halves_found, 1)
        for c in range(2):
            for t in range(NT):
                V.tensor_scalar(in_row[:, c * NT + t, :], iota_r[:, :], row_f[:, c, t:t + 1], None,
                                ALU.is_equal).then_inc(placed, 1)
        dve.wait_ge(mapped, 1)
        after(V.tensor_copy(src_f[:, 0:TILES * HALVES], slot_map[:, 0, :]))
        V.tensor_copy(src[:, 0, :], src_f[:, 0:HALVES]).then_inc(src_done, 1)
        dve.wait_ge(gexp_done, 1)
        after(V.tensor_scalar(gap[:, :], gate[:, 1, :], 1.0, None, ALU.add))
        after(V.reciprocal(gate[:, 0, :], gap[:, :]))
        after(V.tensor_tensor(gate[:, 1, :], gate[:, 1, :], gate[:, 0, :], ALU.mult))
        after(V.scalar_tensor_tensor(dst_f[:, :], slot_map[:, 1, :], -float(T), src_f[:, 0:TILES * HALVES],
                                     ALU.mult, ALU.add))
        after(V.scalar_tensor_tensor(spare_f[:, :], slot_map[:, 1, :], 0.0, own_f[:, :], ALU.is_equal, ALU.mult))
        V.scalar_tensor_tensor(dst_f[:, :], dst_f[:, :], 2.0 * T, spare_f[:, :], ALU.add, ALU.add).then_inc(slot_done, 1)
        dve.wait_ge(slot_done, 1)
        dve.wait_ge(eid_done, 1)

        def ready(n, j, q):
            e = nc.vector.value_load(eid[0:1, bass.ds(n, 1)], min_val=0, max_val=NE - 1)
            V.tensor_copy(b1[:, q, :], b1T[:, bass.ds(e * FM, FM)]).then_inc(b1_done, 1)
            dve.wait_ge(xt_hi, n + 1)
            V.scalar_tensor_tensor(xT[:, q, DC:, :], XB[:, :, :], XS, xT[:, q, 0:DC, :],
                                   ALU.mult, ALU.subtract).then_inc(xt_done, 1)
            V.tensor_copy(src[:, 1 - q, :], src_f[:, bass.ds(n * HALVES + HALVES, HALVES)]).then_inc(src_done, 1)

        def w1_low(n, q):
            dve.wait_ge(w1_hi, n + 1)
            V.scalar_tensor_tensor(w1[:, q, 1, :, :].rearrange("p c f -> p (c f)"),
                                   w1f[:, q, :, :].rearrange("p c f -> p (c f)"), WS,
                                   w1[:, q, 0, :, :].rearrange("p c f -> p (c f)"),
                                   ALU.mult, ALU.subtract).then_inc(w1_split, 1)

        def output(n, j, q):
            e = nc.vector.value_load(eid[0:1, bass.ds(n, 1)], min_val=0, max_val=NE - 1)
            V.tensor_copy(b2[:, q, :], b2_rows[:, bass.ds(e * D, D)]).then_inc(b2_done, 1)
            if not is_int(n, 0, 1):
                dve.wait_ge(y_out[q], j * HALVES * 16)
            V.tensor_copy(dst[:, q, :], dst_f[:, bass.ds(n * HALVES, HALVES)]).then_inc(dst_done, 1)
            dve.wait_ge(b2_done, n + 1)
            dve.wait_ge(y_full, n + 1)
            V.scalar_tensor_tensor(y[:, q, :, :], YB[q][:, :, :], 1.0 / (WS * XS),
                                   wide(b2[:, q, :].unsqueeze(1), 2, D), ALU.mult, ALU.add).then_inc(y_done, 1)

        def step(n, j, q):
            if not is_int(n, TILES - 1):
                w1_low(n + 1, 1 - q)
            if not is_int(n, 0, 1):
                dve.wait_ge(y_full, n - 1)
            for b in range(4):
                pair = slice(2 * b, 2 * b + 2)
                dve.wait_ge(h_gelu, 4 * n + b + 1)
                V.tensor_scalar(h[:, q, 0, pair, :], hf[:, pair, :], XS, None, ALU.mult).then_inc(h_hi, 1)
                dve.wait_ge(h_hi, 4 * n + b + 1)
                V.scalar_tensor_tensor(h[:, q, 1, pair, :], hf[:, pair, :], XS, h[:, q, 0, pair, :],
                                       ALU.mult, ALU.subtract).then_inc(h_split, 1)
            if not is_int(n, TILES - 1):
                ready(*following(n, j, q))
            dve.wait_ge(w2_hi, n + 1)
            V.scalar_tensor_tensor(w2[:, q, 1, :, :].rearrange("p m d -> p (m d)"),
                                   w2f[:, q, :, :].rearrange("p m d -> p (m d)"), WS,
                                   w2[:, q, 0, :, :].rearrange("p m d -> p (m d)"),
                                   ALU.mult, ALU.subtract).then_inc(w2_split, 1)
            if not is_int(n, 0):
                output(n - 1, j - 1 + q, 1 - q)

        dve.wait_ge(b2_in, 16)
        w1_low(0, 0)
        ready(0, 0, 0)
        run_steps(nc.vector, step)
        output(TILES - 1, TILES // 2, 0)

        for k in range(NT // NQ):
            tiles = range(k * NQ, (k + 1) * NQ)
            if k == 0:
                dve.wait_ge(parts_in[k], 2 * 16)
                for t in tiles:
                    last = V.scalar_tensor_tensor(z[:, t, :], parts[:, t, 1, :], gate[:, 1, t:t + 1], z[:, t, :],
                                                  ALU.mult, ALU.add)
                after(last)
            else:
                dve.wait_ge(part_added, k)
            for t in tiles:
                last = V.scalar_tensor_tensor(z[:, t, :], parts[:, t, 0, :], gate[:, 0, t:t + 1], z[:, t, :],
                                              ALU.mult, ALU.add)
            after(last)
            for t in tiles:
                last = V.bn_stats(stats[:, t % NQ, :], z[:, t, :])
            after(last)
            if k >= 2:
                dve.wait_ge(z_done, k - 1)
            for t in tiles:
                last = V.bn_aggr(meanvar[:, k % 2, t % NQ, :], stats[:, t % NQ, :])
            last.then_inc(var_done, 1)

    @block.tensor
    def _(pe):
        M = nc.tensor

        def router(n):
            pe.wait_ge(lt_lo, n + 1)
            for t in range(2):
                at = (2 * n + t) * NE
                last = three(nc, LB[:, at:at + NE], lambda hl, c: xT[:, n % 2, hl * DC + c, t * 128:t * 128 + 128],
                             lambda hl, c: wg[:, hl, c, :], DC)
            last.then_inc(lg_done, 1)

        for n in range(LATE):
            for c in range(DC):
                for t in range(2):
                    last = M.transpose(XBS[n % 2][:, c, t * 128:t * 128 + 128],
                                       z[:, 2 * (EARLY + n) + t, c * 128:c * 128 + 128], ident[:, :])
            last.then_inc(lt_full, 1)
            if n > 0:
                router(n - 1)
        router(LATE - 1)
        pe.wait_ge(consts, 7)
        pe.wait_ge(b1_in, 16)
        M.transpose(b1B, b1r[:, :], ident[0:NE * FM, 0:NE * FM])
        pe.wait_ge(hot_done, 1)
        hot2 = hot16[:, :, :].rearrange("p t e -> p (t e)")
        M.matmul(rank, before[:, :], hot2, start=True, stop=True)
        M.matmul(total, ones16[:, :], hot2, start=True, stop=True).then_inc(ranks, 1)
        for i in range(2 * NT):
            pe.wait_ge(placed, i + 1)
            if i % NT == 0:
                pe.wait_ge(halves_set, i // NT + 1)
            last = M.matmul(slot_map, in_row[:, i, :], in_half[:, :, i, :], start=i == 0, stop=i == 2 * NT - 1)
        last.then_inc(mapped, 1)

        def transposes(n, j, q):
            pe.wait_ge(xg_in[q], (j + 1) * HALVES * 16)
            if not is_int(n, 0):
                pe.wait_ge(xt_done, n)
            for c in range(DC):
                for t in range(HALVES):
                    last = M.transpose(XB[:, c, t * 128:t * 128 + 128], xg[:, q, t, c * 128:c * 128 + 128],
                                       ident[:, :])
            last.then_inc(xt_full, 1)

        def second(n, j, q):
            pe.wait_ge(h_split, 4 * n + 4)
            pe.wait_ge(w2_split, n + 1)
            if not is_int(n, 0, 1):
                pe.wait_ge(y_done, n - 1)
            for t in range(2):
                last = three(nc, YB[q][:, t, :], lambda hl, m: h[:, q, hl, m, t * 128:t * 128 + 128],
                             lambda hl, m: w2[:, q, hl, m, :], FM)
            last.then_inc(y_full, 1)

        def step(n, j, q):
            pe.wait_ge(xt_done, n + 1)
            pe.wait_ge(w1_split, n + 1)
            for b in range(4):
                if not is_int(n, 0):
                    pe.wait_ge(h_gelu, 4 * n - 3 + b)
                for m in range(2):
                    at = (2 * b + m) * 128
                    last = three(nc, HB[b][:, m, :], lambda hl, c: w1[:, q, hl, c, at:at + 128],
                                 lambda hl, c: xT[:, q, hl * DC + c, :], DC)
                last.then_inc(h_full, 1)
            if not is_int(n, TILES - 1):
                transposes(*following(n, j, q))
            if not is_int(n, 0):
                second(n - 1, j - 1 + q, 1 - q)

        transposes(0, 0, 0)
        run_steps(nc.tensor, step)
        second(TILES - 1, TILES // 2, 0)


def decoder_layer(nc, dram):
    def buffers(ctx, keep, *names):
        for name, shape, dt in names:
            keep[name] = ctx.enter_context(nc.sbuf_tensor(name, shape, dt))

    with ExitStack() as outer:
        keep = {"dram": dram}
        buffers(outer, keep, ("ident", [128, 128], F32), ("ident16", [128, 128], F16), ("x2_all", [128, NT, D], F32),
                ("wg", [128, 2, DC, NE], F16), ("logits", [128, NT * NE], F32))
        with ExitStack() as attention:
            buffers(attention, keep,
                    ("causal", [128, 128], F16), ("power", [128, 2 * NQ], F32),
                    ("x_tok", [128, NQ, D], F32), ("x_res", [128, NQ, D], F32),
                    ("xT", [128, 2, DC, S], F16),
                    ("qf", [128, 2, S], F32),
                    ("qk", [128, 2, 4, S], F16),
                    ("qs_m", [128, PAIRS, S], F16), ("ks_m", [128, PAIRS, S], F16),
                    ("qs_e", [128, PAIRS, S], F16), ("ks_e", [128, PAIRS, S], F16),
                    ("v_next", [128, NQ, D], F32), ("v_aug", [128, NQ, H, 32], F32),
                    ("rowmax", [128, NQ, H], F32), ("neg_maxT", [H, S], F16),
                    ("w_hl", [128, 2, 4, DC, D], F16),
                    ("qk_bias", [128, 2, 2], F32), ("b_rows", [128, 3, D], F32))
            with ExitStack() as ctx:
                prepare_block(nc, ctx, dram, keep)
            with ExitStack() as ctx:
                attention_block(nc, ctx, dram, keep)
        with ExitStack() as ctx:
            expert_block(nc, ctx, dram, keep)


_INS = {"x": "x", "ctx_768": "cond", "L0_attn_Wq": "Wq", "L0_attn_bq": "bq", "L0_attn_Wk": "Wk", "L0_attn_bk": "bk",
        "L0_attn_Wv": "Wv", "L0_attn_bv": "bv", "L0_attn_Wo": "Wo", "L0_attn_bo": "bo",
        "L0_xattn_w_q": "w_q", "L0_xattn_w_k": "w_k", "L0_xattn_w_v": "w_v", "L0_xattn_w_out": "w_out",
        "L0_xattn_b_out": "b_out", "L0_ffn_Wg": "WgT", "L0_ffn_W1": "W1", "L0_ffn_b1": "b1",
        "L0_ffn_W2": "W2", "L0_ffn_b2": "b2"}


def kernel(**inputs):
    import numpy as np
    import concourse.bacc as bacc
    from concourse.bass_utils import run_bass_kernel_spmd

    nc = bacc.Bacc("TRN2", target_bir_lowering=False, num_devices=1)
    arrays, dram = {}, {}
    for name, short in _INS.items():
        a = np.asarray(inputs[name])
        if short == "x" or short == "cond" or short in ("W1", "W2"):
            a = a.reshape(-1, a.shape[-1])
        elif short in ("bq", "bk"):
            a = a.reshape(DC, 128).T
        elif short == "WgT":
            a = a.T.reshape(DC, 128, NE).transpose(1, 0, 2)
        a = np.ascontiguousarray(a)
        arrays["in_" + short] = a
        dram[short] = nc.dram_tensor("in_" + short, a.shape, mybir.dt.from_np(a.dtype), kind="ExternalInput").ap()
    dram["out"] = nc.dram_tensor("out", (T, D), F32, kind="ExternalOutput").ap()
    for name, shape, dt in (("qk", (NB * 4 * D, S), F16), ("m", (H, S), F16), ("ax", (NB * 128, 2 * DC * XA), F16),
                            ("vw", (NB * 128, 2 * PAIRS * D), F16),
                            ("xs", (T, D), F32), ("ys", (2 * T + TILES * SLOTS, D), F32)):
        dram[name] = nc.dram_tensor("scratch_" + name, shape, dt).ap()
    decoder_layer(nc, dram)
    r = run_bass_kernel_spmd(nc, [arrays], core_ids=[0])
    return r.results[0]["out"].reshape(NB, S, D)
```
